# Optimizing a Trainium2 kernel written in Bass

```python
import numpy as np
import jax
import jax.numpy as jnp

def _softmax(x, axis=-1):
    return jax.nn.softmax(x, axis=axis)

def _gelu(x):
    return jax.nn.gelu(x, approximate=True)

def _silu(x):
    return jax.nn.silu(x)

def _sigmoid(x):
    return jax.nn.sigmoid(x)

def _layernorm(x, axis=-1, eps=1e-05):
    m = jnp.mean(x, axis=axis, keepdims=True)
    v = jnp.var(x, axis=axis, keepdims=True)
    return (x - m) / jnp.sqrt(v + eps)

def _scatter_add(tgt, idx, src, axis=0):
    return tgt.at[idx].add(src)

def _segment_sum(src, seg, n):
    return jax.ops.segment_sum(src, seg, n)
kernel_name = 'mk_seq_postln_d1_jaxref_r8_080512'

def setup_inputs(seed: int=0):
    np.random.seed(seed)
    _w = jnp.asarray

    def _L0_attn_setup():
        import jax, jax.numpy as jnp
        import numpy as np
        B, N, D, H, BS = (4, 512, 128, 16, 64)
        key = jax.random.key(seed)
        ks = jax.random.split(key, 5)
        s = 0.02
        w = lambda k: jax.random.normal(k, (D, D), dtype=jnp.float32) * s
        return {'x': jax.random.normal(ks[0], (B, N, D), dtype=jnp.float32), 'Wq': w(ks[1]), 'bq': jnp.zeros((D,), jnp.float32), 'Wk': w(ks[2]), 'bk': jnp.zeros((D,), jnp.float32), 'Wv': w(ks[3]), 'bv': jnp.zeros((D,), jnp.float32), 'Wo': w(ks[4]), 'bo': jnp.zeros((D,), jnp.float32), 'global_indices': jnp.array([0, N // BS - 1], dtype=jnp.int32)}
    _L0_attn_in = _L0_attn_setup()

    def _L0_ffn_setup():
        import jax, jax.numpy as jnp
        import numpy as np
        TOP_K = 4
        CAP_FACTOR = 4

        def swiglu(x, w1, w2, w3):
            return jax.nn.silu(x @ w1) * (x @ w3) @ w2
        key = jax.random.key(seed)
        ks = jax.random.split(key, 8)
        B, S, D, H, E = (2, 256, 128, 64, 32)
        Hs = 2 * H
        sd = lambda *sh: 1.0 / np.sqrt(sh[-2])
        x = jax.random.normal(ks[0], (B, S, D), dtype=jnp.float32)
        Wg = jax.random.normal(ks[1], (D, E), dtype=jnp.float32) * (1.0 / np.sqrt(D))
        W1 = jax.random.normal(ks[2], (E, D, H), dtype=jnp.float32) * (1.0 / np.sqrt(D))
        W3 = jax.random.normal(ks[3], (E, D, H), dtype=jnp.float32) * (1.0 / np.sqrt(D))
        W2 = jax.random.normal(ks[4], (E, H, D), dtype=jnp.float32) * (1.0 / np.sqrt(H))
        Ws1 = jax.random.normal(ks[5], (D, Hs), dtype=jnp.float32) * (1.0 / np.sqrt(D))
        Ws3 = jax.random.normal(ks[6], (D, Hs), dtype=jnp.float32) * (1.0 / np.sqrt(D))
        Ws2 = jax.random.normal(ks[7], (Hs, D), dtype=jnp.float32) * (1.0 / np.sqrt(Hs))
        return {'x': x, 'Wg': Wg, 'W1': W1, 'W2': W2, 'W3': W3, 'Ws1': Ws1, 'Ws2': Ws2, 'Ws3': Ws3}
    _L0_ffn_in = _L0_ffn_setup()
    _d = {'L0_attn_x': _L0_attn_in['x'], 'L0_attn_Wq': _L0_attn_in['Wq'], 'L0_attn_bq': _L0_attn_in['bq'], 'L0_attn_Wk': _L0_attn_in['Wk'], 'L0_attn_bk': _L0_attn_in['bk'], 'L0_attn_Wv': _L0_attn_in['Wv'], 'L0_attn_bv': _L0_attn_in['bv'], 'L0_attn_Wo': _L0_attn_in['Wo'], 'L0_attn_bo': _L0_attn_in['bo'], 'L0_attn_global_indices': _L0_attn_in['global_indices'], 'L0_ffn_Wg': _L0_ffn_in['Wg'], 'L0_ffn_W1': _L0_ffn_in['W1'], 'L0_ffn_W2': _L0_ffn_in['W2'], 'L0_ffn_W3': _L0_ffn_in['W3'], 'L0_ffn_Ws1': _L0_ffn_in['Ws1'], 'L0_ffn_Ws2': _L0_ffn_in['Ws2'], 'L0_ffn_Ws3': _L0_ffn_in['Ws3']}
    _x0 = _d['L0_attn_x']
    _d['L0_attn_x'] = jax.random.normal(jax.random.fold_in(jax.random.key(seed), 1), (4, 1024, 128), dtype=_x0.dtype)
    del _x0
    return _d

def reference(L0_attn_x, L0_attn_Wq, L0_attn_bq, L0_attn_Wk, L0_attn_bk, L0_attn_Wv, L0_attn_bv, L0_attn_Wo, L0_attn_bo, L0_attn_global_indices, L0_ffn_Wg, L0_ffn_W1, L0_ffn_W2, L0_ffn_W3, L0_ffn_Ws1, L0_ffn_Ws2, L0_ffn_Ws3):

    def _L0_attn_ref(x, Wq, bq, Wk, bk, Wv, bv, Wo, bo, global_indices):
        import jax, jax.numpy as jnp
        import numpy as np
        B, N, D, H, BS = (4, 512, 128, 16, 64)
        b, n, d_model = x.shape
        h = H
        dh = d_model // h
        bs = BS
        nb = n // bs
        g = global_indices.shape[0]
        scale = 1.0 / np.sqrt(dh).astype(np.float32)

        def proj(W, bias):
            return (x @ W.T + bias).reshape(b, n, h, dh).transpose(0, 2, 1, 3)
        q = proj(Wq, bq)
        k = proj(Wk, bk)
        v = proj(Wv, bv)
        qb = q.reshape(b, h, nb, bs, dh)
        kb = k.reshape(b, h, nb, bs, dh)
        vb = v.reshape(b, h, nb, bs, dh)
        gq = qb[:, :, global_indices]
        row_scores = jnp.einsum('bhgqd,bhkd->bhgqk', gq, k) * scale
        out_rows = jnp.einsum('bhgqk,bhkd->bhgqd', jax.nn.softmax(row_scores, axis=-1), v)
        kw = jnp.concatenate([jnp.roll(kb, 1, axis=2), kb, jnp.roll(kb, -1, axis=2)], axis=3)
        vw = jnp.concatenate([jnp.roll(vb, 1, axis=2), vb, jnp.roll(vb, -1, axis=2)], axis=3)
        local_scores = jnp.einsum('bhnqd,bhnkd->bhnqk', qb, kw) * scale
        out_local = jnp.einsum('bhnqk,bhnkd->bhnqd', jax.nn.softmax(local_scores, axis=-1), vw)
        gk = kb[:, :, global_indices].reshape(b, h, g * bs, dh)
        gv = vb[:, :, global_indices].reshape(b, h, g * bs, dh)
        col_scores = jnp.einsum('bhnqd,bhgd->bhnqg', qb, gk) * scale
        out_gk = jnp.einsum('bhnqg,bhgd->bhnqd', jax.nn.softmax(col_scores, axis=-1), gv)
        final = out_local + out_gk
        final = final.at[:, :, global_indices].set(out_rows)
        ctx = final.reshape(b, h, n, dh).transpose(0, 2, 1, 3).reshape(b, n, d_model)
        return ctx @ Wo.T + bo

    def _L0_ffn_ref(x, Wg, W1, W2, W3, Ws1, Ws2, Ws3):
        import jax, jax.numpy as jnp
        import numpy as np
        TOP_K = 4
        CAP_FACTOR = 4

        def swiglu(x, w1, w2, w3):
            return jax.nn.silu(x @ w1) * (x @ w3) @ w2
        B, S, D = x.shape
        E = Wg.shape[1]
        T = B * S
        xf = x.reshape(T, D)
        scores = jax.nn.softmax(xf @ Wg, axis=-1)
        weights, indices = jax.lax.top_k(scores, TOP_K)
        P = T * TOP_K
        pair_expert = indices.reshape(-1)
        pair_token = jnp.repeat(jnp.arange(T), TOP_K)
        pair_weight = weights.reshape(-1).astype(xf.dtype)
        C = CAP_FACTOR * P // E
        y = jnp.zeros_like(xf)
        for e in range(E):
            pos = jnp.nonzero(pair_expert == e, size=C, fill_value=P)[0]
            valid = pos < P
            safe = jnp.minimum(pos, P - 1)
            tok = jnp.where(valid, pair_token[safe], 0)
            w = jnp.where(valid, pair_weight[safe], 0.0)
            xg = xf[tok]
            out = swiglu(xg, W1[e], W2[e], W3[e]) * w[:, None]
            y = y.at[tok].add(out)
        z = swiglu(xf, Ws1, Ws2, Ws3)
        return (y + z).reshape(B, S, D)
    x = L0_attn_x
    x = _layernorm(x + _L0_attn_ref(x, L0_attn_Wq, L0_attn_bq, L0_attn_Wk, L0_attn_bk, L0_attn_Wv, L0_attn_bv, L0_attn_Wo, L0_attn_bo, L0_attn_global_indices), axis=-1)
    x = _layernorm(x + _L0_ffn_ref(x, L0_ffn_Wg, L0_ffn_W1, L0_ffn_W2, L0_ffn_W3, L0_ffn_Ws1, L0_ffn_Ws2, L0_ffn_Ws3), axis=-1)
    return x

_drawn_inputs = setup_inputs


def setup_inputs(seed=0):
    import zlib

    import numpy as np

    out = dict(_drawn_inputs(seed))
    spreads = {'L0_attn_bq': (0.0, 0.8),
     'L0_attn_bk': (0.0, 0.8),
     'L0_attn_bv': (0.0, 0.1),
     'L0_attn_bo': (0.0, 0.1)}
    factors = {'L0_attn_Wq': 8.0, 'L0_attn_Wk': 8.0, 'L0_attn_Wv': 6.825}
    for name, (base, spread) in spreads.items():
        noise = np.random.default_rng([zlib.crc32(name.encode()), seed]).standard_normal(out[name].shape)
        drawn = base * np.exp(spread * noise) if base else spread * noise
        out[name] = jnp.asarray(drawn.astype(out[name].dtype))
    for name, factor in factors.items():
        out[name] = (out[name] * factor).astype(out[name].dtype)
    return out
```

```python
from contextlib import ExitStack

import numpy as np

import concourse.bass as bass
from concourse import mybir

F32 = mybir.dt.float32
F32R = mybir.dt.float32r
BF16 = mybir.dt.bfloat16
I32 = mybir.dt.int32
ALU = mybir.AluOpType
ACT = mybir.ActivationFunctionType
AX = mybir.AxisListType

P = 128
BS = 64
DH = 8
HG = 4
LANE = 32
MAX_ROW = 24
EPS = 1e-5
TOP_K = 4

S_SLOTS = 14
B_BANKS = 4
O_BANKS = 2


def make_tables(E):
    ident = np.eye(P, dtype=np.float32)
    tri = np.triu(np.ones((P, P), np.float32))
    spread = np.zeros((P, 4, 4, P), np.float32)
    hi_slots = ((0, 1), (0, 2))
    lo_slots = ((2,), (1,))
    for g in range(4):
        for h in range(HG):
            for d in range(DH):
                src = (g * HG + h) * DH + d
                for qk in range(2):
                    for s in hi_slots[qk]:
                        spread[src, g, 2 * qk, LANE * h + DH * s + d] = 1
                    for s in lo_slots[qk]:
                        spread[src, g, 2 * qk + 1, LANE * h + DH * s + d] = 1
    pairs = np.zeros((P, E // 2, P), np.float32)
    for p in range(E // 2):
        for m in range(P):
            for part in range(2):
                pairs[part * E + 2 * p + m // 64, p, m] = 1
    onesrow = np.zeros((P, 2), np.float32)
    onesrow[MAX_ROW, 0] = 1
    onesrow[MAX_ROW + 1, 1] = 1
    return ident, tri, spread.reshape(P, -1), pairs.reshape(P, -1), onesrow


class Item:

    def __init__(self, ring, kind, arg, bank, use, seq):
        self.ring, self.kind, self.arg, self.bank, self.use, self.seq = ring, kind, arg, bank, use, seq


P_ITEMS = ([("main", j) for j in range(8)] + [("corner", jj) for jj in range(4)]
           + [("col", (half, h)) for half in range(2) for h in range(HG)] + [("row", j) for j in range(8)])
S_ITEMS = []
for _jj in range(4):
    S_ITEMS += [("s_main", 2 * _jj), ("s_main", 2 * _jj + 1), ("s_corner", _jj)]
S_ITEMS += [("s_col", j) for j in range(8)] + [("s_row", (h, half)) for h in range(HG) for half in range(2)]
MAX_ITEMS = 20
JOB_END = {11: (0, 1), 15: (2,), 19: (3,), 27: (4,)}


def plan_attention(groups, batch_steps):
    uses, a_seq, plans = [0, 0], 0, []
    for n in range(groups + 1):
        has_s, has_p = n < groups, n >= 1
        fresh = has_s and n % batch_steps == 0
        early = []
        if fresh:
            early += [("proj", (w, c)) for w in (1, 0) for c in range(3)]
        if has_s:
            early += [("spread", (w, c)) for w in (1, 0) for c in range(3)]
        scores = list(S_ITEMS) if has_s else []
        order = []
        if has_p:
            order += [("P", i) for i in range(3)]
            n_scores, given = len(scores), 0
            for i in range(28):
                if i + 3 < 28:
                    order.append(("P", i + 3))
                for _ in range(2):
                    if early:
                        order.append(("A",) + early.pop(0))
                if i >= 8:
                    want = min(n_scores, (i - 7) * n_scores // 18)
                    while given < want:
                        order.append(("A",) + scores[given])
                        given += 1
                if has_s and given >= MAX_ITEMS + 1 and ("A", "maxT", 0) not in order:
                    order.append(("A", "maxT", 0))
                if i in (15, 16, 22, 23):
                    order.append(("A", "ot", (15, 16, 22, 23).index(i)))
                order.append(("PV", i))
            assert given == n_scores and not early
        else:
            order += [("A",) + x for x in early + scores[:MAX_ITEMS + 1]] + [("A", "maxT", 0)]
            order += [("A",) + x for x in scores[MAX_ITEMS + 1:]]
        if has_s:
            order.append(("A", "maxT", 1))
        if has_p:
            order.append(("A", "ot", 4))
        if fresh:
            order += [("A", "vproj", c) for c in range(4)]
        plan = []
        for o in order:
            if o[0] == "A":
                bank = a_seq % 2
                plan.append(Item("A", o[1], o[2], bank, uses[bank], a_seq))
                uses[bank] += 1
                a_seq += 1
            else:
                seq = 28 * (n - 1) + o[1]
                plan.append(Item(o[0], *P_ITEMS[o[1]], seq % B_BANKS, seq, o[1]))
        plans.append(plan)
    return plans


V_TILES = ((0, 3), (3, 6), (6, 8), (8, 9))
CHUNKS = ((0, 512), (512, 1024), (1024, 1152))


class Step:

    def __init__(self, n, it=None):
        self.n, self.it = n, it

    def value(self, f):
        a = f(self.n)
        if self.it is None:
            return a
        d = f(self.n + 4) - a
        assert f(self.n + 8) - f(self.n + 4) == d, (self.n, a, d)
        return self.it * d + a

    def wait(self, eng, sem, f):
        v = self.value(f)
        if isinstance(v, int) and v <= 0:
            return
        eng.wait_ge(sem, v)


    def gate(self, eng, passed, sem, f):
        self.wait(eng, sem, f)
        if self.it is not None:
            eng.sem_inc(passed, 1)


def run_steps(eng, step_fn, groups):
    step_fn(Step(0))
    with eng.Fori(0, groups // 4 - 1) as it:
        for k in range(4):
            step_fn(Step(1 + k, it))
    for n in range(groups - 3, groups + 1):
        step_fn(Step(n))


def build_attention(nc, ctx, d, scratch):
    x_t, gidx = d["xT"], d["gidx"]
    NTOK = x_t.shape[1]
    N = 1024
    B = NTOK // N
    NT = N // P
    NB = N // BS
    H = 16
    GROUPS = B * H // HG
    NG = N + 2 * BS
    SCALE = 1.0 / float(np.sqrt(np.float32(DH)))
    plans = plan_attention(GROUPS, 4)

    def find(n, kind, arg):
        for x in plans[n]:
            if x.ring == "A" and x.kind == kind and x.arg == arg:
                return x
        raise KeyError((n, kind, arg))

    def sb(name, shape, dt=F32):
        return ctx.enter_context(nc.sbuf_tensor(name, shape, dt))

    def sem(name):
        return ctx.enter_context(nc.semaphore(name))

    idx_sb = sb("idx_sb", [1, 2], I32)
    xT = sb("batch_xT", [P, NG])
    wqkv = sb("wqkv", [P, 3, P])
    bqk = sb("bqk", [P, 2])
    bv_all = sb("bv_all", [P, P])
    ident = sb("ident_a", [P, P])
    onesrow = sb("onesrow", [P, 2])
    spread_f = sb("spread_f", [P, 4 * P])
    spread = sb("spread", [P, 4, 4, P], F32R)
    qk_hi = sb("qk_hi", [P, 2, NG], F32R)
    qk_lo = sb("qk_lo", [P, 2, NG], F32R)
    q_stack = sb("q_stack", [P, NG], F32R)
    k_stack = sb("k_stack", [P, 2, NG], F32R)
    q_padded = sb("q_padded", [P, NT, 3, BS], F32R)
    k_padded = sb("k_padded", [P, 2, NT, 3, BS], F32R)
    k_heads = sb("k_heads", [P, HG, NG], F32R)
    q_heads = sb("q_heads", [P, 2, HG, N], F32R)
    q_rows = sb("q_rows", [P, 2, HG, P], F32R)
    v_aug = sb("v_aug", [P, NT + 1, H, DH + 1])
    v_top = sb("v_top", [P, NT, H, DH + 1])
    v_bot = sb("v_bot", [P, NT, H, DH + 1])
    probs = sb("probs", [P, S_SLOTS, 512])
    mx_main = sb("mx_main", [P, HG, NT])
    mx_padded = sb("mx_padded", [P, 2 * HG * NT + HG])
    mx_query = mx_padded[:, 0:2 * HG * NT].rearrange("p (k h t) -> p k h t", k=2, h=HG)
    mx_gathered = sb("mx_gathered", [P, HG])
    mx_corner = sb("mx_corner", [P, HG * NT])
    mx_row = sb("mx_row", [P, HG, 2])
    neg_query = sb("neg_query", [2 * HG * NT, P], F32R)
    neg_gathered = sb("neg_gathered", [HG, P], F32R)
    out_t = sb("out_t", [P, 2 * N + P])
    recip = sb("recip", [P, 5, 16])
    col_tmp = sb("col_tmp", [P, 4, HG, DH])
    heads_out = sb("heads_out", [P, NT, P])
    rows_out = sb("rows_out", [P, P])

    a_psum = [ctx.enter_context(nc.psum_tensor(f"a_psum{i}", [P, 512], F32)) for i in range(2)]
    b_psum = [ctx.enter_context(nc.psum_tensor(f"b_psum{i}", [P, 512], F32)) for i in range(B_BANKS)]
    o_psum = [ctx.enter_context(nc.psum_tensor(f"o_psum{i}", [P, 512], F32)) for i in range(O_BANKS)]

    idx_loaded = sem("idx_loaded")
    consts_loaded = sem("consts_loaded")
    spread_loaded = sem("spread_loaded")
    spread_cast = sem("spread_cast")
    x_loaded = sem("x_loaded")
    pool_zeroed = sem("pool_zeroed")
    dve_zeroed = sem("dve_zeroed")
    a_ready = [sem(f"a_ready{i}") for i in range(2)]
    a_free = [sem(f"a_free{i}") for i in range(2)]
    hi_done = sem("hi_done")
    stack_done = sem("stack_done")
    s_operands_done = sem("s_operands_done")
    p_operands_done = sem("p_operands_done")
    max_done = sem("max_done")
    neg_max_done = sem("neg_max_done")
    query_max_moved = sem("query_max_moved")
    gathered_max_moved = sem("gathered_max_moved")
    v_halves = sem("v_halves")
    b_ready = sem("b_ready")
    exp_done = sem("exp_done")
    pv_done = sem("pv_done")
    o_copied = sem("o_copied")
    recip_done = sem("recip_done")
    tmp_done = sem("tmp_done")
    ctx_stored = sem("ctx_stored")
    pool_passed = sem("pool_passed")
    sp_passed = sem("sp_passed")

    def batch_of(n):
        return n // 4

    def v_count(n):
        return (n - 1) // 4 + 1

    def by_block(stack):
        return stack[:, 0:N].bitcast(F32).rearrange("p (t b c) -> p t b c", b=2, c=BS)

    def job(n, j):
        return 5 * (n - 1) + j


    with nc.Block() as block:

        @block.sync
        def _(sp):
            sp.sem_inc(ctx_stored, 16)
            sp.dma_start(idx_sb[:], gidx.rearrange("(o n) -> o n", o=1)).then_inc(idx_loaded, 16)
            sp.dma_start(wqkv[:], d["wqkvT"].rearrange("w i o -> i w o")).then_inc(consts_loaded, 16)
            sp.dma_start(bqk[:, 0:1], d["bq"].rearrange("(p o) -> p o", o=1)).then_inc(consts_loaded, 16)
            sp.dma_start(bqk[:, 1:2], d["bk"].rearrange("(p o) -> p o", o=1)).then_inc(consts_loaded, 16)
            sp.dma_start(bv_all[:], d["bv"].partition_broadcast(P)).then_inc(consts_loaded, 16)
            sp.dma_start(ident[:], d["t_ident"]).then_inc(consts_loaded, 16)
            sp.dma_start(onesrow[:], d["t_onesrow"]).then_inc(consts_loaded, 16)
            sp.wait_ge(idx_loaded, 16)
            first = [sp.snap((sp.value_load(idx_sb[0:1, i:i + 1], min_val=-NB, max_val=NB - 1) + NB) % NB)
                     for i in range(2)]

            def load_x(b):
                sp.dma_start(xT[:, 0:N], x_t[:, bass.ds(b * N, N)]).then_inc(x_loaded, 16)
                for i in range(2):
                    sp.dma_start(xT[:, N + i * BS:N + (i + 1) * BS],
                                 x_t[:, bass.ds(b * N + first[i] * BS, BS)]).then_inc(x_loaded, 16)

            load_x(0)
            for g in range(4):
                if g:
                    sp.wait_ge(spread_cast, g)
                sp.dma_start(spread_f[:], d["t_spread"][:, g * 4 * P:(g + 1) * 4 * P]).then_inc(spread_loaded, 16)

            def step(s):
                n = s.n
                if n % 4 == 1 and (s.it is None and n < GROUPS - 3 or s.it is not None):
                    last_v = find(n - 1, "vproj", 3)
                    s.gate(sp, sp_passed, a_ready[last_v.bank], lambda m: find(m - 1, "vproj", 3).use + 1)
                    load_x((s.it if s.it is not None else n // 4) + 1)
                if n < GROUPS:
                    par = n % 2
                    s.wait(sp, neg_max_done, lambda m: 2 * m + 1)
                    sp.dma_start(q_heads[MAX_ROW:MAX_ROW + 2, par, :, :].bitcast(F32).rearrange(
                        "r h k -> r (h k)"), neg_query[:].bitcast(F32)).then_inc(query_max_moved, 16)
                    s.wait(sp, neg_max_done, lambda m: 2 * m + 2)
                    sp.dma_start(q_rows[MAX_ROW:MAX_ROW + 1, par, :, :].bitcast(F32).rearrange(
                        "r h k -> r (h k)"), neg_gathered[:].bitcast(F32)).then_inc(gathered_max_moved, 16)
                if n % 4 == 0 and n > 0:
                    b = (s.it if s.it is not None else n // 4 - 1)
                    for k in (3, 4):
                        x = find(n, "ot", k)
                        s.gate(sp, sp_passed, a_free[x.bank], lambda m, k=k: find(m, "ot", k).use + 1)
                    sp.dma_start(scratch[bass.ds(b * N, N), :].rearrange("(t p) c -> p t c", p=P),
                                 heads_out[:]).then_inc(ctx_stored, 16)
                    for i in range(2):
                        s.gate(sp, sp_passed, ctx_stored, lambda m, i=i: 16 + 48 * (m // 4 - 1) + 16 * (i + 1))
                        sp.dma_start(scratch[bass.ds(b * N + first[i] * BS, BS), :],
                                     rows_out[i * BS:(i + 1) * BS, :]).then_inc(ctx_stored, 16)

            run_steps(sp, step, GROUPS)
            sp.wait_ge(ctx_stored, 16 + 48 * B)

        @block.gpsimd
        def _(pool):
            pool.memset(q_padded[:, :, 1, :].bitcast(F32), 0.0).then_inc(pool_zeroed, 1)
            pool.memset(v_top[:], 0.0).then_inc(pool_zeroed, 1)
            pool.memset(v_bot[:], 0.0).then_inc(pool_zeroed, 1)
            pool.memset(v_aug[:, :, :, DH:DH + 1], 1.0).then_inc(pool_zeroed, 1)
            pool.wait_ge(pool_zeroed, 4)
            pool.memset(v_top[0:BS, :, :, DH:DH + 1], 1.0).then_inc(pool_zeroed, 1)
            pool.wait_ge(pool_zeroed, 5)
            pool.memset(v_bot[BS:P, :, :, DH:DH + 1], 1.0).then_inc(pool_zeroed, 1)
            pool.wait_ge(pool_zeroed, 6)
            pool.memset(q_heads[:].bitcast(F32), 0.0).then_inc(pool_zeroed, 1)
            pool.memset(q_rows[:].bitcast(F32), 0.0).then_inc(pool_zeroed, 1)
            pool.memset(mx_padded[:], 0.0).then_inc(pool_zeroed, 1)
            pool.wait_ge(pool_zeroed, 9)

            def step(s):
                if s.n >= GROUPS:
                    return
                par = s.n % 2
                s.gate(pool, pool_passed, stack_done, lambda m: 6 * m + 6)
                pool.tensor_copy(k_padded[:, par, :, 0:3:2, :], by_block(k_stack[:, par, :])
                                 ).then_inc(p_operands_done, 1)
                for h in range(HG):
                    rows = slice(LANE * h, LANE * h + 3 * DH)
                    s.gate(pool, pool_passed, p_operands_done, lambda m: 9 * m + 1 + 2 * h)
                    pool.tensor_copy(q_heads[rows, par, h, :], q_stack[rows, 0:N].bitcast(F32)
                                     ).then_inc(p_operands_done, 1)
                    pool.tensor_copy(q_rows[rows, par, h, :], q_stack[rows, N:NG].bitcast(F32)
                                     ).then_inc(p_operands_done, 1)

            run_steps(pool, step, GROUPS)

        @block.scalar
        def _(act):
            act.sem_inc(exp_done, B_BANKS)
            act.sem_inc(o_copied, O_BANKS)
            act.wait_ge(consts_loaded, 96)
            act.wait_ge(dve_zeroed, 3)
            act.wait_ge(pool_zeroed, 9)

            def a_item(s, x):
                src = a_psum[x.bank]
                if x.kind not in ("proj", "spread", "maxT"):
                    return
                s.wait(act, a_ready[x.bank], lambda m: find(m, x.kind, x.arg).use + 1)
                if x.kind == "proj":
                    w, c = x.arg
                    lo, hi = CHUNKS[c]
                    act.activation(qk_hi[:, w, lo:hi], src[:, 0:hi - lo], ACT.Identity,
                                   bias=bqk[:, w:w + 1]).then_inc(hi_done, 1)
                elif x.kind == "spread":
                    w, c = x.arg
                    par = s.n % 2
                    lo, hi = CHUNKS[c]
                    if w == 0:
                        if c == 0:
                            s.wait(act, p_operands_done, lambda m: 9 * m)
                        act.copy(q_stack[:, lo:hi], src[:, 0:hi - lo]).then_inc(stack_done, 1)
                    else:
                        act.activation(k_stack[:, par, lo:hi], src[:, 0:hi - lo], ACT.Identity,
                                       bias=onesrow[:, c // 2:c // 2 + 1]).then_inc(stack_done, 1)
                else:
                    if x.arg == 0:
                        s.wait(act, query_max_moved, lambda m: 16 * m)
                        act.mul(neg_query[:], src[0:2 * HG * NT, 0:P], -1.0).then_inc(neg_max_done, 1)
                    else:
                        s.wait(act, gathered_max_moved, lambda m: 16 * m)
                        act.mul(neg_gathered[:], src[0:HG, 0:P], -1.0).then_inc(neg_max_done, 1)

            def step(s):
                for x in plans[s.n]:
                    if x.ring == "A":
                        a_item(s, x)
                    elif x.ring == "P":
                        i = x.seq
                        s.wait(act, b_ready, lambda m: 28 * (m - 1) + i + 1)
                        s.wait(act, pv_done, lambda m: 28 * (m - 1) + i + 1)
                        act.activation(probs[:, x.use % S_SLOTS, :], b_psum[x.bank][:], ACT.Exp,
                                       scale=SCALE).then_inc(exp_done, 1)
                    else:
                        for j in JOB_END.get(x.seq, ()):
                            s.wait(act, pv_done, lambda m: S_SLOTS + 28 * (m - 1) + x.seq + 1)
                            width = 512 if j < 4 else P
                            act.copy(out_t[:, 512 * j:512 * j + width],
                                     o_psum[job(s.n, j) % 2][:, 0:width]).then_inc(o_copied, 1)

            run_steps(act, step, GROUPS)

        @block.vector
        def _(dve):
            dve.memset(k_padded[:, :, :, 1, :].bitcast(F32), 0.0).then_inc(dve_zeroed, 1)
            dve.memset(k_heads[:].bitcast(F32), 0.0).then_inc(dve_zeroed, 1)
            for i in range(O_BANKS):
                last = dve.memset(o_psum[i][:], 0.0)
            last.then_inc(dve_zeroed, 1)
            for g in range(4):
                dve.wait_ge(spread_loaded, 16 * (g + 1))
                dve.tensor_copy(spread[:, g, :, :], spread_f[:].rearrange("p (k c) -> p k c", k=4)
                                ).then_inc(spread_cast, 1)
            dve.wait_ge(consts_loaded, 96)
            dve.wait_ge(dve_zeroed, 3)
            dve.wait_ge(pool_zeroed, 9)

            def maxima_of(s, x):
                src = a_psum[x.bank]
                if x.kind == "s_main":
                    return dve.reduce_max(mx_main[:, :, x.arg], src[:].rearrange("p (h k) -> p h k", h=HG),
                                          axis=AX.X)
                if x.kind == "s_corner":
                    out = mx_corner[:].rearrange("p (h t) -> p t h", t=NT)[:, 2 * x.arg:2 * x.arg + 2, :]
                    return dve.reduce_max(out, src[:].rearrange("p (t h k) -> p t h k", t=2, h=HG), axis=AX.X)
                if x.kind == "s_col":
                    return dve.reduce_max(mx_query[:, 1, :, x.arg], src[:].rearrange("p (h k) -> p h k", h=HG),
                                          axis=AX.X)
                h, half = x.arg
                return dve.reduce_max(mx_row[:, h, half:half + 1], src[:], axis=AX.X)

            def outputs_of(s, x):
                j = x.arg
                tiles = 4 if j < 4 else 1
                src = a_psum[x.bank][:, 0:tiles * P].rearrange("p (t h c) -> p t h c", t=tiles, h=HG)
                rec = recip[:, j, 0:tiles * HG].rearrange("p (t h) -> p t h", t=tiles)
                dve.reciprocal(rec, src[:, :, :, DH]).then_inc(recip_done, 1)
                s.wait(dve, recip_done, lambda m: job(m, j) + 1)
                rec = rec.unsqueeze(3).to_broadcast([P, tiles, HG, DH])
                g = (s.n - 1) % 4
                num = src[:, :, :, 0:DH]
                if j == 4:
                    dst = rows_out[:, LANE * g:LANE * (g + 1)].rearrange("p (h c) -> p h c", h=HG)
                    return dve.tensor_tensor(dst, num[:, 0], rec[:, 0], ALU.mult)
                half = j % 2
                dst = heads_out[:, 4 * half:4 * half + 4, LANE * g:LANE * (g + 1)].rearrange(
                    "p t (h c) -> p t h c", h=HG)
                if j < 2:
                    return dve.tensor_tensor(dst, num, rec, ALU.mult)
                local, tmp_user = find(s.n, "ot", j - 2), find(s.n, "ot", 2)
                if j == 3:
                    s.wait(dve, a_free[tmp_user.bank], lambda m: find(m, "ot", 2).use + 1)
                if j == 2 or local.bank != tmp_user.bank:
                    s.wait(dve, a_free[local.bank], lambda m: find(m, "ot", j - 2).use + 1)
                dve.tensor_tensor(col_tmp[:], num, rec, ALU.mult).then_inc(tmp_done, 1)
                s.wait(dve, tmp_done, lambda m: 2 * (m - 1) + half + 1)
                return dve.tensor_tensor(dst, dst, col_tmp[:], ALU.add)

            def a_item(s, x):
                src = a_psum[x.bank]

                def ready():
                    s.wait(dve, a_ready[x.bank], lambda m: find(m, x.kind, x.arg).use + 1)

                if x.kind == "proj":
                    w, c = x.arg
                    lo, hi = CHUNKS[c]
                    s.wait(dve, hi_done, lambda m: 6 * (m // 4) + 3 * (1 - w) + c + 1)
                    dve.scalar_tensor_tensor(out=qk_lo[:, w, lo:hi], in0=src[:, 0:hi - lo],
                                             scalar=bqk[:, w:w + 1], in1=qk_hi[:, w, lo:hi].bitcast(F32),
                                             op0=ALU.add, op1=ALU.subtract).then_inc(a_free[x.bank], 1)
                elif x.kind == "spread":
                    w, c = x.arg
                    s.wait(dve, stack_done, lambda m: 6 * m + 3 * (1 - w) + c + 1)
                    dve.sem_inc(a_free[x.bank], 1)
                    if (w, c) == (1, 2):
                        par = s.n % 2
                        for h in range(HG):
                            rows = slice(LANE * h, LANE * h + 3 * DH)
                            dve.tensor_copy(k_heads[rows, h, :], k_stack[rows, par, :].bitcast(F32)
                                            ).then_inc(s_operands_done, 1)
                    if (w, c) == (0, 2):
                        dve.tensor_copy(q_padded[:, :, 0:3:2, :], by_block(q_stack[:, :])
                                        ).then_inc(s_operands_done, 1)
                elif x.kind == "maxT":
                    s.wait(dve, neg_max_done, lambda m: 2 * m + x.arg + 1)
                    dve.sem_inc(a_free[x.bank], 1)
                elif x.kind == "vproj":
                    ready()
                    t0, t1 = V_TILES[x.arg]
                    dve.tensor_tensor(v_aug[:, t0:t1, :, 0:DH],
                                      src[:, 0:(t1 - t0) * P].rearrange("p (t h c) -> p t h c", h=H, c=DH),
                                      bv_all[:].rearrange("p (h c) -> p h c", h=H).unsqueeze(1).to_broadcast(
                                          [P, t1 - t0, H, DH]), ALU.add).then_inc(a_free[x.bank], 1)
                    if x.arg == 3:
                        for k in (2, 3):
                            y = find(s.n, "vproj", k)
                            s.wait(dve, a_free[y.bank], lambda m, k=k: find(m, "vproj", k).use + 1)
                        dve.tensor_copy(v_top[0:BS, :, :, 0:DH], v_aug[0:BS, 0:NT, :, 0:DH]).then_inc(v_halves, 1)
                        dve.tensor_copy(v_bot[BS:P, :, :, 0:DH], v_aug[BS:P, 0:NT, :, 0:DH]).then_inc(v_halves, 1)
                elif x.kind == "ot":
                    ready()
                    if s.n % 4 == 1 and x.arg == 0:
                        s.wait(dve, ctx_stored, lambda m: 16 + 48 * (m // 4))
                    outputs_of(s, x).then_inc(a_free[x.bank], 1)
                else:
                    ready()
                    maxima_of(s, x).then_inc(a_free[x.bank], 1)
                    for last_item in (MAX_ITEMS - 1, len(S_ITEMS) - 1):
                        if (x.kind, x.arg) != S_ITEMS[last_item]:
                            continue
                        for k in (last_item, last_item - 1):
                            y = find(s.n, *S_ITEMS[k])
                            s.wait(dve, a_free[y.bank], lambda m, k=k: find(m, *S_ITEMS[k]).use + 1)
                        if last_item == MAX_ITEMS - 1:
                            dve.tensor_tensor(mx_query[:, 0], mx_main[:], mx_corner[:].rearrange(
                                "p (h t) -> p h t", h=HG), ALU.max).then_inc(max_done, 1)
                        else:
                            dve.reduce_max(mx_gathered[:], mx_row[:], axis=AX.X).then_inc(max_done, 1)

            def step(s):
                for x in plans[s.n]:
                    if x.ring == "A":
                        a_item(s, x)

            run_steps(dve, step, GROUPS)

        @block.tensor
        def _(pe):
            pe.sem_inc(pv_done, S_SLOTS)
            pe.wait_ge(consts_loaded, 96)
            pe.wait_ge(spread_cast, 4)
            pe.wait_ge(dve_zeroed, 3)
            pe.wait_ge(pool_zeroed, 9)

            def local_scores(out_main, out_corner, stack, padded, heads, kind, j):
                if kind == "main":
                    return pe.matmul(out_main, stack[:, j * P:(j + 1) * P], heads[:, :, j * P:(j + 1) * P],
                                     start=True, stop=True)
                before, after = (2 * j - 1) % NB, (2 * j + 2) % NB
                pe.matmul(out_corner, padded[:, j, 0:2, :], heads[:, :, before * BS:(before + 1) * BS],
                          start=True, stop=False)
                return pe.matmul(out_corner, padded[:, j, 1:3, :], heads[:, :, after * BS:(after + 1) * BS],
                                 start=False, stop=True)

            def four(bank, n=P):
                return bank[:].rearrange("p (h k) -> p h k", h=HG)

            def pair(bank, i):
                return bank[:, i * 256:(i + 1) * 256].rearrange("p (h k) -> p h k", h=HG)

            def a_item(s, x):
                out = a_psum[x.bank]
                if x.kind == "proj" and x.arg == (1, 0):
                    s.wait(pe, x_loaded, lambda m: 48 * (m // 4 + 1))
                if x.kind == "spread" and x.arg == (1, 0) and s.n % 4 == 0:
                    for k in ((0, 1), (0, 2)):
                        y = find(s.n, "proj", k)
                        s.wait(pe, a_free[y.bank], lambda m, k=k: find(m, "proj", k).use + 1)
                if x.kind == "s_main" and x.arg == 0:
                    s.wait(pe, s_operands_done, lambda m: 5 * m + 5)
                    s.wait(pe, stack_done, lambda m: 6 * m + 6)
                if x.kind == "maxT":
                    s.wait(pe, max_done, lambda m: 2 * m + x.arg + 1)
                if x.kind == "ot":
                    s.wait(pe, o_copied, lambda m: O_BANKS + job(m, x.arg) + 1)
                s.wait(pe, a_free[x.bank], lambda m: find(m, x.kind, x.arg).use)
                if x.kind == "proj":
                    w, c = x.arg
                    lo, hi = CHUNKS[c]
                    last = pe.matmul(out[:, 0:hi - lo], wqkv[:, w, :], xT[:, lo:hi], start=True, stop=True)
                elif x.kind == "vproj":
                    t0, t1 = V_TILES[x.arg]
                    for t in range(t0, t1):
                        last = pe.matmul(out[:, (t - t0) * P:(t - t0 + 1) * P], xT[:, t * P:(t + 1) * P],
                                         wqkv[:, 2, :], start=True, stop=True)
                elif x.kind == "spread":
                    w, c = x.arg
                    g = s.n % 4
                    lo, hi = CHUNKS[c]
                    pe.matmul(out[:, 0:hi - lo], spread[:, g, 2 * w, :], qk_hi[:, w, lo:hi], start=True, stop=False)
                    last = pe.matmul(out[:, 0:hi - lo], spread[:, g, 2 * w + 1, :], qk_lo[:, w, lo:hi],
                                     start=False, stop=True)
                elif x.kind == "s_main":
                    last = local_scores(four(out), None, q_stack, q_padded, k_heads, "main", x.arg)
                elif x.kind == "s_corner":
                    for i in range(2):
                        last = local_scores(None, pair(out, i), q_stack, q_padded, k_heads, "corner", 2 * x.arg + i)
                elif x.kind == "s_col":
                    last = pe.matmul(four(out), q_stack[:, x.arg * P:(x.arg + 1) * P], k_heads[:, :, N:NG],
                                     start=True, stop=True)
                elif x.kind == "s_row":
                    h, half = x.arg
                    last = pe.matmul(out[:], q_stack[:, N:NG], k_heads[:, h, half * 512:(half + 1) * 512],
                                     start=True, stop=True)
                elif x.kind == "maxT":
                    maxima = (mx_padded[:], mx_gathered[:])[x.arg]
                    last = pe.transpose(out[0:maxima.shape[1], 0:P], maxima, ident[:])
                else:
                    j = x.arg
                    for t in range(4 if j < 4 else 1):
                        last = pe.transpose(out[:, t * P:(t + 1) * P],
                                            out_t[:, 512 * j + t * P:512 * j + (t + 1) * P], ident[:])
                last.then_inc(a_ready[x.bank], 1)

            def scores_t(s, x):
                i = x.seq
                par = (s.n - 1) % 2
                if i == 0:
                    s.wait(pe, p_operands_done, lambda m: 9 * m)
                    s.wait(pe, query_max_moved, lambda m: 16 * m)
                if i == MAX_ITEMS:
                    s.wait(pe, gathered_max_moved, lambda m: 16 * m)
                s.wait(pe, exp_done, lambda m: 28 * (m - 1) + i + 1)
                out = b_psum[x.bank]
                ks, kp, qh, qr = k_stack[:, par], k_padded[:, par], q_heads[:, par], q_rows[:, par]
                if x.kind == "main":
                    last = local_scores(four(out), None, ks, kp, qh, "main", x.arg)
                elif x.kind == "corner":
                    for k in range(2):
                        last = local_scores(None, pair(out, k), ks, kp, qh, "corner", 2 * x.arg + k)
                elif x.kind == "col":
                    half, h = x.arg
                    last = pe.matmul(out[:], ks[:, N:NG], qh[:, h, half * 512:(half + 1) * 512],
                                     start=True, stop=True)
                else:
                    last = pe.matmul(four(out), ks[:, x.arg * P:(x.arg + 1) * P], qr[:, :, :], start=True, stop=True)
                last.then_inc(b_ready, 1)

            def weighted_v(s, x):
                i = x.seq
                g = (s.n - 1) % 4
                if i == 0:
                    s.wait(pe, v_halves, lambda m: 2 * v_count(m))
                for j, first_item in ((0, 0), (1, 4), (2, 12), (3, 16), (4, 20)):
                    if i == first_item:
                        s.wait(pe, o_copied, lambda m: job(m, j) + 1)
                s.wait(pe, exp_done, lambda m: B_BANKS + 28 * (m - 1) + i + 1)
                probs_i = probs[:, x.use % S_SLOTS, :]
                for h in range(HG):
                    hh = HG * g + h
                    rows = slice(LANE * h, LANE * h + DH + 1)
                    if x.kind == "main":
                        j = x.arg
                        last = pe.matmul(o_psum[job(s.n, j // 4) % 2][rows, (j % 4) * P:(j % 4 + 1) * P],
                                         v_aug[:, j, hh, :], probs_i[:, h * P:(h + 1) * P],
                                         start=j % 4 == 0, stop=False)
                    elif x.kind == "corner":
                        for k in range(2):
                            j = 2 * x.arg + k
                            for v, blk in ((v_top, (2 * j - 1) % NB), (v_bot, (2 * j + 2) % NB)):
                                half, c = blk // 8, blk % 8
                                last = pe.matmul(o_psum[job(s.n, half) % 2][rows, c * BS:(c + 1) * BS],
                                                 v[:, j, hh, :], probs_i[:, k * 256 + h * BS:k * 256 + (h + 1) * BS],
                                                 start=False, stop=j == NT - 1)
                    elif x.kind == "col":
                        half, hx = x.arg
                        if hx != h:
                            continue
                        last = pe.matmul(o_psum[job(s.n, 2 + half) % 2][rows, :], v_aug[:, NT, hh, :], probs_i,
                                         start=True, stop=True)
                    else:
                        j = x.arg
                        last = pe.matmul(o_psum[job(s.n, 4) % 2][rows, 0:P], v_aug[:, j, hh, :],
                                         probs_i[:, h * P:(h + 1) * P], start=j == 0, stop=j == NT - 1)
                last.then_inc(pv_done, 1)

            def step(s):
                for x in plans[s.n]:
                    if x.ring == "A":
                        a_item(s, x)
                    elif x.ring == "P":
                        scores_t(s, x)
                    else:
                        weighted_v(s, x)

            run_steps(pe, step, GROUPS)


def build_experts(nc, ctx, d, scratch, out):
    NTOK = scratch.shape[0]
    C = 512
    CT = C // P
    ITERS = NTOK // C
    E, _, HE = d["W1"].shape
    PAIRS = E // 2
    UNITS = PAIRS + 1
    CAPACITY = 4 * NTOK * TOP_K // E

    def sb(name, shape, dt=F32):
        return ctx.enter_context(nc.sbuf_tensor(name, shape, dt))

    def sem(name):
        return ctx.enter_context(nc.semaphore(name))

    ident = sb("ident_b", [P, P])
    tri_f = sb("tri_f", [P, P])
    tri = sb("tri", [P, P], BF16)
    ones = sb("ones", [P, P], BF16)
    wo_t = sb("wo_t", [P, P])
    bo_all = sb("bo_all", [P, P])
    wg = sb("wg", [P, E])
    eps = sb("eps", [P, 1])
    w13_raw = sb("w13_raw", [P, E + 2, HE])
    w13_hi = sb("w13_hi", [P, 2, E + 2, HE], F32R)
    w13_lo = sb("w13_lo", [P, 2, E + 2, HE], F32R)
    w2 = sb("w2", [P, UNITS, P])
    pair_sel_f = sb("pair_sel_f", [P, PAIRS * P])
    pair_sel = sb("pair_sel", [P, PAIRS, P], F32R)
    x_hi = sb("x_hi", [P, NTOK], F32R)
    x_lo = sb("x_lo", [P, NTOK], F32R)
    gates = sb("gates", [P, NTOK], F32R)
    x1_all = sb("x1_all", [P, NTOK // P, P])
    heads = sb("heads", [P, CT, P])
    x_res = sb("x_res", [P, CT, P])
    heads_t = sb("heads_t", [P, C])
    y1 = sb("y1", [P, CT, P])
    y1b = sb("y1b", [P, CT, P])
    stats = sb("stats", [P, CT, 6])
    moments = sb("moments", [P, CT, 2])
    std = sb("std", [P, CT])
    rstd = sb("rstd", [P, CT])
    x1 = sb("x1", [P, CT, P])
    x1_t = sb("x1_t", [P, C])
    logits = sb("logits", [P, CT, E])
    top8 = sb("top8", [P, CT, 8])
    shifted = sb("shifted", [P, CT, E])
    expd = sb("expd", [P, CT, E])
    esum = sb("esum", [P, CT])
    rsum = sb("rsum", [P, CT])
    above = sb("above", [P, CT, E])
    equal = sb("equal", [P, CT, E])
    n_above = sb("n_above", [P, CT])
    nth_equal = sb("nth_equal", [P, CT, E])
    place = sb("place", [P, CT, E])
    taken = sb("taken", [P, CT, E])
    chosen = sb("chosen", [P, CT, E], BF16)
    before = sb("before", [P, CT + 1, E], BF16)
    kept = sb("kept", [P, CT, E])
    kept_e = sb("kept_e", [P, CT, E])
    weight = sb("weight", [P, CT, E])
    silu = sb("silu", [P, 2, C])
    gated = sb("gated", [P, 2, C])
    hidden = sb("hidden", [P, 2, C])
    y_t = sb("y_t", [P, C])
    z = sb("z", [P, CT, P])
    stats2 = sb("stats2", [P, CT, 6])
    moments2 = sb("moments2", [P, CT, 2])
    std2 = sb("std2", [P, CT])
    rstd2 = sb("rstd2", [P, CT])
    result = sb("result", [P, CT, P])

    chain_psum = [ctx.enter_context(nc.psum_tensor(f"chain_psum{i}", [P, 512], F32)) for i in range(2)]
    up_psum = [ctx.enter_context(nc.psum_tensor(f"up_psum{i}", [P, 2, 512], F32)) for i in range(2)]
    gate_psum = ctx.enter_context(nc.psum_tensor("gate_psum", [P, 512], F32))
    y_psum = ctx.enter_context(nc.psum_tensor("y_psum", [P, 512], F32))

    small_loaded = sem("small_loaded")
    w13_loaded = sem("w13_loaded")
    w2_loaded = sem("w2_loaded")
    w_hi_done = sem("w_hi_done")
    w_lo_done = sem("w_lo_done")
    setup_done = sem("setup_done")
    gates_zeroed = sem("gates_zeroed")
    ctx_loaded = sem("ctx_loaded")
    chain_pe = sem("chain_pe")
    chain_act = sem("chain_act")
    chain_dve = sem("chain_dve")
    x1_kept = sem("x1_kept")
    up_ready = sem("up_ready")
    gate_ready = sem("gate_ready")
    silu_done = sem("silu_done")
    gated_done = sem("gated_done")
    hidden_done = sem("hidden_done")
    down_done = sem("down_done")
    y_copied = sem("y_copied")
    y_turned = sem("y_turned")
    ln2_dve = sem("ln2_dve")
    ln2_act = sem("ln2_act")
    stored = sem("stored")
    dve_passed = sem("dve_passed")
    sp_passed = sem("sp2_passed")

    DVE_STEPS = (["residual", "bias"] + [f"stats{t}" for t in range(CT)] + [f"aggr{t}" for t in range(CT)]
                 + ["rstd"] + [f"norm{t}" for t in range(CT)] + ["x_lo", "logits"]
                 + [f"top{t}" for t in range(CT)] + ["shift", "above", "equal", "n_above"]
                 + [f"nth{t}" for t in range(CT)] + ["place", "taken", "chosen"]
                 + [f"before{t}" for t in range(CT)] + ["esum", "rsum", "kept", "kept_e", "weight",
                                                        "gate_lo", "carry"])
    ACT_STEPS = ["heads_t", "std", "x1_t", "x_hi", "exp", "gate_hi"]
    PE_STEPS = ["heads_t", "proj", "x1_t", "route", "rank", "gates"]
    LN2_DVE = (["add"] + [f"stats{t}" for t in range(CT)] + [f"aggr{t}" for t in range(CT)] + ["rstd"]
               + [f"norm{t}" for t in range(CT)])

    def at(steps, name):
        return steps.index(name) + 1

    def w_dve(eng, i, name):
        eng.wait_ge(chain_dve, i * len(DVE_STEPS) + at(DVE_STEPS, name))

    def w_act(eng, i, name):
        eng.wait_ge(chain_act, i * len(ACT_STEPS) + at(ACT_STEPS, name))

    def w_pe(eng, i, name):
        eng.wait_ge(chain_pe, i * len(PE_STEPS) + at(PE_STEPS, name))

    def tiles_of(dram, i):
        return dram[bass.ds(i * C, C), :].rearrange("(t p) c -> p t c", p=P)

    with nc.Block() as block:

        @block.sync
        def _(sp):
            sp.sem_inc(stored, 16)
            small = [(ident[:], d["t_ident"]), (tri_f[:], d["t_tri"]), (wo_t[:], d["WoT"]),
                     (bo_all[:], d["bo"].partition_broadcast(P)), (wg[:], d["Wg"])]
            for dst, src in small:
                sp.dma_start(dst, src).then_inc(small_loaded, 16)

            def load_chunk(i):
                sp.dma_start(heads[:], tiles_of(scratch, i)).then_inc(ctx_loaded, 16)
                sp.dma_start(x_res[:], tiles_of(d["x"], i)).then_inc(ctx_loaded, 16)

            load_chunk(0)
            sp.dma_start(pair_sel_f[:], d["t_pairs"]).then_inc(small_loaded, 16)
            for k, (w, ws) in enumerate((("W1", "Ws1"), ("W3", "Ws3"))):
                if k:
                    sp.wait_ge(w_lo_done, 1)
                sp.dma_start(w13_raw[:, 0:E, :], d[w].rearrange("e i h -> i e h")).then_inc(w13_loaded, 16)
                sp.dma_start(w13_raw[:, E:E + 2, :], d[ws].rearrange("i (e h) -> i e h", e=2)
                             ).then_inc(w13_loaded, 16)
            sp.dma_start(w2[:, 0:PAIRS, :], d["W2"].rearrange("(p e) h o -> (e h) p o", e=2)
                         ).then_inc(w2_loaded, 16)
            sp.dma_start(w2[:, PAIRS, :], d["Ws2"]).then_inc(w2_loaded, 16)
            with sp.Fori(0, ITERS - 1) as i:
                w_pe(sp, i, "heads_t")
                sp.sem_inc(sp_passed, 1)
                w_dve(sp, i, "residual")
                sp.sem_inc(sp_passed, 1)
                load_chunk(i + 1)
            with sp.Fori(0, ITERS) as i:
                sp.wait_ge(ln2_dve, (i + 1) * len(LN2_DVE))
                sp.sem_inc(sp_passed, 1)
                sp.dma_start(tiles_of(out, i), result[:]).then_inc(stored, 16)
            sp.wait_ge(stored, 16 + 16 * ITERS)

        @block.gpsimd
        def _(pool):
            pool.memset(gates[:].bitcast(F32), 0.0).then_inc(gates_zeroed, 1)
            pool.memset(ones[:], 1.0).then_inc(setup_done, 1)
            pool.memset(eps[:], EPS).then_inc(setup_done, 1)

        @block.scalar
        def _(act):
            act.sem_inc(y_copied, 1)
            act.wait_ge(setup_done, 5)
            act.wait_ge(gates_zeroed, 1)
            for k in range(2):
                act.wait_ge(w13_loaded, 32 * (k + 1))
                act.copy(w13_hi[:, k], w13_raw[:]).then_inc(w_hi_done, 1)
            with act.Fori(0, ITERS) as i:
                cols = bass.ds(i * C, C)
                w_pe(act, i, "heads_t")
                act.copy(heads_t[:], chain_psum[0][:]).then_inc(chain_act, 1)
                w_dve(act, i, f"aggr{CT - 1}")
                act.activation(std[:], moments[:, :, 1], ACT.Sqrt, bias=eps[:]).then_inc(chain_act, 1)
                w_pe(act, i, "x1_t")
                act.copy(x1_t[:], chain_psum[0][:]).then_inc(chain_act, 1)
                act.copy(x_hi[:, cols], chain_psum[0][:]).then_inc(chain_act, 1)
                w_dve(act, i, "shift")
                act.activation(expd[:], shifted[:], ACT.Exp).then_inc(chain_act, 1)
                w_pe(act, i, "gates")
                act.copy(gates[0:E, cols], chain_psum[1][0:E, :]).then_inc(chain_act, 1)
            with act.Fori(0, ITERS) as i:
                for u in range(UNITS):
                    act.wait_ge(up_ready, i * UNITS + u + 1)
                    if u >= 2:
                        act.wait_ge(hidden_done, i * UNITS + u)
                    act.activation(silu[:, u % 2], up_psum[u % 2][:, 0], ACT.Silu).then_inc(silu_done, 1)
                act.wait_ge(down_done, (i + 1) * UNITS)
                act.copy(y_t[:], y_psum[:]).then_inc(y_copied, 1)
                act.wait_ge(ln2_dve, i * len(LN2_DVE) + at(LN2_DVE, f"aggr{CT - 1}"))
                act.activation(std2[:], moments2[:, :, 1], ACT.Sqrt, bias=eps[:]).then_inc(ln2_act, 1)

        @block.vector
        def _(dve):
            dve.sem_inc(hidden_done, 1)
            dve.wait_ge(small_loaded, 96)
            dve.tensor_copy(tri[:], tri_f[:]).then_inc(setup_done, 1)
            dve.tensor_copy(pair_sel[:], pair_sel_f[:].rearrange("p (a b) -> p a b", a=PAIRS)
                            ).then_inc(setup_done, 1)
            dve.memset(before[:], 0.0).then_inc(setup_done, 1)
            dve.wait_ge(setup_done, 5)
            dve.wait_ge(gates_zeroed, 1)
            for k in range(2):
                dve.wait_ge(w_hi_done, k + 1)
                dve.tensor_tensor(w13_lo[:, k], w13_raw[:], w13_hi[:, k].bitcast(F32),
                                  ALU.subtract).then_inc(w_lo_done, 1)

            def per_tile(x, width):
                return x.unsqueeze(2).to_broadcast([P, CT, width])

            with dve.Fori(0, ITERS) as i:
                cols = bass.ds(i * C, C)

                def own(name):
                    w_dve(dve, i, name)
                    dve.sem_inc(dve_passed, 1)

                def done(ins):
                    ins.then_inc(chain_dve, 1)

                proj = chain_psum[1][:].rearrange("p (t c) -> p t c", t=CT)
                dve.wait_ge(ctx_loaded, i * 32 + 32)
                w_pe(dve, i, "proj")
                done(dve.tensor_tensor(y1[:], proj, x_res[:], ALU.add))
                own("residual")
                done(dve.tensor_tensor(y1b[:], y1[:], bo_all[:].unsqueeze(1).to_broadcast([P, CT, P]), ALU.add))
                own("bias")
                for t in range(CT):
                    done(dve.bn_stats(stats[:, t], y1b[:, t]))
                own(f"stats{CT - 1}")
                for t in range(CT):
                    done(dve.bn_aggr(moments[:, t], stats[:, t]))
                w_act(dve, i, "std")
                done(dve.reciprocal(rstd[:], std[:]))
                own("rstd")
                for t in range(CT):
                    done(dve.tensor_scalar(x1[:, t], y1b[:, t], moments[:, t, 0:1], rstd[:, t:t + 1],
                                           ALU.subtract, ALU.mult))
                w_act(dve, i, "x_hi")
                done(dve.tensor_tensor(x_lo[:, cols], chain_psum[0][:], x_hi[:, cols].bitcast(F32),
                                       ALU.subtract))
                w_pe(dve, i, "route")
                done(dve.tensor_copy(logits[:], chain_psum[1][:, 0:CT * E].rearrange("p (t e) -> p t e", t=CT)))
                own("logits")
                for t in range(CT):
                    done(dve.max(top8[:, t], logits[:, t]))
                own(f"top{CT - 1}")
                done(dve.tensor_tensor(shifted[:], logits[:], per_tile(top8[:, :, 0], E), ALU.subtract))
                fourth = per_tile(top8[:, :, TOP_K - 1], E)
                done(dve.tensor_tensor(above[:], logits[:], fourth, ALU.is_gt))
                done(dve.tensor_tensor(equal[:], logits[:], fourth, ALU.is_equal))
                own("equal")
                done(dve.reduce_sum(n_above[:], above[:], axis=AX.X))
                own("n_above")
                for t in range(CT):
                    done(dve.tensor_tensor_scan(nth_equal[:, t], equal[:, t], equal[:, t], n_above[:, t:t + 1],
                                                ALU.add, ALU.bypass))
                own(f"nth{CT - 1}")
                done(dve.tensor_single_scalar(place[:], nth_equal[:], float(TOP_K), ALU.is_le))
                own("place")
                done(dve.tensor_tensor(taken[:], place[:], equal[:], ALU.mult))
                own("taken")
                done(dve.tensor_tensor(chosen[:], taken[:], above[:], ALU.add))
                own("chosen")
                for t in range(CT):
                    done(dve.tensor_tensor(before[:, t + 1], before[:, t], chosen[:, t], ALU.add))
                    own(f"before{t}")
                w_act(dve, i, "exp")
                done(dve.reduce_sum(esum[:], expd[:], axis=AX.X))
                own("esum")
                done(dve.reciprocal(rsum[:], esum[:]))
                w_pe(dve, i, "rank")
                own("rsum")
                rank = chain_psum[0][:, 0:CT * E].rearrange("p (t e) -> p t e", t=CT)
                done(dve.scalar_tensor_tensor(out=kept[:], in0=rank, scalar=float(CAPACITY), in1=chosen[:],
                                              op0=ALU.is_le, op1=ALU.mult))
                own("kept")
                done(dve.tensor_tensor(kept_e[:], kept[:], expd[:], ALU.mult))
                own("kept_e")
                done(dve.tensor_tensor(weight[:], kept_e[:], per_tile(rsum[:], E), ALU.mult))
                w_act(dve, i, "gate_hi")
                done(dve.tensor_tensor(gates[E:2 * E, cols], chain_psum[1][0:E, :],
                                       gates[0:E, cols].bitcast(F32), ALU.subtract))
                done(dve.tensor_copy(before[:, 0], before[:, CT]))
                own("carry")
                done_x1 = dve.tensor_copy(x1_all[:, bass.ds(i * CT, CT), :], x1[:])
                done_x1.then_inc(x1_kept, 1)
                dve.wait_ge(x1_kept, i + 1)
                dve.sem_inc(dve_passed, 1)

            with dve.Fori(0, ITERS) as i:
                def own2(name):
                    dve.wait_ge(ln2_dve, i * len(LN2_DVE) + at(LN2_DVE, name))
                    dve.sem_inc(dve_passed, 1)

                for u in range(UNITS):
                    dve.wait_ge(silu_done, i * UNITS + u + 1)
                    if u >= 2:
                        dve.wait_ge(down_done, i * UNITS + u - 1)
                    if u < PAIRS:
                        dve.tensor_tensor(gated[:, u % 2], silu[:, u % 2], up_psum[u % 2][:, 1],
                                          ALU.mult).then_inc(gated_done, 1)
                        dve.wait_ge(gated_done, i * PAIRS + u + 1)
                        dve.sem_inc(dve_passed, 1)
                        dve.wait_ge(gate_ready, i * PAIRS + u + 1)
                        dve.tensor_tensor(hidden[:, u % 2], gated[:, u % 2], gate_psum[:],
                                          ALU.mult).then_inc(hidden_done, 1)
                    else:
                        dve.tensor_tensor(hidden[:, u % 2], silu[:, u % 2], up_psum[u % 2][:, 1],
                                          ALU.mult).then_inc(hidden_done, 1)
                dve.wait_ge(y_turned, i + 1)
                dve.tensor_tensor(z[:], chain_psum[0][:].rearrange("p (t c) -> p t c", t=CT),
                                  x1_all[:, bass.ds(i * CT, CT), :], ALU.add).then_inc(ln2_dve, 1)
                own2("add")
                for t in range(CT):
                    dve.bn_stats(stats2[:, t], z[:, t]).then_inc(ln2_dve, 1)
                own2(f"stats{CT - 1}")
                for t in range(CT):
                    dve.bn_aggr(moments2[:, t], stats2[:, t]).then_inc(ln2_dve, 1)
                dve.wait_ge(ln2_act, i + 1)
                dve.reciprocal(rstd2[:], std2[:]).then_inc(ln2_dve, 1)
                own2("rstd")
                dve.wait_ge(stored, i * 16 + 16)
                dve.sem_inc(dve_passed, 1)
                for t in range(CT):
                    dve.tensor_scalar(result[:, t], z[:, t], moments2[:, t, 0:1], rstd2[:, t:t + 1],
                                      ALU.subtract, ALU.mult).then_inc(ln2_dve, 1)
                own2(f"norm{CT - 1}")

        @block.tensor
        def _(pe):
            pe.wait_ge(small_loaded, 96)
            pe.wait_ge(setup_done, 5)
            with pe.Fori(0, ITERS) as i:
                pe.wait_ge(ctx_loaded, i * 32 + 32)
                for t in range(CT):
                    last = pe.transpose(chain_psum[0][:, t * P:(t + 1) * P], heads[:, t], ident[:])
                last.then_inc(chain_pe, 1)
                w_act(pe, i, "heads_t")
                for t in range(CT):
                    last = pe.matmul(chain_psum[1][:, t * P:(t + 1) * P], heads_t[:, t * P:(t + 1) * P], wo_t[:],
                                     start=True, stop=True)
                last.then_inc(chain_pe, 1)
                w_dve(pe, i, f"norm{CT - 1}")
                for t in range(CT):
                    last = pe.transpose(chain_psum[0][:, t * P:(t + 1) * P], x1[:, t], ident[:])
                last.then_inc(chain_pe, 1)
                w_act(pe, i, "x1_t")
                for t in range(CT):
                    last = pe.matmul(chain_psum[1][:, t * E:(t + 1) * E], x1_t[:, t * P:(t + 1) * P], wg[:],
                                     start=True, stop=True)
                last.then_inc(chain_pe, 1)
                w_dve(pe, i, f"before{CT - 1}")
                pe.matmul(chain_psum[0][:, 0:CT * E], tri[:], chosen[:].rearrange("p t e -> p (t e)"),
                          start=True, stop=False)
                pe.matmul(chain_psum[0][:, 0:CT * E], ones[:], before[:, 0:CT].rearrange("p t e -> p (t e)"),
                          start=False, stop=True).then_inc(chain_pe, 1)
                w_dve(pe, i, "weight")
                for t in range(CT):
                    last = pe.transpose(chain_psum[1][0:E, t * P:(t + 1) * P], weight[:, t], ident[:])
                last.then_inc(chain_pe, 1)
                w_dve(pe, i, "gate_lo")
            pe.wait_ge(w_lo_done, 2)
            pe.wait_ge(w2_loaded, 32)

            with pe.Fori(0, ITERS) as i:
                cols = bass.ds(i * C, C)

                def up(u):
                    if u >= 2:
                        pe.wait_ge(hidden_done, i * UNITS + u)
                    elif u == 0:
                        pe.wait_ge(hidden_done, i * UNITS + 1)
                    for k in range(2):
                        dst = up_psum[u % 2][:, k]
                        hi, lo = w13_hi[:, k, 2 * u:2 * u + 2, :], w13_lo[:, k, 2 * u:2 * u + 2, :]
                        pe.matmul(dst, hi, x_hi[:, cols], start=True, stop=False)
                        pe.matmul(dst, hi, x_lo[:, cols], start=False, stop=False)
                        last = pe.matmul(dst, lo, x_hi[:, cols], start=False, stop=True)
                    last.then_inc(up_ready, 1)
                    if u < PAIRS:
                        if u >= 1:
                            pe.wait_ge(hidden_done, i * UNITS + u + 1)
                        pe.matmul(gate_psum[:], pair_sel[:, u], gates[:, cols], start=True,
                                  stop=True).then_inc(gate_ready, 1)

                up(0)
                for u in range(UNITS):
                    if u + 1 < UNITS:
                        up(u + 1)
                    pe.wait_ge(hidden_done, i * UNITS + u + 2)
                    if u == 0:
                        pe.wait_ge(y_copied, i + 1)
                    pe.matmul(y_psum[:], w2[:, u], hidden[:, u % 2], start=u == 0,
                              stop=u == UNITS - 1).then_inc(down_done, 1)
                pe.wait_ge(y_copied, i + 2)
                for t in range(CT):
                    last = pe.transpose(chain_psum[0][:, t * P:(t + 1) * P], y_t[:, t * P:(t + 1) * P], ident[:])
                last.then_inc(y_turned, 1)


def kernel(**inputs):
    import concourse.bacc as bacc
    from concourse.bass_utils import run_bass_kernel_spmd

    a = {k: np.ascontiguousarray(v) for k, v in inputs.items()}
    x = a["L0_attn_x"]
    tokens = x.reshape(-1, x.shape[-1])
    ident, tri, spread, pairs, onesrow = make_tables(a["L0_ffn_Wg"].shape[1])
    arrays = {
        "x": tokens, "xT": np.ascontiguousarray(tokens.T), "gidx": a["L0_attn_global_indices"],
        "wqkvT": np.stack([np.ascontiguousarray(a[f"L0_attn_W{c}"].T) for c in "qkv"]),
        "bq": a["L0_attn_bq"], "bk": a["L0_attn_bk"], "bv": a["L0_attn_bv"], "bo": a["L0_attn_bo"],
        "WoT": np.ascontiguousarray(a["L0_attn_Wo"].T),
        "Wg": a["L0_ffn_Wg"], "W1": a["L0_ffn_W1"], "W2": a["L0_ffn_W2"], "W3": a["L0_ffn_W3"],
        "Ws1": a["L0_ffn_Ws1"], "Ws2": a["L0_ffn_Ws2"], "Ws3": a["L0_ffn_Ws3"],
        "t_ident": ident, "t_tri": tri, "t_spread": spread, "t_pairs": pairs, "t_onesrow": onesrow,
    }
    nc = bacc.Bacc("TRN2", target_bir_lowering=False, num_devices=1)
    d = {n: nc.dram_tensor(n, v.shape, mybir.dt.from_np(v.dtype), kind="ExternalInput").ap()
         for n, v in arrays.items()}
    out = nc.dram_tensor("out", tokens.shape, F32, kind="ExternalOutput").ap()
    scratch = nc.dram_tensor("scratch", tokens.shape, F32, kind="Internal").ap()
    with ExitStack() as ctx:
        build_attention(nc, ctx, d, scratch)
    with ExitStack() as ctx:
        build_experts(nc, ctx, d, scratch, out)
    r = run_bass_kernel_spmd(nc, [arrays], core_ids=[0])
    return r.results[0]["out"].reshape(x.shape)
```

```python
from contextlib import ExitStack

import numpy as np

import concourse.bass as bass
from concourse import mybir

F32 = mybir.dt.float32
F32R = mybir.dt.float32r
BF16 = mybir.dt.bfloat16
I32 = mybir.dt.int32
ALU = mybir.AluOpType
ACT = mybir.ActivationFunctionType
AX = mybir.AxisListType

P = 128
BS = 64
DH = 8
HG = 4
LANE = 32
MAX_ROW = 24
EPS = 1e-5
TOP_K = 4

S_SLOTS = 14
A_BANKS = 3
B_BANKS = 3
O_BANKS = 2


def make_tables(E):
    ident = np.eye(P, dtype=np.float32)
    tri = np.triu(np.ones((P, P), np.float32))
    spread = np.zeros((P, 4, 4, P), np.float32)
    hi_slots = ((0, 1), (0, 2))
    lo_slots = ((2,), (1,))
    for g in range(4):
        for h in range(HG):
            for d in range(DH):
                src = (g * HG + h) * DH + d
                for qk in range(2):
                    for s in hi_slots[qk]:
                        spread[src, g, 2 * qk, LANE * h + DH * s + d] = 1
                    for s in lo_slots[qk]:
                        spread[src, g, 2 * qk + 1, LANE * h + DH * s + d] = 1
    pairs = np.zeros((P, E // 2, P), np.float32)
    for p in range(E // 2):
        for m in range(P):
            for part in range(2):
                pairs[part * E + 2 * p + m // 64, p, m] = 1
    onesrow = np.zeros((P, 2), np.float32)
    onesrow[MAX_ROW, 0] = 1
    onesrow[MAX_ROW + 1, 1] = 1
    return ident, tri, spread.reshape(P, -1), pairs.reshape(P, -1), onesrow


class Item:

    def __init__(self, ring, kind, arg, bank, use, seq):
        self.ring, self.kind, self.arg, self.bank, self.use, self.seq = ring, kind, arg, bank, use, seq


P_ITEMS = ([("main", j) for j in range(8)] + [("corner", jj) for jj in range(4)]
           + [("col", (half, h)) for half in range(2) for h in range(HG)] + [("row", j) for j in range(8)])
S_ITEMS = [("s_main", j) for j in range(8)] + [("s_corner", jj) for jj in range(4)]
S_ITEMS += [("s_col", j) for j in range(8)] + [("s_row", (h, half)) for h in range(HG) for half in range(2)]
STACKS = [(w, c) for c in range(3) for w in (1, 0)]
COPIES_AFTER = {(1, 0): 4, (0, 0): 5, (1, 1): 9, (0, 1): 10, (1, 2): 14}
COPIES = 14
P_COST = {"main": 10, "corner": 23, "col": 10, "row": 10}
MAX_ITEMS = 20
LOOKAHEAD, EARLY_RATE, S_START, S_SPAN, MAXT0_LAG, MAXT1_AT, VPROJ_AT = 2, 2, 4, 24, 4, 2, (24, 25, 26, 27)
OT_AT = (16, 18, 24, 26)
BURST = 3
JOB_END = {11: (0, 1), 15: (2,), 19: (3,), 27: (4,)}


def plan_attention(groups, batch_steps):
    uses, a_seq, plans = [0] * A_BANKS, 0, []
    for n in range(groups + 1):
        has_s, has_p = n < groups, n >= 1
        fresh = has_s and n % batch_steps == 0
        early = []
        if fresh:
            early += [("proj", x) for x in STACKS]
        if has_s:
            early += [("spread", x) for x in STACKS]
        scores = list(S_ITEMS) if has_s else []
        order = []
        if has_p:
            order += [("P", i) for i in range(LOOKAHEAD)]
            n_scores, given = len(scores), 0
            cost = [P_COST[kind] for kind, _ in P_ITEMS]
            for i in range(0, 28, 2):
                todo = []
                if i >= S_START:
                    share = sum(cost[S_START:i + 2]) / sum(cost[S_START:S_START + S_SPAN])
                    want = min(n_scores, int(share * n_scores + 0.5))
                    todo, given = [("A",) + x for x in scores[given:want]], want
                parts = 3 if len(todo) > BURST else 2
                cuts = [len(todo) * k // parts for k in range(parts + 1)] + [len(todo)]
                for k in range(2):
                    for _ in range(EARLY_RATE):
                        if early:
                            order.append(("A",) + early.pop(0))
                    if i + LOOKAHEAD + k < 28:
                        order.append(("P", i + LOOKAHEAD + k))
                    if k == 1 and i == MAXT1_AT:
                        order.append(("A", "maxT", 1))
                    order += todo[cuts[k]:cuts[k + 1]]
                if has_s and given >= MAX_ITEMS + MAXT0_LAG and ("A", "maxT", 0) not in order:
                    order.append(("A", "maxT", 0))
                for k in (i, i + 1):
                    if k in OT_AT:
                        order.append(("A", "ot", OT_AT.index(k)))
                    if fresh and k in VPROJ_AT:
                        order.append(("A", "vproj", VPROJ_AT.index(k)))
                order.append(("PV", i))
                order += todo[cuts[2]:]
                order.append(("PV", i + 1))
            assert given == n_scores and not early
        else:
            order += [("A",) + x for x in early + scores[:MAX_ITEMS + 1]] + [("A", "maxT", 0)]
            order += [("A",) + x for x in scores[MAX_ITEMS + 1:]]
            order += [("A", "vproj", c) for c in range(4)]
        if has_p:
            order.append(("A", "ot", 4))
        plan = []
        for o in order:
            if o[0] == "A":
                bank = a_seq % A_BANKS
                plan.append(Item("A", o[1], o[2], bank, uses[bank], a_seq))
                uses[bank] += 1
                a_seq += 1
            else:
                seq = 28 * (n - 1) + o[1]
                bank = seq % (28 * batch_steps) % B_BANKS
                plan.append(Item(o[0], *P_ITEMS[o[1]], bank, seq, o[1]))
        plans.append(plan)
    return plans


V_TILES = ((0, 3), (3, 6), (6, 8), (8, 9))
CHUNKS = ((0, 512), (512, 1024), (1024, 1152))


class Step:

    def __init__(self, n, it=None):
        self.n, self.it = n, it

    def value(self, f):
        a = f(self.n)
        if self.it is None:
            return a
        d = f(self.n + 4) - a
        assert f(self.n + 8) - f(self.n + 4) == d, (self.n, a, d)
        return self.it * d + a

    def wait(self, eng, sem, f):
        v = self.value(f)
        if isinstance(v, int) and v <= 0:
            return
        eng.wait_ge(sem, v)


    def gate(self, eng, passed, sem, f):
        self.wait(eng, sem, f)
        if self.it is not None:
            eng.sem_inc(passed, 1)


def run_steps(eng, step_fn, groups):
    step_fn(Step(0))
    with eng.Fori(0, groups // 4 - 1) as it:
        for k in range(4):
            step_fn(Step(1 + k, it))
    for n in range(groups - 3, groups + 1):
        step_fn(Step(n))


def build_attention(nc, ctx, d, scratch):
    x_t, gidx = d["xT"], d["gidx"]
    NTOK = x_t.shape[1]
    N = 1024
    B = NTOK // N
    NT = N // P
    NB = N // BS
    H = 16
    GROUPS = B * H // HG
    NG = N + 2 * BS
    SCALE = 1.0 / float(np.sqrt(np.float32(DH)))
    plans = plan_attention(GROUPS, 4)

    def find(n, kind, arg):
        for x in plans[n]:
            if x.ring == "A" and x.kind == kind and x.arg == arg:
                return x
        raise KeyError((n, kind, arg))

    def wait_free(s, eng, items, gate=None):
        last = {}
        for kind, arg in items:
            x = find(s.n, kind, arg)
            if x.bank not in last or x.use > last[x.bank].use:
                last[x.bank] = x
        for x in last.values():
            count = lambda m, x=x: find(m, x.kind, x.arg).use + 1
            if gate is None:
                s.wait(eng, a_free[x.bank], count)
            else:
                s.gate(eng, gate, a_free[x.bank], count)

    def sb(name, shape, dt=F32):
        return ctx.enter_context(nc.sbuf_tensor(name, shape, dt))

    def sem(name):
        return ctx.enter_context(nc.semaphore(name))

    idx_sb = sb("idx_sb", [1, 2], I32)
    xT = sb("batch_xT", [P, NG])
    wqkv = sb("wqkv", [P, 3, P])
    bqk = sb("bqk", [P, 2])
    bv_all = sb("bv_all", [P, P])
    ident = sb("ident_a", [P, P])
    onesrow = sb("onesrow", [P, 2])
    spread = sb("spread", [P, 4, 4, P], F32R)
    qk_hi = sb("qk_hi", [P, 2, NG], F32R)
    qk_lo = sb("qk_lo", [P, 2, NG], F32R)
    q_stack = sb("q_stack", [P, NG], F32R)
    k_stack = sb("k_stack", [P, 2, NG], F32R)
    q_padded = sb("q_padded", [P, NT, 3, BS], F32R)
    k_padded = sb("k_padded", [P, 2, NT, 3, BS], F32R)
    k_heads = sb("k_heads", [P, HG, NG], F32R)
    q_heads = sb("q_heads", [P, 2, HG, N], F32R)
    q_rows = sb("q_rows", [P, 2, HG, P], F32R)
    v_next = sb("v_next", [P, NT + 1, P])
    v_aug = sb("v_aug", [P, NT + 1, H, DH + 1])
    v_top = sb("v_top", [P, NT, H, DH + 1])
    v_bot = sb("v_bot", [P, NT, H, DH + 1])
    probs = sb("probs", [P, S_SLOTS, 512])
    mx_main = sb("mx_main", [P, HG, NT])
    mx_padded = sb("mx_padded", [P, 2 * HG * NT + HG])
    mx_query = mx_padded[:, 0:2 * HG * NT].rearrange("p (k h t) -> p k h t", k=2, h=HG)
    mx_gathered = sb("mx_gathered", [P, HG])
    mx_corner = sb("mx_corner", [P, HG * NT])
    mx_row = sb("mx_row", [P, HG, 2])
    neg_query = sb("neg_query", [2 * HG * NT, P], F32R)
    neg_gathered = sb("neg_gathered", [HG, P], F32R)
    out_t = sb("out_t", [P, 2 * N + P])
    recip = sb("recip", [P, 5, 16])
    col_tmp = sb("col_tmp", [P, 4, HG, DH])
    heads_out = sb("heads_out", [P, NT, P])
    rows_out = sb("rows_out", [P, P])

    a_psum = [ctx.enter_context(nc.psum_tensor(f"a_psum{i}", [P, 512], F32)) for i in range(A_BANKS)]
    b_psum = [ctx.enter_context(nc.psum_tensor(f"b_psum{i}", [P, 512], F32)) for i in range(B_BANKS)]
    o_psum = [ctx.enter_context(nc.psum_tensor(f"o_psum{i}", [P, 512], F32)) for i in range(O_BANKS)]

    idx_loaded = sem("idx_loaded")
    proj_loaded = sem("proj_loaded")
    spread_loaded = sem("spread_loaded")
    spread_rounded = sem("spread_rounded")
    tables_loaded = sem("att_tables_loaded")
    x_loaded = sem("x_loaded")
    pool_zeroed = sem("pool_zeroed")
    dve_zeroed = sem("dve_zeroed")
    a_ready = [sem(f"a_ready{i}") for i in range(A_BANKS)]
    a_free = [sem(f"a_free{i}") for i in range(A_BANKS)]
    hi_done = sem("hi_done")
    stack_done = sem("stack_done")
    s_operands_done = sem("s_operands_done")
    p_operands_done = sem("p_operands_done")
    max_done = sem("max_done")
    neg_max_done = sem("neg_max_done")
    query_max_moved = sem("query_max_moved")
    gathered_max_moved = sem("gathered_max_moved")
    v_placed = sem("v_placed")
    b_ready = sem("b_ready")
    exp_done = sem("exp_done")
    pv_done = sem("pv_done")
    o_copied = sem("o_copied")
    recip_done = sem("recip_done")
    tmp_done = sem("tmp_done")
    ctx_stored = sem("ctx_stored")
    pool_passed = sem("pool_passed")
    sp_passed = sem("sp_passed")

    def batch_of(n):
        return n // 4

    def v_count(n):
        return (n - 1) // 4 + 1

    def by_block(stack):
        return stack[:, 0:N].bitcast(F32).rearrange("p (t b c) -> p t b c", b=2, c=BS)

    def job(n, j):
        return 5 * (n - 1) + j


    with nc.Block() as block:

        @block.sync
        def _(sp):
            sp.sem_inc(ctx_stored, 16)
            sp.dma_start(idx_sb[:], gidx.rearrange("(o n) -> o n", o=1)).then_inc(idx_loaded, 16)
            sp.dma_start(wqkv[:], d["wqkvT"].rearrange("w i o -> i w o")).then_inc(proj_loaded, 16)
            sp.dma_start(probs[:, 0:4].rearrange("p s c -> p (s c)"), d["t_spread"]).then_inc(spread_loaded, 16)
            sp.dma_start(xT[:, 0:N], x_t[:, 0:N]).then_inc(x_loaded, 16)
            sp.dma_start(bqk[:, 0:1], d["bq"].rearrange("(p o) -> p o", o=1)).then_inc(proj_loaded, 16)
            sp.dma_start(bqk[:, 1:2], d["bk"].rearrange("(p o) -> p o", o=1)).then_inc(proj_loaded, 16)
            sp.wait_ge(idx_loaded, 16)
            first = [sp.snap((sp.value_load(idx_sb[0:1, i:i + 1], min_val=-NB, max_val=NB - 1) + NB) % NB)
                     for i in range(2)]

            def load_gathered(b):
                for i in range(2):
                    sp.dma_start(xT[:, N + i * BS:N + (i + 1) * BS],
                                 x_t[:, bass.ds(b * N + first[i] * BS, BS)]).then_inc(x_loaded, 16)

            load_gathered(0)
            sp.dma_start(onesrow[:], d["t_onesrow"]).then_inc(tables_loaded, 16)
            sp.dma_start(ident[:], d["t_ident"]).then_inc(tables_loaded, 16)
            sp.dma_start(bv_all[:], d["bv"].partition_broadcast(P)).then_inc(tables_loaded, 16)
            sp.wait_ge(pool_zeroed, 9)

            def step(s):
                n = s.n
                if n % 4 == 1 and (s.it is None and n < GROUPS - 3 or s.it is not None):
                    last_v = find(n - 1, "vproj", 3)
                    s.gate(sp, sp_passed, a_ready[last_v.bank], lambda m: find(m - 1, "vproj", 3).use + 1)
                    following = (s.it if s.it is not None else n // 4) + 1
                    sp.dma_start(xT[:, 0:N], x_t[:, bass.ds(following * N, N)]).then_inc(x_loaded, 16)
                    load_gathered(following)
                if n > 0:
                    par = (n - 1) % 2
                    s.wait(sp, neg_max_done, lambda m: 2 * m)
                    sp.dma_start(q_rows[MAX_ROW:MAX_ROW + 1, par, :, :].bitcast(F32).rearrange(
                        "r h k -> r (h k)"), neg_gathered[:].bitcast(F32)).then_inc(gathered_max_moved, 16)
                if n < GROUPS:
                    par = n % 2
                    s.wait(sp, neg_max_done, lambda m: 2 * m + 1)
                    sp.dma_start(q_heads[MAX_ROW:MAX_ROW + 2, par, :, :].bitcast(F32).rearrange(
                        "r h k -> r (h k)"), neg_query[:].bitcast(F32)).then_inc(query_max_moved, 16)
                if n % 4 == 0 and n > 0:
                    b = (s.it if s.it is not None else n // 4 - 1)
                    wait_free(s, sp, [("ot", k) for k in range(5)], gate=sp_passed)
                    sp.dma_start(scratch[bass.ds(b * N, N), :].rearrange("(t p) c -> p t c", p=P),
                                 heads_out[:]).then_inc(ctx_stored, 16)
                    for i in range(2):
                        s.gate(sp, sp_passed, ctx_stored, lambda m, i=i: 16 + 48 * (m // 4 - 1) + 16 * (i + 1))
                        sp.dma_start(scratch[bass.ds(b * N + first[i] * BS, BS), :],
                                     rows_out[i * BS:(i + 1) * BS, :]).then_inc(ctx_stored, 16)

            run_steps(sp, step, GROUPS)
            sp.wait_ge(ctx_stored, 16 + 48 * B)

        @block.gpsimd
        def _(pool):
            pool.memset(q_padded[:, :, 1, :].bitcast(F32), 0.0).then_inc(pool_zeroed, 1)
            pool.memset(v_top[:], 0.0).then_inc(pool_zeroed, 1)
            pool.memset(v_bot[:], 0.0).then_inc(pool_zeroed, 1)
            pool.memset(v_aug[:, :, :, DH:DH + 1], 1.0).then_inc(pool_zeroed, 1)
            pool.wait_ge(pool_zeroed, 4)
            pool.memset(v_top[0:BS, :, :, DH:DH + 1], 1.0).then_inc(pool_zeroed, 1)
            pool.wait_ge(pool_zeroed, 5)
            pool.memset(v_bot[BS:P, :, :, DH:DH + 1], 1.0).then_inc(pool_zeroed, 1)
            pool.wait_ge(pool_zeroed, 6)
            pool.memset(mx_padded[:], 0.0).then_inc(pool_zeroed, 1)
            pool.memset(q_rows[:].bitcast(F32), 0.0).then_inc(pool_zeroed, 1)
            pool.memset(q_heads[:].bitcast(F32), 0.0).then_inc(pool_zeroed, 1)
            pool.wait_ge(pool_zeroed, 9)

            def step(s):
                if s.n >= GROUPS:
                    return
                par = s.n % 2
                s.gate(pool, pool_passed, stack_done, lambda m: 6 * m + 6)
                pool.tensor_copy(k_padded[:, par, :, 0:3:2, :], by_block(k_stack[:, par, :])
                                 ).then_inc(p_operands_done, 1)
                for h in range(HG):
                    rows = slice(LANE * h, LANE * h + 3 * DH)
                    s.gate(pool, pool_passed, p_operands_done, lambda m: 9 * m + 1 + 2 * h)
                    pool.tensor_copy(q_heads[rows, par, h, :], q_stack[rows, 0:N].bitcast(F32)
                                     ).then_inc(p_operands_done, 1)
                    pool.tensor_copy(q_rows[rows, par, h, :], q_stack[rows, N:NG].bitcast(F32)
                                     ).then_inc(p_operands_done, 1)

            run_steps(pool, step, GROUPS)

        @block.scalar
        def _(act):
            act.sem_inc(exp_done, B_BANKS)
            act.sem_inc(o_copied, O_BANKS)
            act.wait_ge(spread_loaded, 16)
            act.copy(spread[:].rearrange("p g k c -> p (g k c)"), probs[:, 0:4].rearrange("p s c -> p (s c)")
                     ).then_inc(spread_rounded, 1)
            act.wait_ge(proj_loaded, 48)

            def a_item(s, x):
                src = a_psum[x.bank]
                if x.kind not in ("proj", "spread", "maxT"):
                    return
                s.wait(act, a_ready[x.bank], lambda m: find(m, x.kind, x.arg).use + 1)
                if x.kind == "proj":
                    w, c = x.arg
                    lo, hi = CHUNKS[c]
                    act.activation(qk_hi[:, w, lo:hi], src[:, 0:hi - lo], ACT.Identity,
                                   bias=bqk[:, w:w + 1]).then_inc(hi_done, 1)
                elif x.kind == "spread":
                    w, c = x.arg
                    par = s.n % 2
                    lo, hi = CHUNKS[c]
                    if w == 0:
                        if c == 0:
                            s.wait(act, p_operands_done, lambda m: 9 * m)
                        act.copy(q_stack[:, lo:hi], src[:, 0:hi - lo]).then_inc(stack_done, 1)
                    else:
                        act.activation(k_stack[:, par, lo:hi], src[:, 0:hi - lo], ACT.Identity,
                                       bias=onesrow[:, c // 2:c // 2 + 1]).then_inc(stack_done, 1)
                else:
                    if x.arg == 0:
                        s.wait(act, query_max_moved, lambda m: 16 * m)
                        act.mul(neg_query[:], src[0:2 * HG * NT, 0:P], -1.0).then_inc(neg_max_done, 1)
                    else:
                        s.wait(act, gathered_max_moved, lambda m: 16 * (m - 1))
                        act.mul(neg_gathered[:], src[0:HG, 0:P], -1.0).then_inc(neg_max_done, 1)

            def step(s):
                for x in plans[s.n]:
                    if s.n == 0 and x.kind == "spread" and x.arg == (1, 0):
                        act.wait_ge(tables_loaded, 48)
                    if x.ring == "A":
                        a_item(s, x)
                    elif x.ring == "P":
                        i = x.seq
                        s.wait(act, b_ready, lambda m: 28 * (m - 1) + i + 1)
                        s.wait(act, pv_done, lambda m: 28 * (m - 1) + i + 1)
                        act.activation(probs[:, x.use % S_SLOTS, :], b_psum[x.bank][:], ACT.Exp,
                                       scale=SCALE).then_inc(exp_done, 1)
                    else:
                        for j in JOB_END.get(x.seq, ()):
                            s.wait(act, pv_done, lambda m: S_SLOTS + 28 * (m - 1) + x.seq + 1)
                            width = 512 if j < 4 else P
                            act.copy(out_t[:, 512 * j:512 * j + width],
                                     o_psum[job(s.n, j) % 2][:, 0:width]).then_inc(o_copied, 1)

            run_steps(act, step, GROUPS)

        @block.vector
        def _(dve):
            dve.memset(k_padded[:, :, :, 1, :].bitcast(F32), 0.0).then_inc(dve_zeroed, 1)
            dve.memset(k_heads[:].bitcast(F32), 0.0).then_inc(dve_zeroed, 1)
            for i in range(O_BANKS):
                last = dve.memset(o_psum[i][:], 0.0)
            last.then_inc(dve_zeroed, 1)
            dve.wait_ge(proj_loaded, 48)

            def maxima_of(s, x):
                src = a_psum[x.bank]
                if x.kind == "s_main":
                    return dve.reduce_max(mx_main[:, :, x.arg], src[:].rearrange("p (h k) -> p h k", h=HG),
                                          axis=AX.X)
                if x.kind == "s_corner":
                    out = mx_corner[:].rearrange("p (h t) -> p t h", t=NT)[:, 2 * x.arg:2 * x.arg + 2, :]
                    return dve.reduce_max(out, src[:].rearrange("p (t h k) -> p t h k", t=2, h=HG), axis=AX.X)
                if x.kind == "s_col":
                    return dve.reduce_max(mx_query[:, 1, :, x.arg], src[:].rearrange("p (h k) -> p h k", h=HG),
                                          axis=AX.X)
                h, half = x.arg
                return dve.reduce_max(mx_row[:, h, half:half + 1], src[:], axis=AX.X)

            def outputs_of(s, x):
                j = x.arg
                tiles = 4 if j < 4 else 1
                src = a_psum[x.bank][:, 0:tiles * P].rearrange("p (t h c) -> p t h c", t=tiles, h=HG)
                rec = recip[:, j, 0:tiles * HG].rearrange("p (t h) -> p t h", t=tiles)
                dve.reciprocal(rec, src[:, :, :, DH]).then_inc(recip_done, 1)
                s.wait(dve, recip_done, lambda m: job(m, j) + 1)
                rec = rec.unsqueeze(3).to_broadcast([P, tiles, HG, DH])
                g = (s.n - 1) % 4
                num = src[:, :, :, 0:DH]
                if j == 4:
                    dst = rows_out[:, LANE * g:LANE * (g + 1)].rearrange("p (h c) -> p h c", h=HG)
                    return dve.tensor_tensor(dst, num[:, 0], rec[:, 0], ALU.mult)
                half = j % 2
                dst = heads_out[:, 4 * half:4 * half + 4, LANE * g:LANE * (g + 1)].rearrange(
                    "p t (h c) -> p t h c", h=HG)
                if j < 2:
                    return dve.tensor_tensor(dst, num, rec, ALU.mult)
                wait_free(s, dve, [("ot", j - 2)] + [("ot", 2)] * (j == 3))
                dve.tensor_tensor(col_tmp[:], num, rec, ALU.mult).then_inc(tmp_done, 1)
                s.wait(dve, tmp_done, lambda m: 2 * (m - 1) + half + 1)
                return dve.tensor_tensor(dst, dst, col_tmp[:], ALU.add)

            def a_item(s, x):
                src = a_psum[x.bank]

                def ready():
                    s.wait(dve, a_ready[x.bank], lambda m: find(m, x.kind, x.arg).use + 1)

                if x.kind == "proj":
                    w, c = x.arg
                    lo, hi = CHUNKS[c]
                    s.wait(dve, hi_done, lambda m: 6 * (m // 4) + STACKS.index((w, c)) + 1)
                    dve.scalar_tensor_tensor(out=qk_lo[:, w, lo:hi], in0=src[:, 0:hi - lo],
                                             scalar=bqk[:, w:w + 1], in1=qk_hi[:, w, lo:hi].bitcast(F32),
                                             op0=ALU.add, op1=ALU.subtract).then_inc(a_free[x.bank], 1)
                elif x.kind == "spread":
                    w, c = x.arg
                    s.wait(dve, stack_done, lambda m: 6 * m + STACKS.index((w, c)) + 1)
                    dve.sem_inc(a_free[x.bank], 1)
                    lo, hi = CHUNKS[c]
                    if w == 1:
                        for h in range(HG):
                            rows = slice(LANE * h, LANE * h + 3 * DH)
                            dve.tensor_copy(k_heads[rows, h, lo:hi], k_stack[rows, s.n % 2, lo:hi].bitcast(F32)
                                            ).then_inc(s_operands_done, 1)
                    elif c < 2:
                        tiles = slice(lo // P, hi // P)
                        dve.tensor_copy(q_padded[:, tiles, 0:3:2, :], by_block(q_stack[:, :])[:, tiles]
                                        ).then_inc(s_operands_done, 1)
                elif x.kind == "maxT":
                    s.wait(dve, neg_max_done, lambda m: 2 * m + 1 - x.arg)
                    dve.sem_inc(a_free[x.bank], 1)
                elif x.kind == "vproj":
                    ready()
                    t0, t1 = V_TILES[x.arg]
                    dve.tensor_tensor(v_next[:, t0:t1, :], src[:, 0:(t1 - t0) * P].rearrange(
                        "p (t c) -> p t c", c=P), bv_all[:].unsqueeze(1).to_broadcast([P, t1 - t0, P]),
                        ALU.add).then_inc(a_free[x.bank], 1)
                elif x.kind == "ot":
                    ready()
                    if s.n % 4 == 1 and x.arg == 0:
                        s.wait(dve, ctx_stored, lambda m: 16 + 48 * (m // 4))
                    outputs_of(s, x).then_inc(a_free[x.bank], 1)
                else:
                    ready()
                    maxima_of(s, x).then_inc(a_free[x.bank], 1)
                    for last_item in (MAX_ITEMS - 1, len(S_ITEMS) - 1):
                        if (x.kind, x.arg) != S_ITEMS[last_item]:
                            continue
                        wait_free(s, dve, S_ITEMS[:last_item + 1])
                        if last_item == MAX_ITEMS - 1:
                            dve.tensor_tensor(mx_query[:, 0], mx_main[:], mx_corner[:].rearrange(
                                "p (h t) -> p h t", h=HG), ALU.max).then_inc(max_done, 1)
                        else:
                            dve.reduce_max(mx_gathered[:], mx_row[:], axis=AX.X).then_inc(max_done, 1)

            def place_v(s):
                heads_of = v_next[:].rearrange("p t (h c) -> p t h c", h=H)
                wait_free(s, dve, [("vproj", k) for k in range(4)])
                s.wait(dve, pv_done, lambda m: S_SLOTS + 28 * m)
                dve.tensor_copy(v_aug[:, :, :, 0:DH], heads_of).then_inc(v_placed, 1)
                dve.tensor_copy(v_top[0:BS, :, :, 0:DH], heads_of[0:BS, 0:NT]).then_inc(v_placed, 1)
                dve.tensor_copy(v_bot[BS:P, :, :, 0:DH], heads_of[BS:P, 0:NT]).then_inc(v_placed, 1)

            def step(s):
                for x in plans[s.n]:
                    if s.n == 0 and x.kind == "spread" and x.arg == (1, 0):
                        dve.wait_ge(tables_loaded, 48)
                        dve.wait_ge(dve_zeroed, 3)
                        dve.wait_ge(pool_zeroed, 7)
                    if x.ring == "A":
                        a_item(s, x)
                if s.n % 4 == 0 and s.n < GROUPS:
                    place_v(s)

            run_steps(dve, step, GROUPS)

        @block.tensor
        def _(pe):
            pe.sem_inc(pv_done, S_SLOTS)
            pe.wait_ge(proj_loaded, 48)

            def local_scores(out_main, out_corner, stack, padded, heads, kind, j):
                if kind == "main":
                    return pe.matmul(out_main, stack[:, j * P:(j + 1) * P], heads[:, :, j * P:(j + 1) * P],
                                     start=True, stop=True)
                before, after = (2 * j - 1) % NB, (2 * j + 2) % NB
                pe.matmul(out_corner, padded[:, j, 0:2, :], heads[:, :, before * BS:(before + 1) * BS],
                          start=True, stop=False)
                return pe.matmul(out_corner, padded[:, j, 1:3, :], heads[:, :, after * BS:(after + 1) * BS],
                                 start=False, stop=True)

            def four(bank, n=P):
                return bank[:].rearrange("p (h k) -> p h k", h=HG)

            def pair(bank, i):
                return bank[:, i * 256:(i + 1) * 256].rearrange("p (h k) -> p h k", h=HG)

            def a_item(s, x):
                out = a_psum[x.bank]
                if x.kind == "proj" and x.arg == STACKS[0]:
                    s.wait(pe, x_loaded, lambda m: 48 * (m // 4 + 1))
                if x.kind == "spread" and x.arg == (1, 0) and s.n % 4 == 0:
                    wait_free(s, pe, [("proj", (w, c)) for w in range(2) for c in range(3)])
                for first, last_stack, copies in ((("s_main", 0), (0, 0), (0, 0)),
                                                  (("s_main", 4), (0, 1), (0, 1)),
                                                  (("s_col", 0), (0, 2), (1, 2))):
                    if (x.kind, x.arg) == first:
                        s.wait(pe, stack_done, lambda m: 6 * m + STACKS.index(last_stack) + 1)
                        s.wait(pe, s_operands_done, lambda m: COPIES * m + COPIES_AFTER[copies])
                if x.kind == "maxT":
                    s.wait(pe, max_done, lambda m: 2 * m + 1 - x.arg)
                if x.kind == "ot":
                    s.wait(pe, o_copied, lambda m: O_BANKS + job(m, x.arg) + 1)
                s.wait(pe, a_free[x.bank], lambda m: find(m, x.kind, x.arg).use)
                if x.kind == "proj":
                    w, c = x.arg
                    lo, hi = CHUNKS[c]
                    last = pe.matmul(out[:, 0:hi - lo], wqkv[:, w, :], xT[:, lo:hi], start=True, stop=True)
                elif x.kind == "vproj":
                    t0, t1 = V_TILES[x.arg]
                    for t in range(t0, t1):
                        last = pe.matmul(out[:, (t - t0) * P:(t - t0 + 1) * P], xT[:, t * P:(t + 1) * P],
                                         wqkv[:, 2, :], start=True, stop=True)
                elif x.kind == "spread":
                    w, c = x.arg
                    g = s.n % 4
                    lo, hi = CHUNKS[c]
                    pe.matmul(out[:, 0:hi - lo], spread[:, g, 2 * w, :], qk_hi[:, w, lo:hi], start=True, stop=False)
                    last = pe.matmul(out[:, 0:hi - lo], spread[:, g, 2 * w + 1, :], qk_lo[:, w, lo:hi],
                                     start=False, stop=True)
                elif x.kind == "s_main":
                    last = local_scores(four(out), None, q_stack, q_padded, k_heads, "main", x.arg)
                elif x.kind == "s_corner":
                    for i in range(2):
                        last = local_scores(None, pair(out, i), q_stack, q_padded, k_heads, "corner", 2 * x.arg + i)
                elif x.kind == "s_col":
                    last = pe.matmul(four(out), q_stack[:, x.arg * P:(x.arg + 1) * P], k_heads[:, :, N:NG],
                                     start=True, stop=True)
                elif x.kind == "s_row":
                    h, half = x.arg
                    last = pe.matmul(out[:], q_stack[:, N:NG], k_heads[:, h, half * 512:(half + 1) * 512],
                                     start=True, stop=True)
                elif x.kind == "maxT":
                    maxima = (mx_padded[:], mx_gathered[:])[x.arg]
                    last = pe.transpose(out[0:maxima.shape[1], 0:P], maxima, ident[:])
                else:
                    j = x.arg
                    for t in range(4 if j < 4 else 1):
                        last = pe.transpose(out[:, t * P:(t + 1) * P],
                                            out_t[:, 512 * j + t * P:512 * j + (t + 1) * P], ident[:])
                last.then_inc(a_ready[x.bank], 1)

            def scores_t(s, x):
                i = x.seq
                par = (s.n - 1) % 2
                if i == 0:
                    s.wait(pe, p_operands_done, lambda m: 9 * m)
                    s.wait(pe, query_max_moved, lambda m: 16 * m)
                if i == MAX_ITEMS:
                    s.wait(pe, gathered_max_moved, lambda m: 16 * m)
                since = B_BANKS if i == 0 and s.n % 4 == 1 else 1
                s.wait(pe, exp_done, lambda m: 28 * (m - 1) + i + since)
                out = b_psum[x.bank]
                ks, kp, qh, qr = k_stack[:, par], k_padded[:, par], q_heads[:, par], q_rows[:, par]
                if x.kind == "main":
                    last = local_scores(four(out), None, ks, kp, qh, "main", x.arg)
                elif x.kind == "corner":
                    for k in range(2):
                        last = local_scores(None, pair(out, k), ks, kp, qh, "corner", 2 * x.arg + k)
                elif x.kind == "col":
                    half, h = x.arg
                    last = pe.matmul(out[:], ks[:, N:NG], qh[:, h, half * 512:(half + 1) * 512],
                                     start=True, stop=True)
                else:
                    last = pe.matmul(four(out), ks[:, x.arg * P:(x.arg + 1) * P], qr[:, :, :], start=True, stop=True)
                last.then_inc(b_ready, 1)

            def weighted_v(s, x):
                i = x.seq
                g = (s.n - 1) % 4
                if i == 0:
                    s.wait(pe, v_placed, lambda m: 3 * v_count(m))
                for j, first_item in ((0, 0), (1, 4), (2, 12), (3, 16), (4, 20)):
                    if i == first_item:
                        s.wait(pe, o_copied, lambda m: job(m, j) + 1)
                s.wait(pe, exp_done, lambda m: B_BANKS + 28 * (m - 1) + i + 1)
                probs_i = probs[:, x.use % S_SLOTS, :]
                for h in range(HG):
                    hh = HG * g + h
                    rows = slice(LANE * h, LANE * h + DH + 1)
                    if x.kind == "main":
                        j = x.arg
                        last = pe.matmul(o_psum[job(s.n, j // 4) % 2][rows, (j % 4) * P:(j % 4 + 1) * P],
                                         v_aug[:, j, hh, :], probs_i[:, h * P:(h + 1) * P],
                                         start=j % 4 == 0, stop=False)
                    elif x.kind == "corner":
                        for k in range(2):
                            j = 2 * x.arg + k
                            for v, blk in ((v_top, (2 * j - 1) % NB), (v_bot, (2 * j + 2) % NB)):
                                half, c = blk // 8, blk % 8
                                last = pe.matmul(o_psum[job(s.n, half) % 2][rows, c * BS:(c + 1) * BS],
                                                 v[:, j, hh, :], probs_i[:, k * 256 + h * BS:k * 256 + (h + 1) * BS],
                                                 start=False, stop=j == NT - 1)
                    elif x.kind == "col":
                        half, hx = x.arg
                        if hx != h:
                            continue
                        last = pe.matmul(o_psum[job(s.n, 2 + half) % 2][rows, :], v_aug[:, NT, hh, :], probs_i,
                                         start=True, stop=True)
                    else:
                        j = x.arg
                        last = pe.matmul(o_psum[job(s.n, 4) % 2][rows, 0:P], v_aug[:, j, hh, :],
                                         probs_i[:, h * P:(h + 1) * P], start=j == 0, stop=j == NT - 1)
                last.then_inc(pv_done, 1)

            def step(s):
                for x in plans[s.n]:
                    if s.n == 0 and x.kind == "spread" and x.arg == (1, 0):
                        pe.wait_ge(spread_rounded, 1)
                        pe.wait_ge(tables_loaded, 48)
                        pe.wait_ge(dve_zeroed, 3)
                        pe.wait_ge(pool_zeroed, 7)
                    if x.ring == "A":
                        a_item(s, x)
                    elif x.ring == "P":
                        scores_t(s, x)
                    else:
                        weighted_v(s, x)

            run_steps(pe, step, GROUPS)


class Chunk:

    def __init__(self, k, it=None):
        self.k, self.it = k, it
        self.parity = k % 2

    def plus(self, more):
        return Chunk(self.k + more, self.it)

    def times(self, per_chunk, more=0):
        if self.it is None:
            return self.k * per_chunk + more
        return self.it * (2 * per_chunk) + (self.k * per_chunk + more)

    def wait(self, eng, sem, per_chunk, more):
        v = self.times(per_chunk, more)
        if isinstance(v, int) and v <= 0:
            return
        eng.wait_ge(sem, v)

    def gate(self, eng, passed, sem, per_chunk, more):
        self.wait(eng, sem, per_chunk, more)
        if self.it is not None:
            eng.sem_inc(passed, 1)


def run_chunks(eng, body, chunks):
    body(Chunk(0))
    with eng.Fori(0, (chunks - 2) // 2) as it:
        body(Chunk(1, it))
        body(Chunk(2, it))
    body(Chunk(chunks - 1))


def build_experts(nc, ctx, d, scratch, out):
    NTOK = scratch.shape[0]
    C = 512
    CT = C // P
    CHUNKS_B = NTOK // C
    E, _, HE = d["W1"].shape
    PAIRS = E // 2
    UNITS = PAIRS + 1
    CAPACITY = 4 * NTOK * TOP_K // E

    def sb(name, shape, dt=F32):
        return ctx.enter_context(nc.sbuf_tensor(name, shape, dt))

    def sem(name):
        return ctx.enter_context(nc.semaphore(name))

    ident = sb("ident_b", [P, P])
    tri_f = sb("tri_f", [P, P])
    tri = sb("tri", [P, P], BF16)
    ones = sb("ones", [P, P], BF16)
    wo_t = sb("wo_t", [P, P])
    bo_all = sb("bo_all", [P, P])
    wg = sb("wg", [P, E])
    eps = sb("eps", [P, 1])
    w13_raw = sb("w13_raw", [P, 2, E + 2, HE])
    w13_hi = sb("w13_hi", [P, 2, E + 2, HE], F32R)
    w13_lo = sb("w13_lo", [P, 2, E + 2, HE], F32R)
    w2 = sb("w2", [P, UNITS, P])
    pair_sel_f = sb("pair_sel_f", [P, PAIRS * P])
    pair_sel = sb("pair_sel", [P, PAIRS * P], F32R)
    heads = sb("heads", [P, CT, P])
    x_res = sb("x_res", [P, CT, P])
    x_hi = sb("x_hi", [P, 2, C], F32R)
    x_lo = sb("x_lo", [P, 2, C], F32R)
    gates = sb("gates", [P, 2, C], F32R)
    x1 = sb("x1", [P, 2, CT, P])
    heads_t = sb("heads_t", [P, C])
    x_bias = sb("x_bias", [P, CT, P])
    y1 = sb("y1", [P, CT, P])
    stats = sb("stats", [P, CT, 6])
    moments = sb("moments", [P, CT, 2])
    std = sb("std", [P, CT])
    rstd = sb("rstd", [P, CT])
    x1_t = sb("x1_t", [P, C])
    logits = sb("logits", [P, CT, E])
    top8 = sb("top8", [P, CT, 8])
    shifted = sb("shifted", [P, CT, E])
    expd = sb("expd", [P, CT, E])
    esum = sb("esum", [P, CT])
    rsum = sb("rsum", [P, CT])
    above = sb("above", [P, CT, E])
    equal = sb("equal", [P, CT, E])
    n_above = sb("n_above", [P, CT])
    nth_equal = sb("nth_equal", [P, CT, E])
    taken = sb("taken", [P, CT, E])
    chosen = sb("chosen", [P, CT, E], BF16)
    before = sb("before", [P, CT + 1, E], BF16)
    kept = sb("kept", [P, CT, E])
    kept_e = sb("kept_e", [P, CT, E])
    weight = sb("weight", [P, CT, E])
    silu = sb("silu", [P, 2, C])
    gated = sb("gated", [P, 2, C])
    hidden = sb("hidden", [P, 2, C])
    y_t = sb("y_t", [P, C])
    z = sb("z", [P, CT, P])
    stats2 = sb("stats2", [P, CT, 6])
    moments2 = sb("moments2", [P, CT, 2])
    std2 = sb("std2", [P, CT])
    rstd2 = sb("rstd2", [P, CT])
    result = sb("result", [P, CT, P])

    chain_psum = ctx.enter_context(nc.psum_tensor("chain_psum", [P, 512], F32))
    up_psum = [ctx.enter_context(nc.psum_tensor(f"up_psum{i}", [P, 2, 512], F32)) for i in range(2)]
    gate_psum = [ctx.enter_context(nc.psum_tensor(f"gate_psum{i}", [P, 512], F32)) for i in range(2)]
    y_psum = ctx.enter_context(nc.psum_tensor("y_psum", [P, 512], F32))

    small_loaded = sem("small_loaded")
    tables_loaded = sem("tables_loaded")
    w13_loaded = [sem(f"w{n}_loaded") for n in (1, 3)]
    w2_loaded = sem("w2_loaded")
    w_hi_done = sem("w_hi_done")
    w_lo_done = sem("w_lo_done")
    pool_setup = sem("pool_setup")
    tri_cast = sem("tri_cast")
    pairs_loaded = sem("pairs_loaded")
    pairs_rounded = sem("pairs_rounded")
    ctx_loaded = sem("ctx_loaded")
    x_bias_done = sem("x_bias_done")
    chain_pe = sem("chain_pe")
    chain_act = sem("chain_act")
    chain_dve = sem("chain_dve")
    up_ready = sem("up_ready")
    gate_ready = sem("gate_ready")
    silu_done = sem("silu_done")
    gated_done = sem("gated_done")
    hidden_done = sem("hidden_done")
    down_done = sem("down_done")
    y_copied = sem("y_copied")
    y_turned = sem("y_turned")
    ln2_dve = sem("ln2_dve")
    ln2_act = sem("ln2_act")
    stored = sem("stored")
    dve_passed = sem("dve_passed")
    sp_passed = sem("sp2_passed")
    pool_passed = sem("pool2_passed")

    DVE_STEPS = (["residual"] + [f"stats{t}" for t in range(CT)] + [f"aggr{t}" for t in range(CT)]
                 + ["rstd"] + [f"norm{t}" for t in range(CT)] + ["x_lo", "logits"]
                 + [f"top{t}" for t in range(CT)] + ["shift", "above", "equal", "n_above"]
                 + [f"nth{t}" for t in range(CT)] + ["taken", "chosen"]
                 + [f"before{t}" for t in range(CT)] + ["esum", "rsum", "kept", "kept_e", "weight",
                                                        "gate_lo", "carry"])
    ACT_STEPS = ["heads_t", "std", "x1_t", "x_hi", "exp", "gate_hi"]
    PE_STEPS = ["heads_t", "proj", "x1_t", "route", "rank", "gates"]
    LN2_DVE = (["add"] + [f"stats{t}" for t in range(CT)] + [f"aggr{t}" for t in range(CT)] + ["rstd"]
               + [f"norm{t}" for t in range(CT)])
    STAGES = (("ln2_copy", 1), ("ln2_turn", 0), ("ln2_add", 1), ("heads_t", 1), ("ln2_stats", 2), ("heads_copy", 3), ("proj", 2),
              ("residual", 3), ("stats", 4), ("std", 6), ("ln2_std", 6), ("norm", 6), ("x1_turn", 6),
              ("x1_copy", 8), ("x_lo", 7), ("route", 8), ("logits", 9), ("compare", 9), ("exp", 12),
              ("choose", 10), ("count", 11), ("rank", 11), ("weight", 12), ("gates", 12), ("gate_hi", 14),
              ("gate_lo", 13), ("ln2_norm", 15))

    def at(steps, name):
        return steps.index(name) + 1

    def w_dve(eng, c, name):
        c.wait(eng, chain_dve, len(DVE_STEPS), at(DVE_STEPS, name))

    def w_act(eng, c, name):
        c.wait(eng, chain_act, len(ACT_STEPS), at(ACT_STEPS, name))

    def w_pe(eng, c, name):
        c.wait(eng, chain_pe, len(PE_STEPS), at(PE_STEPS, name))

    def tiles_of(dram, c):
        return dram[bass.ds(c.times(C), C), :].rearrange("(t p) c -> p t c", p=P)

    def run_stages(c, u, chain, ln2):
        for stage, unit in STAGES:
            if unit != u:
                continue
            if stage.startswith("ln2"):
                if not (c.it is None and c.k == 0):
                    ln2(c.plus(-1), stage)
            elif not (c.it is None and c.k == CHUNKS_B - 1):
                chain(c.plus(1), stage)

    def unit_after(c, u, more):
        u += more
        while u >= UNITS:
            u, c = u - UNITS, c.plus(1)
        while u < 0:
            u, c = u + UNITS, c.plus(-1)
        if c.it is None and not 0 <= c.k < CHUNKS_B:
            return None
        return c, u

    def slot(c, u):
        return (c.k * UNITS + u) % 2

    with nc.Block() as block:

        @block.sync
        def _(sp):
            def load_chunk(c):
                sp.dma_start(heads[:], tiles_of(scratch, c)).then_inc(ctx_loaded, 16)
                sp.dma_start(x_res[:], tiles_of(d["x"], c)).then_inc(ctx_loaded, 16)

            load_chunk(Chunk(0))
            for dst, src in ((ident[:], d["t_ident"]), (bo_all[:], d["bo"].partition_broadcast(P)),
                             (wo_t[:], d["WoT"]), (wg[:], d["Wg"])):
                sp.dma_start(dst, src).then_inc(small_loaded, 16)
            for k, (w, ws) in enumerate((("W1", "Ws1"), ("W3", "Ws3"))):
                sp.dma_start(w13_raw[:, k, 0:E, :], d[w].rearrange("e i h -> i e h")).then_inc(w13_loaded[k], 16)
                sp.dma_start(w13_raw[:, k, E:E + 2, :], d[ws].rearrange("i (e h) -> i e h", e=2)
                             ).then_inc(w13_loaded[k], 16)
            sp.dma_start(tri_f[:], d["t_tri"]).then_inc(tables_loaded, 16)
            sp.dma_start(pair_sel_f[:], d["t_pairs"]).then_inc(pairs_loaded, 16)
            sp.dma_start(w2[:, 0:PAIRS, :], d["W2"].rearrange("(p e) h o -> (e h) p o", e=2)
                         ).then_inc(w2_loaded, 16)
            sp.dma_start(w2[:, PAIRS, :], d["Ws2"]).then_inc(w2_loaded, 16)

            def next_chunk(c):
                before_c = c.plus(-1)
                before_c.gate(sp, sp_passed, chain_pe, len(PE_STEPS), at(PE_STEPS, "heads_t"))
                before_c.gate(sp, sp_passed, x_bias_done, 1, 1)
                load_chunk(c)

            def store(c):
                c.gate(sp, sp_passed, ln2_dve, len(LN2_DVE), len(LN2_DVE))
                sp.dma_start(tiles_of(out, c), result[:]).then_inc(stored, 16)

            next_chunk(Chunk(1))

            def body(c):
                if not (c.it is None and c.k == CHUNKS_B - 1) and not (c.it is None and c.k == 0):
                    next_chunk(c.plus(1))
                if not (c.it is None and c.k == 0):
                    store(c.plus(-1))

            run_chunks(sp, body, CHUNKS_B)
            store(Chunk(CHUNKS_B - 1))
            sp.wait_ge(stored, 16 * CHUNKS_B)

        @block.gpsimd
        def _(pool):
            pool.memset(ones[:], 1.0).then_inc(pool_setup, 1)
            pool.memset(eps[:], EPS).then_inc(pool_setup, 1)
            pool.memset(before[:], 0.0).then_inc(pool_setup, 1)
            pool.memset(gates[:].bitcast(F32), 0.0).then_inc(pool_setup, 1)
            pool.wait_ge(small_loaded, 64)

            def add_bias(c):
                c.gate(pool, pool_passed, ctx_loaded, 32, 32)
                c.gate(pool, pool_passed, chain_dve, len(DVE_STEPS), at(DVE_STEPS, "residual") - len(DVE_STEPS))
                pool.tensor_tensor(x_bias[:], x_res[:], bo_all[:].unsqueeze(1).to_broadcast([P, CT, P]),
                                   ALU.add).then_inc(x_bias_done, 1)

            add_bias(Chunk(0))
            for k in range(2):
                if k == 1:
                    pool.wait_ge(tables_loaded, 16)
                    pool.tensor_copy(tri[:], tri_f[:]).then_inc(tri_cast, 1)
                pool.wait_ge(w_hi_done, k + 1)
                pool.tensor_tensor(w13_lo[:, k], w13_raw[:, k], w13_hi[:, k].bitcast(F32),
                                   ALU.subtract).then_inc(w_lo_done, 1)

            def body(c):
                if not (c.it is None and c.k == CHUNKS_B - 1):
                    add_bias(c.plus(1))

            run_chunks(pool, body, CHUNKS_B)

        @block.scalar
        def _(act):
            act.wait_ge(pool_setup, 4)

            def chain(c, stage):
                par = c.parity
                if stage == "heads_copy":
                    w_pe(act, c, "heads_t")
                    act.copy(heads_t[:], chain_psum[:]).then_inc(chain_act, 1)
                elif stage == "std":
                    w_dve(act, c, f"aggr{CT - 1}")
                    act.activation(std[:], moments[:, :, 1], ACT.Sqrt, bias=eps[:]).then_inc(chain_act, 1)
                elif stage == "x1_copy":
                    w_pe(act, c, "x1_t")
                    act.copy(x1_t[:], chain_psum[:]).then_inc(chain_act, 1)
                    act.copy(x_hi[:, par], chain_psum[:]).then_inc(chain_act, 1)
                elif stage == "exp":
                    w_dve(act, c, "shift")
                    act.activation(expd[:], shifted[:], ACT.Exp).then_inc(chain_act, 1)
                elif stage == "gate_hi":
                    w_pe(act, c, "gates")
                    act.copy(gates[0:E, par], chain_psum[0:E, :]).then_inc(chain_act, 1)

            def ln2(c, stage):
                if stage == "ln2_copy":
                    c.wait(act, down_done, UNITS, UNITS)
                    c.wait(act, y_turned, 1, 0)
                    act.copy(y_t[:], y_psum[:]).then_inc(y_copied, 1)
                elif stage == "ln2_std":
                    c.wait(act, ln2_dve, len(LN2_DVE), at(LN2_DVE, f"aggr{CT - 1}"))
                    act.activation(std2[:], moments2[:, :, 1], ACT.Sqrt, bias=eps[:]).then_inc(ln2_act, 1)

            for stage, _ in STAGES:
                chain(Chunk(0), stage)
                if stage in ("std", "x1_copy"):
                    k = ("std", "x1_copy").index(stage)
                    act.wait_ge(w13_loaded[k], 32)
                    act.copy(w13_hi[:, k], w13_raw[:, k]).then_inc(w_hi_done, 1)

            def body(c):
                for u in range(UNITS):
                    c.wait(act, up_ready, UNITS, u + 1)
                    s = slot(c, u)
                    act.activation(silu[:, s], up_psum[s][:, 0], ACT.Silu).then_inc(silu_done, 1)
                    run_stages(c, u, chain, ln2)

            run_chunks(act, body, CHUNKS_B)
            ln2(Chunk(CHUNKS_B - 1), "ln2_copy")
            ln2(Chunk(CHUNKS_B - 1), "ln2_std")

        @block.vector
        def _(dve):
            dve.wait_ge(pool_setup, 4)

            def own(c, name):
                w_dve(dve, c, name)
                if c.it is not None:
                    dve.sem_inc(dve_passed, 1)

            def own2(c, name):
                c.gate(dve, dve_passed, ln2_dve, len(LN2_DVE), at(LN2_DVE, name))

            def done(ins):
                ins.then_inc(chain_dve, 1)

            def per_tile(x, width):
                return x.unsqueeze(2).to_broadcast([P, CT, width])

            def chain(c, stage):
                par = c.parity
                if stage == "residual":
                    c.gate(dve, dve_passed, x_bias_done, 1, 1)
                    w_pe(dve, c, "proj")
                    done(dve.tensor_tensor(y1[:], chain_psum[:].rearrange("p (t c) -> p t c", t=CT), x_bias[:],
                                           ALU.add))
                elif stage == "stats":
                    own(c, "residual")
                    for t in range(CT):
                        done(dve.bn_stats(stats[:, t], y1[:, t]))
                    own(c, f"stats{CT - 1}")
                    for t in range(CT):
                        done(dve.bn_aggr(moments[:, t], stats[:, t]))
                elif stage == "norm":
                    w_act(dve, c, "std")
                    done(dve.reciprocal(rstd[:], std[:]))
                    own(c, "rstd")
                    for t in range(CT):
                        done(dve.tensor_scalar(x1[:, par, t], y1[:, t], moments[:, t, 0:1], rstd[:, t:t + 1],
                                               ALU.subtract, ALU.mult))
                elif stage == "x_lo":
                    w_act(dve, c, "x_hi")
                    done(dve.tensor_tensor(x_lo[:, par], chain_psum[:], x_hi[:, par].bitcast(F32),
                                           ALU.subtract))
                elif stage == "logits":
                    w_pe(dve, c, "route")
                    done(dve.tensor_copy(logits[:], chain_psum[:, 0:CT * E].rearrange("p (t e) -> p t e", t=CT)))
                    own(c, "logits")
                    for t in range(CT):
                        done(dve.max(top8[:, t], logits[:, t]))
                elif stage == "compare":
                    own(c, f"top{CT - 1}")
                    done(dve.tensor_tensor(shifted[:], logits[:], per_tile(top8[:, :, 0], E), ALU.subtract))
                    fourth = per_tile(top8[:, :, TOP_K - 1], E)
                    done(dve.tensor_tensor(above[:], logits[:], fourth, ALU.is_gt))
                    done(dve.tensor_tensor(equal[:], logits[:], fourth, ALU.is_equal))
                    own(c, "equal")
                    done(dve.reduce_sum(n_above[:], above[:], axis=AX.X))
                elif stage == "choose":
                    own(c, "n_above")
                    for t in range(CT):
                        done(dve.tensor_tensor_scan(nth_equal[:, t], equal[:, t], equal[:, t], n_above[:, t:t + 1],
                                                    ALU.add, ALU.bypass))
                    own(c, f"nth{CT - 1}")
                    done(dve.scalar_tensor_tensor(out=taken[:], in0=nth_equal[:], scalar=float(TOP_K),
                                                  in1=equal[:], op0=ALU.is_le, op1=ALU.mult))
                    own(c, "taken")
                    done(dve.tensor_tensor(chosen[:], taken[:], above[:], ALU.add))
                elif stage == "count":
                    own(c, "chosen")
                    for t in range(CT):
                        done(dve.tensor_tensor(before[:, t + 1], before[:, t], chosen[:, t], ALU.add))
                        own(c, f"before{t}")
                elif stage == "weight":
                    w_act(dve, c, "exp")
                    done(dve.reduce_sum(esum[:], expd[:], axis=AX.X))
                    own(c, "esum")
                    done(dve.reciprocal(rsum[:], esum[:]))
                    w_pe(dve, c, "rank")
                    own(c, "rsum")
                    rank = chain_psum[:, 0:CT * E].rearrange("p (t e) -> p t e", t=CT)
                    done(dve.scalar_tensor_tensor(out=kept[:], in0=rank, scalar=float(CAPACITY), in1=chosen[:],
                                                  op0=ALU.is_le, op1=ALU.mult))
                    own(c, "kept")
                    done(dve.tensor_tensor(kept_e[:], kept[:], expd[:], ALU.mult))
                    own(c, "kept_e")
                    done(dve.tensor_tensor(weight[:], kept_e[:], per_tile(rsum[:], E), ALU.mult))
                elif stage == "gate_lo":
                    w_act(dve, c, "gate_hi")
                    done(dve.tensor_tensor(gates[E:2 * E, par], chain_psum[0:E, :],
                                           gates[0:E, par].bitcast(F32), ALU.subtract))
                    done(dve.tensor_copy(before[:, 0], before[:, CT]))
                    own(c, "carry")

            def ln2(c, stage):
                if stage == "ln2_add":
                    c.wait(dve, y_turned, 1, 1)
                    dve.tensor_tensor(z[:], chain_psum[:].rearrange("p (t c) -> p t c", t=CT),
                                      x1[:, c.parity], ALU.add).then_inc(ln2_dve, 1)
                elif stage == "ln2_stats":
                    own2(c, "add")
                    for t in range(CT):
                        dve.bn_stats(stats2[:, t], z[:, t]).then_inc(ln2_dve, 1)
                    own2(c, f"stats{CT - 1}")
                    for t in range(CT):
                        dve.bn_aggr(moments2[:, t], stats2[:, t]).then_inc(ln2_dve, 1)
                elif stage == "ln2_norm":
                    c.wait(dve, ln2_act, 1, 1)
                    dve.reciprocal(rstd2[:], std2[:]).then_inc(ln2_dve, 1)
                    c.gate(dve, dve_passed, stored, 16, 0)
                    own2(c, "rstd")
                    for t in range(CT):
                        dve.tensor_scalar(result[:, t], z[:, t], moments2[:, t, 0:1], rstd2[:, t:t + 1],
                                          ALU.subtract, ALU.mult).then_inc(ln2_dve, 1)

            for stage, _ in STAGES:
                chain(Chunk(0), stage)
                if stage == "x_lo":
                    dve.wait_ge(pairs_loaded, 16)
                    dve.tensor_copy(pair_sel[:], pair_sel_f[:]).then_inc(pairs_rounded, 1)

            def body(c):
                for u in range(UNITS):
                    s = slot(c, u)
                    c.wait(dve, silu_done, UNITS, u + 1)
                    if u < PAIRS:
                        c.gate(dve, dve_passed, hidden_done, UNITS, u - 1)
                        dve.tensor_tensor(gated[:, s], silu[:, s], up_psum[s][:, 1],
                                          ALU.mult).then_inc(gated_done, 1)
                        c.gate(dve, dve_passed, gated_done, PAIRS, u + 1)
                        c.gate(dve, dve_passed, gate_ready, PAIRS, u + 1)
                    c.wait(dve, down_done, UNITS, u - 1)
                    if u < PAIRS:
                        dve.tensor_tensor(hidden[:, s], gated[:, s], gate_psum[s][:],
                                          ALU.mult).then_inc(hidden_done, 1)
                    else:
                        dve.tensor_tensor(hidden[:, s], silu[:, s], up_psum[s][:, 1],
                                          ALU.mult).then_inc(hidden_done, 1)
                    run_stages(c, u, chain, ln2)

            run_chunks(dve, body, CHUNKS_B)
            for stage in ("ln2_add", "ln2_stats", "ln2_norm"):
                ln2(Chunk(CHUNKS_B - 1), stage)

        @block.tensor
        def _(pe):
            pe.wait_ge(small_loaded, 64)

            def chain(c, stage):
                if stage == "heads_t":
                    c.wait(pe, ctx_loaded, 32, 32)
                    c.plus(-2).wait(pe, ln2_dve, len(LN2_DVE), at(LN2_DVE, "add"))
                    c.plus(-1).wait(pe, chain_dve, len(DVE_STEPS), at(DVE_STEPS, "gate_lo"))
                    for t in range(CT):
                        last = pe.transpose(chain_psum[:, t * P:(t + 1) * P], heads[:, t], ident[:])
                    last.then_inc(chain_pe, 1)
                elif stage == "proj":
                    w_act(pe, c, "heads_t")
                    for t in range(CT):
                        last = pe.matmul(chain_psum[:, t * P:(t + 1) * P], heads_t[:, t * P:(t + 1) * P], wo_t[:],
                                         start=True, stop=True)
                    last.then_inc(chain_pe, 1)
                elif stage == "x1_turn":
                    w_dve(pe, c, f"norm{CT - 1}")
                    for t in range(CT):
                        last = pe.transpose(chain_psum[:, t * P:(t + 1) * P], x1[:, c.parity, t], ident[:])
                    last.then_inc(chain_pe, 1)
                elif stage == "route":
                    w_act(pe, c, "x1_t")
                    w_dve(pe, c, "x_lo")
                    for t in range(CT):
                        last = pe.matmul(chain_psum[:, t * E:(t + 1) * E], x1_t[:, t * P:(t + 1) * P], wg[:],
                                         start=True, stop=True)
                    last.then_inc(chain_pe, 1)
                elif stage == "rank":
                    w_dve(pe, c, f"before{CT - 1}")
                    pe.matmul(chain_psum[:, 0:CT * E], tri[:], chosen[:].rearrange("p t e -> p (t e)"),
                              start=True, stop=False)
                    pe.matmul(chain_psum[:, 0:CT * E], ones[:], before[:, 0:CT].rearrange("p t e -> p (t e)"),
                              start=False, stop=True).then_inc(chain_pe, 1)
                elif stage == "gates":
                    w_dve(pe, c, "weight")
                    for t in range(CT):
                        last = pe.transpose(chain_psum[0:E, t * P:(t + 1) * P], weight[:, t], ident[:])
                    last.then_inc(chain_pe, 1)

            def ln2(c, stage):
                if stage == "ln2_turn":
                    c.wait(pe, y_copied, 1, 1)
                    if c.it is None and c.k == CHUNKS_B - 1:
                        c.plus(-1).wait(pe, ln2_dve, len(LN2_DVE), at(LN2_DVE, "add"))
                    else:
                        c.plus(1).wait(pe, chain_dve, len(DVE_STEPS), at(DVE_STEPS, "gate_lo"))
                    for t in range(CT):
                        last = pe.transpose(chain_psum[:, t * P:(t + 1) * P], y_t[:, t * P:(t + 1) * P], ident[:])
                    last.then_inc(y_turned, 1)

            def up(c, u):
                s, par = slot(c, u), c.parity
                if u == 0:
                    w_dve(pe, c, "gate_lo")
                if (u - 2) % UNITS < PAIRS:
                    c.wait(pe, gated_done, PAIRS, max(u - 1, 0))
                else:
                    c.wait(pe, hidden_done, UNITS, u - 1)
                for k in range(2):
                    dst = up_psum[s][:, k]
                    hi, lo = w13_hi[:, k, 2 * u:2 * u + 2, :], w13_lo[:, k, 2 * u:2 * u + 2, :]
                    pe.matmul(dst, hi, x_hi[:, par], start=True, stop=False)
                    pe.matmul(dst, hi, x_lo[:, par], start=False, stop=False)
                    last = pe.matmul(dst, lo, x_hi[:, par], start=False, stop=True)
                last.then_inc(up_ready, 1)

            def gate(c, u):
                if u < PAIRS:
                    c.wait(pe, hidden_done, UNITS, u - 1)
                    pe.matmul(gate_psum[slot(c, u)][:], pair_sel[:, u * P:(u + 1) * P], gates[:, c.parity], start=True,
                              stop=True).then_inc(gate_ready, 1)

            first = Chunk(0)
            for stage, _ in STAGES:
                if stage == "rank":
                    pe.wait_ge(tri_cast, 1)
                    pe.wait_ge(pool_setup, 4)
                chain(first, stage)
            pe.wait_ge(w_lo_done, 2)
            pe.wait_ge(w2_loaded, 32)
            pe.wait_ge(pairs_rounded, 1)
            for u in range(2):
                up(first, u)
                gate(first, u)

            def body(c):
                for u in range(UNITS):
                    ahead = unit_after(c, u, 2)
                    if ahead:
                        up(*ahead)
                        gate(*ahead)
                    if u == 0:
                        c.wait(pe, y_copied, 1, 0)
                    c.wait(pe, hidden_done, UNITS, u + 1)
                    pe.matmul(y_psum[:], w2[:, u], hidden[:, slot(c, u)], start=u == 0,
                              stop=u == UNITS - 1).then_inc(down_done, 1)
                    run_stages(c, u, chain, ln2)

            run_chunks(pe, body, CHUNKS_B)
            ln2(Chunk(CHUNKS_B - 1), "ln2_turn")


def kernel(**inputs):
    import concourse.bacc as bacc
    from concourse.bass_utils import run_bass_kernel_spmd

    a = {k: np.ascontiguousarray(v) for k, v in inputs.items()}
    x = a["L0_attn_x"]
    tokens = x.reshape(-1, x.shape[-1])
    ident, tri, spread, pairs, onesrow = make_tables(a["L0_ffn_Wg"].shape[1])
    arrays = {
        "x": tokens, "xT": np.ascontiguousarray(tokens.T), "gidx": a["L0_attn_global_indices"],
        "wqkvT": np.stack([np.ascontiguousarray(a[f"L0_attn_W{c}"].T) for c in "qkv"]),
        "bq": a["L0_attn_bq"], "bk": a["L0_attn_bk"], "bv": a["L0_attn_bv"], "bo": a["L0_attn_bo"],
        "WoT": np.ascontiguousarray(a["L0_attn_Wo"].T),
        "Wg": a["L0_ffn_Wg"], "W1": a["L0_ffn_W1"], "W2": a["L0_ffn_W2"], "W3": a["L0_ffn_W3"],
        "Ws1": a["L0_ffn_Ws1"], "Ws2": a["L0_ffn_Ws2"], "Ws3": a["L0_ffn_Ws3"],
        "t_ident": ident, "t_tri": tri, "t_spread": spread, "t_pairs": pairs, "t_onesrow": onesrow,
    }
    nc = bacc.Bacc("TRN2", target_bir_lowering=False, num_devices=1)
    d = {n: nc.dram_tensor(n, v.shape, mybir.dt.from_np(v.dtype), kind="ExternalInput").ap()
         for n, v in arrays.items()}
    out = nc.dram_tensor("out", tokens.shape, F32, kind="ExternalOutput").ap()
    scratch = nc.dram_tensor("scratch", tokens.shape, F32, kind="Internal").ap()
    with ExitStack() as ctx:
        build_attention(nc, ctx, d, scratch)
    with ExitStack() as ctx:
        build_experts(nc, ctx, d, scratch, out)
    r = run_bass_kernel_spmd(nc, [arrays], core_ids=[0])
    return r.results[0]["out"].reshape(x.shape)
```

```python
from contextlib import ExitStack

import numpy as np

import concourse.bass as bass
from concourse import mybir

F32 = mybir.dt.float32
F32R = mybir.dt.float32r
BF16 = mybir.dt.bfloat16
I32 = mybir.dt.int32
ALU = mybir.AluOpType
ACT = mybir.ActivationFunctionType
AX = mybir.AxisListType

P = 128
BS = 64
DH = 8
HG = 4
LANE = 32
MAX_ROW = 24
EPS = 1e-5
TOP_K = 4

S_SLOTS = 8
A_BANKS = 3
B_BANKS = 3
O_BANKS = 2


def make_tables(E):
    ident = np.eye(P, dtype=np.float32)
    tri = np.triu(np.ones((P, P), np.float32))
    spread = np.zeros((P, 4, 4, P), np.float32)
    hi_slots = ((0, 1), (0, 2))
    lo_slots = ((2,), (1,))
    for g in range(4):
        for h in range(HG):
            for d in range(DH):
                src = (g * HG + h) * DH + d
                for qk in range(2):
                    for s in hi_slots[qk]:
                        spread[src, g, 2 * qk, LANE * h + DH * s + d] = 1
                    for s in lo_slots[qk]:
                        spread[src, g, 2 * qk + 1, LANE * h + DH * s + d] = 1
    pairs = np.zeros((P, E // 2, P), np.float32)
    for p in range(E // 2):
        for m in range(P):
            for part in range(2):
                pairs[part * E + 2 * p + m // 64, p, m] = 1
    onesrow = np.zeros((P, 2), np.float32)
    onesrow[MAX_ROW, 0] = 1
    onesrow[MAX_ROW + 1, 1] = 1
    return ident, tri, spread.reshape(P, -1), pairs.reshape(P, -1), onesrow


class Item:

    def __init__(self, ring, kind, arg, bank, use, seq):
        self.ring, self.kind, self.arg, self.bank, self.use, self.seq = ring, kind, arg, bank, use, seq


P_ITEMS = ([("main", j) for j in range(8)] + [("corner", jj) for jj in range(4)]
           + [("col", (half, h)) for half in range(2) for h in range(HG)] + [("row", j) for j in range(8)])
S_ITEMS = [("s_main", j) for j in range(8)] + [("s_corner", jj) for jj in range(4)]
S_ITEMS += [("s_col", j) for j in range(8)] + [("s_row", (h, half)) for h in range(HG) for half in range(2)]
STACKS = [(w, c) for c in range(3) for w in (1, 0)]
COPIES_AFTER = {(1, 0): 4, (0, 0): 5, (1, 1): 9, (0, 1): 10, (1, 2): 14}
COPIES = 14
P_COST = {"main": 10, "corner": 23, "col": 10, "row": 10}
MAX_ITEMS = 20
LOOKAHEAD, EARLY_RATE, S_START, S_SPAN, MAXT0_LAG, MAXT1_AT, VPROJ_AT = 2, 2, 4, 22, 5, 2, (24, 25, 26, 27)
OT_AT = (16, 18, 24, 28)
BURST = 3
FRESH_RATE, FRESH_START = 2, 6
JOB_END = {11: (0, 1), 15: (2,), 19: (3,), 27: (4,)}


def plan_attention(groups, batch_steps):
    uses, a_seq, plans = [0] * A_BANKS, 0, []
    for n in range(groups + 1):
        has_s, has_p = n < groups, n >= 1
        fresh = has_s and n % batch_steps == 0
        early = []
        if fresh:
            early += [("proj", x) for x in STACKS]
        if has_s:
            early += [("spread", x) for x in STACKS]
        scores = list(S_ITEMS) if has_s else []
        order = []
        if has_p:
            order += [("P", i) for i in range(LOOKAHEAD)]
            n_scores, given = len(scores), 0
            cost = [P_COST[kind] for kind, _ in P_ITEMS]
            start = FRESH_START if fresh else S_START
            for i in range(0, 28, 2):
                todo = []
                if i >= start:
                    share = sum(cost[start:i + 2]) / sum(cost[start:S_START + S_SPAN])
                    want = min(n_scores, int(share * n_scores + 0.5))
                    todo, given = [("A",) + x for x in scores[given:want]], want
                parts = 3 if len(todo) > BURST else 2
                cuts = [len(todo) * k // parts for k in range(parts + 1)] + [len(todo)]
                for k in range(2):
                    for _ in range(FRESH_RATE if fresh else EARLY_RATE):
                        if early:
                            order.append(("A",) + early.pop(0))
                    if i + LOOKAHEAD + k < 28:
                        order.append(("P", i + LOOKAHEAD + k))
                    if k == 1 and i == MAXT1_AT:
                        order.append(("A", "maxT", 1))
                    order += todo[cuts[k]:cuts[k + 1]]
                if has_s and given >= MAX_ITEMS + MAXT0_LAG and ("A", "maxT", 0) not in order:
                    order.append(("A", "maxT", 0))
                for k in (i, i + 1):
                    if k in OT_AT:
                        order.append(("A", "ot", OT_AT.index(k)))
                    if fresh and k in VPROJ_AT:
                        order.append(("A", "vproj", VPROJ_AT.index(k)))
                order.append(("PV", i))
                order += todo[cuts[2]:]
                order.append(("PV", i + 1))
            assert given == n_scores and not early
        else:
            order += [("A",) + x for x in early + scores[:MAX_ITEMS + MAXT0_LAG]] + [("A", "maxT", 0)]
            order += [("A",) + x for x in scores[MAX_ITEMS + MAXT0_LAG:]]
            order += [("A", "vproj", c) for c in range(4)]
        if has_p:
            order += [("A", "ot", j) for j in range(4) if OT_AT[j] == 28]
            order += [("A", "vproj", c) for c in range(4) if fresh and VPROJ_AT[c] == 28]
            order.append(("A", "ot", 4))
        plan = []
        for o in order:
            if o[0] == "A":
                bank = a_seq % A_BANKS
                plan.append(Item("A", o[1], o[2], bank, uses[bank], a_seq))
                uses[bank] += 1
                a_seq += 1
            else:
                seq = 28 * (n - 1) + o[1]
                bank = seq % (28 * batch_steps) % B_BANKS
                plan.append(Item(o[0], *P_ITEMS[o[1]], bank, seq, o[1]))
        plans.append(plan)
    return plans


V_TILES = ((0, 3), (3, 6), (6, 8), (8, 9))
CHUNKS = ((0, 512), (512, 1024), (1024, 1152))


class Step:

    def __init__(self, n, it=None):
        self.n, self.it = n, it

    def value(self, f):
        a = f(self.n)
        if self.it is None:
            return a
        d = f(self.n + 4) - a
        assert f(self.n + 8) - f(self.n + 4) == d, (self.n, a, d)
        return self.it * d + a

    def wait(self, eng, sem, f):
        v = self.value(f)
        assert self.it is None or f(self.n) > 0
        if isinstance(v, int) and v <= 0:
            return
        eng.wait_ge(sem, v)


    def gate(self, eng, passed, sem, f):
        self.wait(eng, sem, f)
        if self.it is not None:
            eng.sem_inc(passed, 1)


def run_steps(eng, step_fn, groups):
    step_fn(Step(0))
    with eng.Fori(0, groups // 4 - 1) as it:
        for k in range(4):
            step_fn(Step(1 + k, it))
    for n in range(groups - 3, groups + 1):
        step_fn(Step(n))


class Shared:

    def __init__(self, nc, ctx, d):
        E, _, HE = d["W1"].shape
        pairs = E // 2

        def sb(name, shape):
            return ctx.enter_context(nc.sbuf_tensor(name, shape, F32))

        self.w13 = sb("w13_raw", [P, 2, E + 2, HE])
        self.w2 = sb("w2", [P, pairs + 1, P])
        self.wo_t = sb("wo_t", [P, P])
        self.bo_all = sb("bo_all", [P, P])
        self.wg = sb("wg", [P, E])
        self.ident = sb("ident", [P, P])
        self.chunk = 4 * P
        self.heads = sb("heads", [P, 4, P])
        self.x_res = sb("x_res", [P, 4, P])
        self.idx = ctx.enter_context(nc.sbuf_tensor("idx", [1, 2], I32))
        self.heads_out = sb("heads_out", [P, 8, P])
        self.rows_out = sb("rows_out", [P, P])
        self.ctx_loaded = ctx.enter_context(nc.semaphore("ctx_loaded"))
        self.ctx_stored = ctx.enter_context(nc.semaphore("ctx_stored"))
        self.loaded = ctx.enter_context(nc.semaphore("weights_loaded"))
        self.transfers = [(self.wo_t[:], d["WoT"]), (self.bo_all[:], d["bo"].partition_broadcast(P)),
                          (self.wg[:], d["Wg"])]
        for k, (w, ws) in enumerate((("W1", "Ws1"), ("W3", "Ws3"))):
            self.transfers += [(self.w13[:, k, 0:E, :], d[w].rearrange("e i h -> i e h")),
                               (self.w13[:, k, E:E + 2, :], d[ws].rearrange("i (e h) -> i e h", e=2))]
        self.transfers += [(self.w2[:, 0:pairs, :], d["W2"].rearrange("(p e) h o -> (e h) p o", e=2)),
                           (self.w2[:, pairs, :], d["Ws2"])]
        self.all_loaded = 16 * len(self.transfers)
        self.all_stored = 16 + 48 * (d["xT"].shape[1] // 1024)

    def first_blocks(self, sp):
        NB = 1024 // BS
        return [sp.snap((sp.value_load(self.idx[0:1, i:i + 1], min_val=-NB, max_val=NB - 1) + NB) % NB)
                for i in range(2)]

    def store_rows(self, sp, scratch, start, block, i):
        sp.dma_start(scratch[bass.ds(start + block * BS, BS), :], self.rows_out[i * BS:(i + 1) * BS, :]
                     ).then_inc(self.ctx_stored, 16)

    def load_chunk(self, sp, scratch, x, start):
        for dst, src in ((self.heads, scratch), (self.x_res, x)):
            sp.dma_start(dst[:], src[bass.ds(start, self.chunk), :].rearrange("(t p) c -> p t c", p=P)
                         ).then_inc(self.ctx_loaded, 16)


def build_attention(nc, ctx, d, scratch, shared):
    x_t, gidx = d["xT"], d["gidx"]
    NTOK = x_t.shape[1]
    N = 1024
    B = NTOK // N
    NT = N // P
    NB = N // BS
    H = 16
    GROUPS = B * H // HG
    NG = N + 2 * BS
    SCALE = 1.0 / float(np.sqrt(np.float32(DH)))
    plans = plan_attention(GROUPS, 4)

    def find(n, kind, arg):
        for x in plans[n]:
            if x.ring == "A" and x.kind == kind and x.arg == arg:
                return x
        raise KeyError((n, kind, arg))

    def wait_free(s, eng, items, gate=None):
        last = {}
        for kind, arg in items:
            x = find(s.n, kind, arg)
            if x.bank not in last or x.use > last[x.bank].use:
                last[x.bank] = x
        for x in last.values():
            count = lambda m, x=x: find(m, x.kind, x.arg).use + 1
            if gate is None:
                s.wait(eng, a_free[x.bank], count)
            else:
                s.gate(eng, gate, a_free[x.bank], count)

    def sb(name, shape, dt=F32):
        return ctx.enter_context(nc.sbuf_tensor(name, shape, dt))

    def sem(name):
        return ctx.enter_context(nc.semaphore(name))

    idx_sb = shared.idx
    xT = sb("batch_xT", [P, NG])
    wqkv = sb("wqkv", [P, 3, P])
    bqk = sb("bqk", [P, 2])
    bv_all = sb("bv_all", [P, P])
    ident = shared.ident
    onesrow = sb("onesrow", [P, 2])
    spread = sb("spread", [P, 4, 4, P], F32R)
    qk_hi = sb("qk_hi", [P, 2, NG], F32R)
    qk_lo = sb("qk_lo", [P, 2, NG], F32R)
    q_stack = sb("q_stack", [P, NG], F32R)
    k_stack = sb("k_stack", [P, 2, NG], F32R)
    q_padded = sb("q_padded", [P, NT, 3, BS], F32R)
    k_padded = sb("k_padded", [P, 2, NT, 3, BS], F32R)
    k_heads = sb("k_heads", [P, HG, NG], F32R)
    q_heads = sb("q_heads", [P, 2, HG, N], F32R)
    q_rows = sb("q_rows", [P, 2, HG, P], F32R)
    v_next = sb("v_next", [P, NT + 1, P])
    v_aug = sb("v_aug", [P, NT + 1, H, DH + 1])
    v_top = sb("v_top", [P, NT, H, DH + 1])
    v_bot = sb("v_bot", [P, NT, H, DH + 1])
    probs = sb("probs", [P, S_SLOTS, 512])
    mx_main = sb("mx_main", [P, HG, NT])
    mx_padded = sb("mx_padded", [P, 2 * HG * NT + HG])
    mx_query = mx_padded[:, 0:2 * HG * NT].rearrange("p (k h t) -> p k h t", k=2, h=HG)
    mx_gathered = sb("mx_gathered", [P, HG])
    mx_corner = sb("mx_corner", [P, HG * NT])
    mx_row = sb("mx_row", [P, HG, 2])
    neg_query = sb("neg_query", [2 * HG * NT, P], F32R)
    neg_gathered = sb("neg_gathered", [HG, P], F32R)
    out_t = sb("out_t", [P, 2 * N + P])
    recip = sb("recip", [P, 5, 16])
    col_tmp = sb("col_tmp", [P, 4, HG, DH])
    heads_out, rows_out = shared.heads_out, shared.rows_out

    a_psum = [ctx.enter_context(nc.psum_tensor(f"a_psum{i}", [P, 512], F32)) for i in range(A_BANKS)]
    b_psum = [ctx.enter_context(nc.psum_tensor(f"b_psum{i}", [P, 512], F32)) for i in range(B_BANKS)]
    o_psum = [ctx.enter_context(nc.psum_tensor(f"o_psum{i}", [P, 512], F32)) for i in range(O_BANKS)]

    idx_loaded = sem("idx_loaded")
    proj_loaded = sem("proj_loaded")
    spread_loaded = sem("spread_loaded")
    spread_rounded = sem("spread_rounded")
    tables_loaded = sem("att_tables_loaded")
    x_loaded = sem("x_loaded")
    pool_zeroed = sem("pool_zeroed")
    dve_zeroed = sem("dve_zeroed")
    a_ready = [sem(f"a_ready{i}") for i in range(A_BANKS)]
    a_free = [sem(f"a_free{i}") for i in range(A_BANKS)]
    hi_done = sem("hi_done")
    stack_done = sem("stack_done")
    s_operands_done = sem("s_operands_done")
    p_operands_done = sem("p_operands_done")
    max_done = sem("max_done")
    neg_max_done = sem("neg_max_done")
    query_max_moved = sem("query_max_moved")
    gathered_max_moved = sem("gathered_max_moved")
    v_placed = sem("v_placed")
    b_ready = sem("b_ready")
    exp_done = sem("exp_done")
    pv_done = sem("pv_done")
    o_copied = sem("o_copied")
    recip_done = sem("recip_done")
    tmp_done = sem("tmp_done")
    ctx_stored = shared.ctx_stored
    pool_passed = sem("pool_passed")
    sp_passed = sem("sp_passed")

    def batch_of(n):
        return n // 4

    def v_count(n):
        return (n - 1) // 4 + 1

    def by_block(stack):
        return stack[:, 0:N].bitcast(F32).rearrange("p (t b c) -> p t b c", b=2, c=BS)

    def job(n, j):
        return 5 * (n - 1) + j


    with nc.Block() as block:

        @block.sync
        def _(sp):
            sp.sem_inc(ctx_stored, 16)
            sp.sem_inc(gathered_max_moved, 16)
            sp.dma_start(idx_sb[:], gidx.rearrange("(o n) -> o n", o=1)).then_inc(idx_loaded, 16)
            sp.dma_start(wqkv[:], d["wqkvT"].rearrange("w i o -> i w o")).then_inc(proj_loaded, 16)
            sp.dma_start(probs[:, 0:4].rearrange("p s c -> p (s c)"), d["t_spread"]).then_inc(spread_loaded, 16)
            sp.dma_start(xT[:, 0:N], x_t[:, 0:N]).then_inc(x_loaded, 16)
            sp.dma_start(bqk[:, 0:1], d["bq"].rearrange("(p o) -> p o", o=1)).then_inc(proj_loaded, 16)
            sp.dma_start(bqk[:, 1:2], d["bk"].rearrange("(p o) -> p o", o=1)).then_inc(proj_loaded, 16)
            sp.wait_ge(idx_loaded, 16)
            first = shared.first_blocks(sp)

            def load_gathered(b):
                for i in range(2):
                    sp.dma_start(xT[:, N + i * BS:N + (i + 1) * BS],
                                 x_t[:, bass.ds(b * N + first[i] * BS, BS)]).then_inc(x_loaded, 16)

            load_gathered(0)
            sp.dma_start(onesrow[:], d["t_onesrow"]).then_inc(tables_loaded, 16)
            sp.dma_start(ident[:], d["t_ident"]).then_inc(tables_loaded, 16)
            sp.dma_start(bv_all[:], d["bv"].partition_broadcast(P)).then_inc(tables_loaded, 16)
            for dst, src in shared.transfers:
                sp.dma_start(dst, src).then_inc(shared.loaded, 16)
            sp.wait_ge(pool_zeroed, 9)

            def step(s):
                n = s.n
                if n == GROUPS - 2:
                    sp.wait_ge(ctx_stored, 16 + 48)
                    shared.load_chunk(sp, scratch, d["x"], 0)
                if n % 4 == 1 and (s.it is None and n < GROUPS - 3 or s.it is not None):
                    last_v = find(n - 1, "vproj", 3)
                    s.gate(sp, sp_passed, a_ready[last_v.bank], lambda m: find(m - 1, "vproj", 3).use + 1)
                    following = (s.it if s.it is not None else n // 4) + 1
                    sp.dma_start(xT[:, 0:N], x_t[:, bass.ds(following * N, N)]).then_inc(x_loaded, 16)
                    load_gathered(following)
                if n > 0:
                    par = (n - 1) % 2
                    s.wait(sp, neg_max_done, lambda m: 2 * m)
                    sp.dma_start(q_rows[MAX_ROW:MAX_ROW + 1, par, :, :].bitcast(F32).rearrange(
                        "r h k -> r (h k)"), neg_gathered[:].bitcast(F32)).then_inc(gathered_max_moved, 16)
                if n < GROUPS:
                    par = n % 2
                    s.wait(sp, neg_max_done, lambda m: 2 * m + 1)
                    sp.dma_start(q_heads[MAX_ROW:MAX_ROW + 2, par, :, :].bitcast(F32).rearrange(
                        "r h k -> r (h k)"), neg_query[:].bitcast(F32)).then_inc(query_max_moved, 16)
                if n % 4 == 0 and n > 0:
                    b = (s.it if s.it is not None else n // 4 - 1)
                    wait_free(s, sp, [("ot", k) for k in range(5)], gate=sp_passed)
                    sp.dma_start(scratch[bass.ds(b * N, N), :].rearrange("(t p) c -> p t c", p=P),
                                 heads_out[:]).then_inc(ctx_stored, 16)
                    for i in range(2 if n < GROUPS else 0):
                        s.gate(sp, sp_passed, ctx_stored, lambda m, i=i: 16 + 48 * (m // 4 - 1) + 16 * (i + 1))
                        shared.store_rows(sp, scratch, b * N, first[i], i)

            run_steps(sp, step, GROUPS)

        @block.gpsimd
        def _(pool):
            pool.memset(q_padded[:, :, 1, :].bitcast(F32), 0.0).then_inc(pool_zeroed, 1)
            pool.memset(v_top[:], 0.0).then_inc(pool_zeroed, 1)
            pool.memset(v_bot[:], 0.0).then_inc(pool_zeroed, 1)
            pool.memset(v_aug[:, :, :, DH:DH + 1], 1.0).then_inc(pool_zeroed, 1)
            pool.wait_ge(pool_zeroed, 4)
            pool.memset(v_top[0:BS, :, :, DH:DH + 1], 1.0).then_inc(pool_zeroed, 1)
            pool.wait_ge(pool_zeroed, 5)
            pool.memset(v_bot[BS:P, :, :, DH:DH + 1], 1.0).then_inc(pool_zeroed, 1)
            pool.wait_ge(pool_zeroed, 6)
            pool.memset(mx_padded[:], 0.0).then_inc(pool_zeroed, 1)
            pool.memset(q_rows[:].bitcast(F32), 0.0).then_inc(pool_zeroed, 1)
            pool.memset(q_heads[:].bitcast(F32), 0.0).then_inc(pool_zeroed, 1)
            pool.wait_ge(pool_zeroed, 9)

            def step(s):
                if s.n >= GROUPS:
                    return
                par = s.n % 2
                s.gate(pool, pool_passed, stack_done, lambda m: 6 * m + 6)
                pool.tensor_copy(k_padded[:, par, :, 0:3:2, :], by_block(k_stack[:, par, :])
                                 ).then_inc(p_operands_done, 1)
                for h in range(HG):
                    rows = slice(LANE * h, LANE * h + 3 * DH)
                    s.gate(pool, pool_passed, p_operands_done, lambda m: 9 * m + 1 + 2 * h)
                    pool.tensor_copy(q_heads[rows, par, h, :], q_stack[rows, 0:N].bitcast(F32)
                                     ).then_inc(p_operands_done, 1)
                    pool.tensor_copy(q_rows[rows, par, h, :], q_stack[rows, N:NG].bitcast(F32)
                                     ).then_inc(p_operands_done, 1)

            run_steps(pool, step, GROUPS)

        @block.scalar
        def _(act):
            act.sem_inc(exp_done, B_BANKS)
            act.sem_inc(o_copied, O_BANKS)
            act.wait_ge(spread_loaded, 16)
            act.copy(spread[:].rearrange("p g k c -> p (g k c)"), probs[:, 0:4].rearrange("p s c -> p (s c)")
                     ).then_inc(spread_rounded, 1)
            act.wait_ge(proj_loaded, 48)

            def a_item(s, x):
                src = a_psum[x.bank]
                if x.kind not in ("proj", "spread", "maxT"):
                    return
                s.wait(act, a_ready[x.bank], lambda m: find(m, x.kind, x.arg).use + 1)
                if x.kind == "proj":
                    w, c = x.arg
                    lo, hi = CHUNKS[c]
                    act.activation(qk_hi[:, w, lo:hi], src[:, 0:hi - lo], ACT.Identity,
                                   bias=bqk[:, w:w + 1]).then_inc(hi_done, 1)
                elif x.kind == "spread":
                    w, c = x.arg
                    par = s.n % 2
                    lo, hi = CHUNKS[c]
                    if w == 0:
                        if c == 0:
                            s.wait(act, p_operands_done, lambda m: 9 * m)
                        act.copy(q_stack[:, lo:hi], src[:, 0:hi - lo]).then_inc(stack_done, 1)
                    else:
                        act.activation(k_stack[:, par, lo:hi], src[:, 0:hi - lo], ACT.Identity,
                                       bias=onesrow[:, c // 2:c // 2 + 1]).then_inc(stack_done, 1)
                else:
                    if x.arg == 0:
                        s.wait(act, query_max_moved, lambda m: 16 * m)
                        act.mul(neg_query[:], src[0:2 * HG * NT, 0:P], -1.0).then_inc(neg_max_done, 1)
                    else:
                        s.wait(act, gathered_max_moved, lambda m: 16 * m)
                        act.mul(neg_gathered[:], src[0:HG, 0:P], -1.0).then_inc(neg_max_done, 1)

            def step(s):
                for x in plans[s.n]:
                    if s.n == 0 and x.kind == "spread" and x.arg == (1, 0):
                        act.wait_ge(tables_loaded, 48)
                    if x.ring == "A":
                        a_item(s, x)
                    elif x.ring == "P":
                        i = x.seq
                        s.wait(act, b_ready, lambda m: 28 * (m - 1) + i + 1)
                        s.wait(act, pv_done, lambda m: 28 * (m - 1) + i + 1)
                        act.activation(probs[:, x.use % S_SLOTS, :], b_psum[x.bank][:], ACT.Exp,
                                       scale=SCALE).then_inc(exp_done, 1)
                    else:
                        for j in JOB_END.get(x.seq, ()):
                            s.wait(act, pv_done, lambda m: S_SLOTS + 28 * (m - 1) + x.seq + 1)
                            width = 512 if j < 4 else P
                            act.copy(out_t[:, 512 * j:512 * j + width],
                                     o_psum[job(s.n, j) % 2][:, 0:width]).then_inc(o_copied, 1)

            run_steps(act, step, GROUPS)

        @block.vector
        def _(dve):
            dve.memset(k_padded[:, :, :, 1, :].bitcast(F32), 0.0).then_inc(dve_zeroed, 1)
            dve.memset(k_heads[:].bitcast(F32), 0.0).then_inc(dve_zeroed, 1)
            for i in range(O_BANKS):
                last = dve.memset(o_psum[i][:], 0.0)
            last.then_inc(dve_zeroed, 1)
            dve.wait_ge(proj_loaded, 48)

            def maxima_of(s, x):
                src = a_psum[x.bank]
                if x.kind == "s_main":
                    return dve.reduce_max(mx_main[:, :, x.arg], src[:].rearrange("p (h k) -> p h k", h=HG),
                                          axis=AX.X)
                if x.kind == "s_corner":
                    out = mx_corner[:].rearrange("p (h t) -> p t h", t=NT)[:, 2 * x.arg:2 * x.arg + 2, :]
                    return dve.reduce_max(out, src[:].rearrange("p (t h k) -> p t h k", t=2, h=HG), axis=AX.X)
                if x.kind == "s_col":
                    return dve.reduce_max(mx_query[:, 1, :, x.arg], src[:].rearrange("p (h k) -> p h k", h=HG),
                                          axis=AX.X)
                h, half = x.arg
                return dve.reduce_max(mx_row[:, h, half:half + 1], src[:], axis=AX.X)

            def outputs_of(s, x):
                j = x.arg
                tiles = 4 if j < 4 else 1
                src = a_psum[x.bank][:, 0:tiles * P].rearrange("p (t h c) -> p t h c", t=tiles, h=HG)
                rec = recip[:, j, 0:tiles * HG].rearrange("p (t h) -> p t h", t=tiles)
                dve.reciprocal(rec, src[:, :, :, DH]).then_inc(recip_done, 1)
                s.wait(dve, recip_done, lambda m: job(m, j) + 1)
                rec = rec.unsqueeze(3).to_broadcast([P, tiles, HG, DH])
                g = (s.n - 1) % 4
                num = src[:, :, :, 0:DH]
                if j == 4:
                    dst = rows_out[:, LANE * g:LANE * (g + 1)].rearrange("p (h c) -> p h c", h=HG)
                    return dve.tensor_tensor(dst, num[:, 0], rec[:, 0], ALU.mult)
                half = j % 2
                dst = heads_out[:, 4 * half:4 * half + 4, LANE * g:LANE * (g + 1)].rearrange(
                    "p t (h c) -> p t h c", h=HG)
                if j < 2:
                    return dve.tensor_tensor(dst, num, rec, ALU.mult)
                wait_free(s, dve, [("ot", j - 2)] + [("ot", 2)] * (j == 3))
                dve.tensor_tensor(col_tmp[:], num, rec, ALU.mult).then_inc(tmp_done, 1)
                s.wait(dve, tmp_done, lambda m: 2 * (m - 1) + half + 1)
                return dve.tensor_tensor(dst, dst, col_tmp[:], ALU.add)

            def a_item(s, x):
                src = a_psum[x.bank]

                def ready():
                    s.wait(dve, a_ready[x.bank], lambda m: find(m, x.kind, x.arg).use + 1)

                if x.kind == "proj":
                    w, c = x.arg
                    lo, hi = CHUNKS[c]
                    s.wait(dve, hi_done, lambda m: 6 * (m // 4) + STACKS.index((w, c)) + 1)
                    dve.scalar_tensor_tensor(out=qk_lo[:, w, lo:hi], in0=src[:, 0:hi - lo],
                                             scalar=bqk[:, w:w + 1], in1=qk_hi[:, w, lo:hi].bitcast(F32),
                                             op0=ALU.add, op1=ALU.subtract).then_inc(a_free[x.bank], 1)
                elif x.kind == "spread":
                    w, c = x.arg
                    s.wait(dve, stack_done, lambda m: 6 * m + STACKS.index((w, c)) + 1)
                    dve.sem_inc(a_free[x.bank], 1)
                    lo, hi = CHUNKS[c]
                    if w == 1:
                        for h in range(HG):
                            rows = slice(LANE * h, LANE * h + 3 * DH)
                            dve.tensor_copy(k_heads[rows, h, lo:hi], k_stack[rows, s.n % 2, lo:hi].bitcast(F32)
                                            ).then_inc(s_operands_done, 1)
                    elif c < 2:
                        tiles = slice(lo // P, hi // P)
                        dve.tensor_copy(q_padded[:, tiles, 0:3:2, :], by_block(q_stack[:, :])[:, tiles]
                                        ).then_inc(s_operands_done, 1)
                elif x.kind == "maxT":
                    s.wait(dve, neg_max_done, lambda m: 2 * m + 1 - x.arg)
                    dve.sem_inc(a_free[x.bank], 1)
                elif x.kind == "vproj":
                    ready()
                    t0, t1 = V_TILES[x.arg]
                    dve.tensor_tensor(v_next[:, t0:t1, :], src[:, 0:(t1 - t0) * P].rearrange(
                        "p (t c) -> p t c", c=P), bv_all[:].unsqueeze(1).to_broadcast([P, t1 - t0, P]),
                        ALU.add).then_inc(a_free[x.bank], 1)
                elif x.kind == "ot":
                    ready()
                    if s.n % 4 == 1 and x.arg == 0:
                        s.wait(dve, ctx_stored, lambda m: 16 + 48 * (m // 4))
                    outputs_of(s, x).then_inc(a_free[x.bank], 1)
                else:
                    ready()
                    maxima_of(s, x).then_inc(a_free[x.bank], 1)
                    for last_item in (MAX_ITEMS - 1, len(S_ITEMS) - 1):
                        if (x.kind, x.arg) != S_ITEMS[last_item]:
                            continue
                        wait_free(s, dve, S_ITEMS[:last_item + 1])
                        if last_item == MAX_ITEMS - 1:
                            dve.tensor_tensor(mx_query[:, 0], mx_main[:], mx_corner[:].rearrange(
                                "p (h t) -> p h t", h=HG), ALU.max).then_inc(max_done, 1)
                        else:
                            dve.reduce_max(mx_gathered[:], mx_row[:], axis=AX.X).then_inc(max_done, 1)

            def place_v(s):
                heads_of = v_next[:].rearrange("p t (h c) -> p t h c", h=H)
                wait_free(s, dve, [("vproj", k) for k in range(4)])
                s.wait(dve, pv_done, lambda m: S_SLOTS + 28 * m)
                dve.tensor_copy(v_aug[:, :, :, 0:DH], heads_of).then_inc(v_placed, 1)
                dve.tensor_copy(v_top[0:BS, :, :, 0:DH], heads_of[0:BS, 0:NT]).then_inc(v_placed, 1)
                dve.tensor_copy(v_bot[BS:P, :, :, 0:DH], heads_of[BS:P, 0:NT]).then_inc(v_placed, 1)

            def step(s):
                for x in plans[s.n]:
                    if s.n == 0 and x.kind == "spread" and x.arg == (1, 0):
                        dve.wait_ge(tables_loaded, 48)
                        dve.wait_ge(dve_zeroed, 3)
                        dve.wait_ge(pool_zeroed, 7)
                    if x.ring == "A":
                        a_item(s, x)
                if s.n % 4 == 0 and s.n < GROUPS:
                    place_v(s)

            run_steps(dve, step, GROUPS)

        @block.tensor
        def _(pe):
            pe.sem_inc(pv_done, S_SLOTS)
            pe.wait_ge(proj_loaded, 48)

            def local_scores(out_main, out_corner, stack, padded, heads, kind, j):
                if kind == "main":
                    return pe.matmul(out_main, stack[:, j * P:(j + 1) * P], heads[:, :, j * P:(j + 1) * P],
                                     start=True, stop=True)
                before, after = (2 * j - 1) % NB, (2 * j + 2) % NB
                pe.matmul(out_corner, padded[:, j, 0:2, :], heads[:, :, before * BS:(before + 1) * BS],
                          start=True, stop=False)
                return pe.matmul(out_corner, padded[:, j, 1:3, :], heads[:, :, after * BS:(after + 1) * BS],
                                 start=False, stop=True)

            def four(bank, n=P):
                return bank[:].rearrange("p (h k) -> p h k", h=HG)

            def pair(bank, i):
                return bank[:, i * 256:(i + 1) * 256].rearrange("p (h k) -> p h k", h=HG)

            def a_item(s, x):
                out = a_psum[x.bank]
                if x.kind == "proj" and x.arg == STACKS[0]:
                    s.wait(pe, x_loaded, lambda m: 48 * (m // 4 + 1))
                if x.kind == "spread" and s.n % 4 == 0:
                    wait_free(s, pe, [("proj", x.arg)])
                for first, last_stack, copies in ((("s_main", 0), (0, 0), (0, 0)),
                                                  (("s_main", 4), (0, 1), (0, 1)),
                                                  (("s_col", 0), (0, 2), (1, 2))):
                    if (x.kind, x.arg) == first:
                        s.wait(pe, stack_done, lambda m: 6 * m + STACKS.index(last_stack) + 1)
                        s.wait(pe, s_operands_done, lambda m: COPIES * m + COPIES_AFTER[copies])
                if x.kind == "maxT":
                    s.wait(pe, max_done, lambda m: 2 * m + 1 - x.arg)
                if x.kind == "ot":
                    s.wait(pe, o_copied, lambda m: O_BANKS + job(m, x.arg) + 1)
                s.wait(pe, a_free[x.bank], lambda m: find(m, x.kind, x.arg).use)
                if x.kind == "proj":
                    w, c = x.arg
                    lo, hi = CHUNKS[c]
                    last = pe.matmul(out[:, 0:hi - lo], wqkv[:, w, :], xT[:, lo:hi], start=True, stop=True)
                elif x.kind == "vproj":
                    t0, t1 = V_TILES[x.arg]
                    for t in range(t0, t1):
                        last = pe.matmul(out[:, (t - t0) * P:(t - t0 + 1) * P], xT[:, t * P:(t + 1) * P],
                                         wqkv[:, 2, :], start=True, stop=True)
                elif x.kind == "spread":
                    w, c = x.arg
                    g = s.n % 4
                    lo, hi = CHUNKS[c]
                    pe.matmul(out[:, 0:hi - lo], spread[:, g, 2 * w, :], qk_hi[:, w, lo:hi], start=True, stop=False)
                    last = pe.matmul(out[:, 0:hi - lo], spread[:, g, 2 * w + 1, :], qk_lo[:, w, lo:hi],
                                     start=False, stop=True)
                elif x.kind == "s_main":
                    last = local_scores(four(out), None, q_stack, q_padded, k_heads, "main", x.arg)
                elif x.kind == "s_corner":
                    for i in range(2):
                        last = local_scores(None, pair(out, i), q_stack, q_padded, k_heads, "corner", 2 * x.arg + i)
                elif x.kind == "s_col":
                    last = pe.matmul(four(out), q_stack[:, x.arg * P:(x.arg + 1) * P], k_heads[:, :, N:NG],
                                     start=True, stop=True)
                elif x.kind == "s_row":
                    h, half = x.arg
                    last = pe.matmul(out[:], q_stack[:, N:NG], k_heads[:, h, half * 512:(half + 1) * 512],
                                     start=True, stop=True)
                elif x.kind == "maxT":
                    maxima = (mx_padded[:], mx_gathered[:])[x.arg]
                    last = pe.transpose(out[0:maxima.shape[1], 0:P], maxima, ident[:])
                else:
                    j = x.arg
                    for t in range(4 if j < 4 else 1):
                        last = pe.transpose(out[:, t * P:(t + 1) * P],
                                            out_t[:, 512 * j + t * P:512 * j + (t + 1) * P], ident[:])
                last.then_inc(a_ready[x.bank], 1)

            def scores_t(s, x):
                i = x.seq
                par = (s.n - 1) % 2
                if i == 0:
                    s.wait(pe, p_operands_done, lambda m: 9 * m)
                    s.wait(pe, query_max_moved, lambda m: 16 * m)
                if i == MAX_ITEMS:
                    s.wait(pe, gathered_max_moved, lambda m: 16 * m + 16)
                since = B_BANKS if i == 0 and s.n % 4 == 1 else 1
                s.wait(pe, exp_done, lambda m: 28 * (m - 1) + i + since)
                out = b_psum[x.bank]
                ks, kp, qh, qr = k_stack[:, par], k_padded[:, par], q_heads[:, par], q_rows[:, par]
                if x.kind == "main":
                    last = local_scores(four(out), None, ks, kp, qh, "main", x.arg)
                elif x.kind == "corner":
                    for k in range(2):
                        last = local_scores(None, pair(out, k), ks, kp, qh, "corner", 2 * x.arg + k)
                elif x.kind == "col":
                    half, h = x.arg
                    last = pe.matmul(out[:], ks[:, N:NG], qh[:, h, half * 512:(half + 1) * 512],
                                     start=True, stop=True)
                else:
                    last = pe.matmul(four(out), ks[:, x.arg * P:(x.arg + 1) * P], qr[:, :, :], start=True, stop=True)
                last.then_inc(b_ready, 1)

            def weighted_v(s, x):
                i = x.seq
                g = (s.n - 1) % 4
                if i == 0:
                    s.wait(pe, v_placed, lambda m: 3 * v_count(m))
                for j, first_item in ((0, 0), (1, 4), (2, 12), (3, 16), (4, 20)):
                    if i == first_item:
                        s.wait(pe, o_copied, lambda m: job(m, j) + 1)
                s.wait(pe, exp_done, lambda m: B_BANKS + 28 * (m - 1) + i + 1)
                probs_i = probs[:, x.use % S_SLOTS, :]
                for h in range(HG):
                    hh = HG * g + h
                    rows = slice(LANE * h, LANE * h + DH + 1)
                    if x.kind == "main":
                        j = x.arg
                        last = pe.matmul(o_psum[job(s.n, j // 4) % 2][rows, (j % 4) * P:(j % 4 + 1) * P],
                                         v_aug[:, j, hh, :], probs_i[:, h * P:(h + 1) * P],
                                         start=j % 4 == 0, stop=False)
                    elif x.kind == "corner":
                        for k in range(2):
                            j = 2 * x.arg + k
                            for v, blk in ((v_top, (2 * j - 1) % NB), (v_bot, (2 * j + 2) % NB)):
                                half, c = blk // 8, blk % 8
                                last = pe.matmul(o_psum[job(s.n, half) % 2][rows, c * BS:(c + 1) * BS],
                                                 v[:, j, hh, :], probs_i[:, k * 256 + h * BS:k * 256 + (h + 1) * BS],
                                                 start=False, stop=j == NT - 1)
                    elif x.kind == "col":
                        half, hx = x.arg
                        if hx != h:
                            continue
                        last = pe.matmul(o_psum[job(s.n, 2 + half) % 2][rows, :], v_aug[:, NT, hh, :], probs_i,
                                         start=True, stop=True)
                    else:
                        j = x.arg
                        last = pe.matmul(o_psum[job(s.n, 4) % 2][rows, 0:P], v_aug[:, j, hh, :],
                                         probs_i[:, h * P:(h + 1) * P], start=j == 0, stop=j == NT - 1)
                last.then_inc(pv_done, 1)

            def step(s):
                for x in plans[s.n]:
                    if s.n == 0 and x.kind == "spread" and x.arg == (1, 0):
                        pe.wait_ge(spread_rounded, 1)
                        pe.wait_ge(tables_loaded, 48)
                        pe.wait_ge(dve_zeroed, 3)
                        pe.wait_ge(pool_zeroed, 7)
                    if x.ring == "A":
                        a_item(s, x)
                    elif x.ring == "P":
                        scores_t(s, x)
                    else:
                        weighted_v(s, x)

            run_steps(pe, step, GROUPS)


class Chunk:

    def __init__(self, k, it=None):
        self.k, self.it = k, it
        self.parity = k % 2

    def plus(self, more):
        return Chunk(self.k + more, self.it)

    def times(self, per_chunk, more=0):
        if self.it is None:
            return self.k * per_chunk + more
        return self.it * (2 * per_chunk) + (self.k * per_chunk + more)

    def wait(self, eng, sem, per_chunk, more):
        v = self.times(per_chunk, more)
        assert self.it is None or self.k * per_chunk + more > 0
        if isinstance(v, int) and v <= 0:
            return
        eng.wait_ge(sem, v)

    def gate(self, eng, passed, sem, per_chunk, more):
        self.wait(eng, sem, per_chunk, more)
        if self.it is not None:
            eng.sem_inc(passed, 1)


def run_chunks(eng, body, chunks):
    body(Chunk(0))
    with eng.Fori(0, (chunks - 2) // 2) as it:
        body(Chunk(1, it))
        body(Chunk(2, it))
    body(Chunk(chunks - 1))


def build_experts(nc, ctx, d, scratch, out, shared):
    NTOK = scratch.shape[0]
    C = 512
    CT = C // P
    CHUNKS_B = NTOK // C
    E, _, HE = d["W1"].shape
    PAIRS = E // 2
    UNITS = PAIRS + 1
    RING = 4
    CAPACITY = 4 * NTOK * TOP_K // E

    def sb(name, shape, dt=F32):
        return ctx.enter_context(nc.sbuf_tensor(name, shape, dt))

    def sem(name):
        return ctx.enter_context(nc.semaphore(name))

    tri_f = sb("tri_f", [P, P])
    tri = sb("tri", [P, P], BF16)
    ones = sb("ones", [P, P], BF16)
    ident, heads, x_res, ctx_loaded = shared.ident, shared.heads, shared.x_res, shared.ctx_loaded
    wo_t, bo_all, wg, w13_raw, w2 = shared.wo_t, shared.bo_all, shared.wg, shared.w13, shared.w2
    eps = sb("eps", [P, 1])
    w13_hi = sb("w13_hi", [P, 2, E + 2, HE], F32R)
    w13_lo = sb("w13_lo", [P, 2, E + 2, HE], F32R)
    w2_hi = sb("w2_hi", [P, UNITS, P], F32R)
    w2_lo = sb("w2_lo", [P, UNITS, P], F32R)
    pair_sel_f = sb("pair_sel_f", [P, PAIRS * P])
    pair_sel = sb("pair_sel", [P, PAIRS * P], F32R)
    x_hi = sb("x_hi", [P, 2, C], F32R)
    x_lo = sb("x_lo", [P, 2, C], F32R)
    gates = sb("gates", [P, 2, C], F32R)
    x1 = sb("x1", [P, 2, CT, P])
    heads_t = sb("heads_t", [P, C])
    x_bias = sb("x_bias", [P, CT, P])
    y1 = sb("y1", [P, CT, P])
    stats = sb("stats", [P, CT, 6])
    moments = sb("moments", [P, CT, 2])
    std = sb("std", [P, CT])
    rstd = sb("rstd", [P, CT])
    x1_t = sb("x1_t", [P, C])
    logits = sb("logits", [P, CT, E])
    top8 = sb("top8", [P, CT, 8])
    shifted = sb("shifted", [P, CT, E])
    expd = sb("expd", [P, CT, E])
    esum = sb("esum", [P, CT])
    rsum = sb("rsum", [P, CT])
    above = sb("above", [P, CT, E])
    equal = sb("equal", [P, CT, E])
    n_above = sb("n_above", [P, CT])
    nth_equal = sb("nth_equal", [P, CT, E])
    taken = sb("taken", [P, CT, E])
    chosen = sb("chosen", [P, CT, E], BF16)
    n_chosen = sb("n_chosen", [P, E])
    before = sb("before", [P, E], BF16)
    kept = sb("kept", [P, CT, E])
    kept_e = sb("kept_e", [P, CT, E])
    weight = sb("weight", [P, CT, E])
    silu = sb("silu", [P, 2, C])
    gated = sb("gated", [P, 2, C])
    hidden = sb("hidden", [P, RING + 1, C])
    hidden_hi = sb("hidden_hi", [P, RING + 1, C], F32R)
    hidden_lo = sb("hidden_lo", [P, RING + 1, C], F32R)
    y_t = sb("y_t", [P, C])
    z = sb("z", [P, CT, P])
    stats2 = sb("stats2", [P, CT, 6])
    moments2 = sb("moments2", [P, CT, 2])
    std2 = sb("std2", [P, CT])
    rstd2 = sb("rstd2", [P, CT])
    result = sb("result", [P, CT, P])

    chain_psum = ctx.enter_context(nc.psum_tensor("chain_psum", [P, 512], F32))
    up_psum = [ctx.enter_context(nc.psum_tensor(f"up_psum{i}", [P, 2, 512], F32)) for i in range(2)]
    gate_psum = [ctx.enter_context(nc.psum_tensor(f"gate_psum{i}", [P, 512], F32)) for i in range(2)]
    y_psum = ctx.enter_context(nc.psum_tensor("y_psum", [P, 512], F32))

    tables_loaded = sem("tables_loaded")
    w_hi_done = sem("w_hi_done")
    w_lo_done = sem("w_lo_done")
    pool_setup = sem("pool_setup")
    tri_cast = sem("tri_cast")
    pairs_loaded = sem("pairs_loaded")
    pairs_rounded = sem("pairs_rounded")
    x_bias_done = sem("x_bias_done")
    chain_pe = sem("chain_pe")
    chain_act = sem("chain_act")
    chain_dve = sem("chain_dve")
    up_ready = sem("up_ready")
    gate_ready = sem("gate_ready")
    silu_done = sem("silu_done")
    gated_done = sem("gated_done")
    hidden_done = sem("hidden_done")
    hidden_hi_done = sem("hidden_hi_done")
    hidden_lo_done = sem("hidden_lo_done")
    down_done = sem("down_done")
    y_copied = sem("y_copied")
    y_turned = sem("y_turned")
    ln2_dve = sem("ln2_dve")
    ln2_act = sem("ln2_act")
    stored = sem("stored")
    dve_passed = sem("dve_passed")
    sp_passed = sem("sp2_passed")
    pool_passed = sem("pool2_passed")

    DVE_STEPS = (["residual"] + [f"stats{t}" for t in range(CT)] + [f"aggr{t}" for t in range(CT)]
                 + ["rstd"] + [f"norm{t}" for t in range(CT)] + ["x_lo", "logits"]
                 + [f"top{t}" for t in range(CT)] + ["shift", "above", "equal", "n_above"]
                 + [f"nth{t}" for t in range(CT)] + ["taken", "chosen"]
                 + ["esum", "rsum", "kept", "kept_e", "weight", "gate_lo", "n_chosen", "carry"])
    ACT_STEPS = ["heads_t", "std", "x1_t", "x_hi", "exp", "gate_hi"]
    PE_STEPS = ["heads_t", "proj", "x1_t", "route", "rank", "gates"]
    LN2_DVE = (["add"] + [f"stats{t}" for t in range(CT)] + [f"aggr{t}" for t in range(CT)] + ["rstd"]
               + [f"norm{t}" for t in range(CT)])
    STAGES = (("heads_t", 0), ("heads_copy", 2), ("proj", 1), ("residual", 2), ("ln2_copy", 3),
              ("ln2_turn", 3), ("stats", 3), ("ln2_add", 4), ("ln2_stats", 5), ("std", 8), ("ln2_std", 8),
              ("norm", 7), ("x1_turn", 7), ("x1_copy", 9), ("x_lo", 8), ("route", 8), ("logits", 9),
              ("compare", 10), ("exp", 13), ("choose", 11), ("rank", 11), ("weight", 12), ("gates", 12),
              ("gate_hi", 14), ("gate_lo", 13), ("ln2_norm", 15))

    def at(steps, name):
        return steps.index(name) + 1

    def w_dve(eng, c, name):
        c.wait(eng, chain_dve, len(DVE_STEPS), at(DVE_STEPS, name))

    def w_act(eng, c, name):
        c.wait(eng, chain_act, len(ACT_STEPS), at(ACT_STEPS, name))

    def w_pe(eng, c, name):
        c.wait(eng, chain_pe, len(PE_STEPS), at(PE_STEPS, name))

    def tiles_of(dram, c):
        return dram[bass.ds(c.times(C), C), :].rearrange("(t p) c -> p t c", p=P)

    def run_stages(c, u, chain, ln2):
        for stage, unit in STAGES:
            if unit != u:
                continue
            if stage.startswith("ln2"):
                if not (c.it is None and c.k == 0):
                    ln2(c.plus(-1), stage)
            elif not (c.it is None and c.k == CHUNKS_B - 1):
                chain(c.plus(1), stage)

    def unit_after(c, u, more):
        u += more
        while u >= UNITS:
            u, c = u - UNITS, c.plus(1)
        while u < 0:
            u, c = u + UNITS, c.plus(-1)
        if c.it is None and not 0 <= c.k < CHUNKS_B:
            return None
        return c, u

    def slot(c, u):
        return (c.k * UNITS + u) % 2

    def ring(u):
        return u % RING if u < PAIRS else RING

    def ring_user(u):
        return 0 if u == PAIRS else u - RING + 1 if u >= RING else u - RING

    with nc.Block() as block:

        @block.sync
        def _(sp):
            sp.sem_inc(stored, 16)
            sp.dma_start(tri_f[:], d["t_tri"]).then_inc(tables_loaded, 16)
            sp.dma_start(pair_sel_f[:], d["t_pairs"]).then_inc(pairs_loaded, 16)

            def next_chunk(c):
                before_c = c.plus(-1)
                before_c.gate(sp, sp_passed, chain_pe, len(PE_STEPS), at(PE_STEPS, "heads_t"))
                before_c.gate(sp, sp_passed, x_bias_done, 1, 1)
                shared.load_chunk(sp, scratch, d["x"], c.times(C))

            def store(c):
                c.gate(sp, sp_passed, ln2_dve, len(LN2_DVE), len(LN2_DVE))
                sp.dma_start(tiles_of(out, c), result[:]).then_inc(stored, 16)

            first = shared.first_blocks(sp)
            for i in range(2):
                sp.wait_ge(shared.ctx_stored, shared.all_stored - 32 + 16 * i)
                shared.store_rows(sp, scratch, NTOK - 1024, first[i], i)
            sp.wait_ge(shared.ctx_stored, shared.all_stored)
            next_chunk(Chunk(1))

            def body(c):
                if not (c.it is None and c.k == CHUNKS_B - 1) and not (c.it is None and c.k == 0):
                    next_chunk(c.plus(1))
                if not (c.it is None and c.k == 0):
                    store(c.plus(-1))

            run_chunks(sp, body, CHUNKS_B)
            store(Chunk(CHUNKS_B - 1))
            sp.wait_ge(stored, 16 + 16 * CHUNKS_B)

        @block.gpsimd
        def _(pool):
            pool.memset(ones[:], 1.0).then_inc(pool_setup, 1)
            pool.memset(eps[:], EPS).then_inc(pool_setup, 1)
            pool.memset(before[:], 0.0).then_inc(pool_setup, 1)
            pool.memset(gates[:].bitcast(F32), 0.0).then_inc(pool_setup, 1)
            pool.wait_ge(shared.loaded, shared.all_loaded)

            def add_bias(c):
                c.gate(pool, pool_passed, ctx_loaded, 32, 32)
                c.gate(pool, pool_passed, chain_dve, len(DVE_STEPS), at(DVE_STEPS, "residual") - len(DVE_STEPS))
                pool.tensor_tensor(x_bias[:], x_res[:], bo_all[:].unsqueeze(1).to_broadcast([P, CT, P]),
                                   ALU.add).then_inc(x_bias_done, 1)

            add_bias(Chunk(0))
            for k in range(2):
                if k == 1:
                    pool.wait_ge(tables_loaded, 16)
                    pool.tensor_copy(tri[:], tri_f[:]).then_inc(tri_cast, 1)
                pool.wait_ge(w_hi_done, k + 1)
                pool.tensor_tensor(w13_lo[:, k], w13_raw[:, k], w13_hi[:, k].bitcast(F32),
                                   ALU.subtract).then_inc(w_lo_done, 1)

            pool.wait_ge(w_hi_done, 3)
            pool.tensor_tensor(w2_lo[:], w2[:], w2_hi[:].bitcast(F32), ALU.subtract).then_inc(w_lo_done, 1)

            def body(c):
                if not (c.it is None and c.k == CHUNKS_B - 1):
                    add_bias(c.plus(1))
                for u in range(UNITS):
                    s = ring(u)
                    c.gate(pool, pool_passed, down_done, UNITS, ring_user(u) + 1)
                    c.gate(pool, pool_passed, hidden_hi_done, UNITS, u + 1)
                    pool.tensor_tensor(hidden_lo[:, s], hidden[:, s], hidden_hi[:, s].bitcast(F32),
                                       ALU.subtract).then_inc(hidden_lo_done, 1)

            run_chunks(pool, body, CHUNKS_B)

        @block.scalar
        def _(act):
            act.wait_ge(shared.loaded, shared.all_loaded)
            act.wait_ge(pool_setup, 4)

            def chain(c, stage):
                par = c.parity
                if stage == "heads_copy":
                    w_pe(act, c, "heads_t")
                    act.copy(heads_t[:], chain_psum[:]).then_inc(chain_act, 1)
                elif stage == "std":
                    w_dve(act, c, f"aggr{CT - 1}")
                    act.activation(std[:], moments[:, :, 1], ACT.Sqrt, bias=eps[:]).then_inc(chain_act, 1)
                elif stage == "x1_copy":
                    w_pe(act, c, "x1_t")
                    act.copy(x1_t[:], chain_psum[:]).then_inc(chain_act, 1)
                    act.copy(x_hi[:, par], chain_psum[:]).then_inc(chain_act, 1)
                elif stage == "exp":
                    w_dve(act, c, "shift")
                    act.activation(expd[:], shifted[:], ACT.Exp).then_inc(chain_act, 1)
                elif stage == "gate_hi":
                    w_pe(act, c, "gates")
                    act.copy(gates[0:E, par], chain_psum[0:E, :]).then_inc(chain_act, 1)

            def ln2(c, stage):
                if stage == "ln2_copy":
                    c.wait(act, down_done, UNITS, UNITS + 1)
                    c.wait(act, y_turned, 1, 1)
                    act.copy(y_t[:], y_psum[:]).then_inc(y_copied, 1)
                elif stage == "ln2_std":
                    c.wait(act, ln2_dve, len(LN2_DVE), at(LN2_DVE, f"aggr{CT - 1}"))
                    act.activation(std2[:], moments2[:, :, 1], ACT.Sqrt, bias=eps[:]).then_inc(ln2_act, 1)

            for stage, _ in STAGES:
                chain(Chunk(0), stage)
                if stage in ("heads_copy", "std"):
                    k = ("heads_copy", "std").index(stage)
                    act.copy(w13_hi[:, k], w13_raw[:, k]).then_inc(w_hi_done, 1)
                elif stage == "x1_copy":
                    act.copy(w2_hi[:], w2[:]).then_inc(w_hi_done, 1)

            def split_hidden(c, u):
                s = ring(u)
                c.wait(act, hidden_done, UNITS, u + 1)
                c.wait(act, down_done, UNITS, ring_user(u) + 1)
                act.copy(hidden_hi[:, s], hidden[:, s]).then_inc(hidden_hi_done, 1)

            def body(c):
                for u in range(UNITS):
                    c.wait(act, up_ready, UNITS, u + 1)
                    s = slot(c, u)
                    act.activation(silu[:, s], up_psum[s][:, 0], ACT.Silu).then_inc(silu_done, 1)
                    if unit_after(c, u, -2):
                        split_hidden(*unit_after(c, u, -2))
                    run_stages(c, u, chain, ln2)

            run_chunks(act, body, CHUNKS_B)
            for u in (UNITS - 2, UNITS - 1):
                split_hidden(Chunk(CHUNKS_B - 1), u)
            ln2(Chunk(CHUNKS_B - 1), "ln2_copy")
            ln2(Chunk(CHUNKS_B - 1), "ln2_std")

        @block.vector
        def _(dve):
            dve.wait_ge(pool_setup, 4)

            def own(c, name):
                w_dve(dve, c, name)
                if c.it is not None:
                    dve.sem_inc(dve_passed, 1)

            def own2(c, name):
                c.gate(dve, dve_passed, ln2_dve, len(LN2_DVE), at(LN2_DVE, name))

            def done(ins):
                ins.then_inc(chain_dve, 1)

            def per_tile(x, width):
                return x.unsqueeze(2).to_broadcast([P, CT, width])

            def chain(c, stage):
                par = c.parity
                if stage == "residual":
                    c.gate(dve, dve_passed, x_bias_done, 1, 1)
                    w_pe(dve, c, "proj")
                    done(dve.tensor_tensor(y1[:], chain_psum[:].rearrange("p (t c) -> p t c", t=CT), x_bias[:],
                                           ALU.add))
                elif stage == "stats":
                    own(c, "residual")
                    for t in range(CT):
                        done(dve.bn_stats(stats[:, t], y1[:, t]))
                    own(c, f"stats{CT - 1}")
                    for t in range(CT):
                        done(dve.bn_aggr(moments[:, t], stats[:, t]))
                elif stage == "norm":
                    w_act(dve, c, "std")
                    done(dve.reciprocal(rstd[:], std[:]))
                    own(c, "rstd")
                    for t in range(CT):
                        done(dve.tensor_scalar(x1[:, par, t], y1[:, t], moments[:, t, 0:1], rstd[:, t:t + 1],
                                               ALU.subtract, ALU.mult))
                elif stage == "x_lo":
                    w_act(dve, c, "x_hi")
                    done(dve.tensor_tensor(x_lo[:, par], chain_psum[:], x_hi[:, par].bitcast(F32),
                                           ALU.subtract))
                elif stage == "logits":
                    w_pe(dve, c, "route")
                    done(dve.tensor_copy(logits[:], chain_psum[:, 0:CT * E].rearrange("p (t e) -> p t e", t=CT)))
                    own(c, "logits")
                    for t in range(CT):
                        done(dve.max(top8[:, t], logits[:, t]))
                elif stage == "compare":
                    own(c, f"top{CT - 1}")
                    done(dve.tensor_tensor(shifted[:], logits[:], per_tile(top8[:, :, 0], E), ALU.subtract))
                    fourth = per_tile(top8[:, :, TOP_K - 1], E)
                    done(dve.tensor_tensor(above[:], logits[:], fourth, ALU.is_gt))
                    done(dve.tensor_tensor(equal[:], logits[:], fourth, ALU.is_equal))
                    own(c, "equal")
                    done(dve.reduce_sum(n_above[:], above[:], axis=AX.X))
                elif stage == "choose":
                    own(c, "n_above")
                    for t in range(CT):
                        done(dve.tensor_tensor_scan(nth_equal[:, t], equal[:, t], equal[:, t], n_above[:, t:t + 1],
                                                    ALU.add, ALU.bypass))
                    own(c, f"nth{CT - 1}")
                    done(dve.scalar_tensor_tensor(out=taken[:], in0=nth_equal[:], scalar=float(TOP_K),
                                                  in1=equal[:], op0=ALU.is_le, op1=ALU.mult))
                    own(c, "taken")
                    done(dve.tensor_tensor(chosen[:], taken[:], above[:], ALU.add))
                elif stage == "weight":
                    w_act(dve, c, "exp")
                    done(dve.reduce_sum(esum[:], expd[:], axis=AX.X))
                    own(c, "esum")
                    done(dve.reciprocal(rsum[:], esum[:]))
                    w_pe(dve, c, "rank")
                    own(c, "rsum")
                    rank = chain_psum[:, 0:CT * E].rearrange("p (t e) -> p t e", t=CT)
                    done(dve.scalar_tensor_tensor(out=kept[:], in0=rank, scalar=float(CAPACITY), in1=chosen[:],
                                                  op0=ALU.is_le, op1=ALU.mult))
                    own(c, "kept")
                    done(dve.tensor_tensor(kept_e[:], kept[:], expd[:], ALU.mult))
                    own(c, "kept_e")
                    done(dve.tensor_tensor(weight[:], kept_e[:], per_tile(rsum[:], E), ALU.mult))
                elif stage == "gate_lo":
                    w_act(dve, c, "gate_hi")
                    done(dve.tensor_tensor(gates[E:2 * E, par], chain_psum[0:E, :],
                                           gates[0:E, par].bitcast(F32), ALU.subtract))
                    done(dve.reduce_sum(n_chosen[:], chosen[:].rearrange("p t e -> p e t"), axis=AX.X))
                    own(c, "n_chosen")
                    done(dve.tensor_tensor(before[:], before[:], n_chosen[:], ALU.add))

            def ln2(c, stage):
                if stage == "ln2_add":
                    c.wait(dve, y_turned, 1, 2)
                    dve.tensor_tensor(z[:], chain_psum[:].rearrange("p (t c) -> p t c", t=CT),
                                      x1[:, c.parity], ALU.add).then_inc(ln2_dve, 1)
                elif stage == "ln2_stats":
                    own2(c, "add")
                    for t in range(CT):
                        dve.bn_stats(stats2[:, t], z[:, t]).then_inc(ln2_dve, 1)
                    own2(c, f"stats{CT - 1}")
                    for t in range(CT):
                        dve.bn_aggr(moments2[:, t], stats2[:, t]).then_inc(ln2_dve, 1)
                elif stage == "ln2_norm":
                    c.wait(dve, ln2_act, 1, 1)
                    dve.reciprocal(rstd2[:], std2[:]).then_inc(ln2_dve, 1)
                    c.gate(dve, dve_passed, stored, 16, 16)
                    own2(c, "rstd")
                    for t in range(CT):
                        dve.tensor_scalar(result[:, t], z[:, t], moments2[:, t, 0:1], rstd2[:, t:t + 1],
                                          ALU.subtract, ALU.mult).then_inc(ln2_dve, 1)

            for stage, _ in STAGES:
                chain(Chunk(0), stage)
                if stage == "x_lo":
                    dve.wait_ge(pairs_loaded, 16)
                    dve.tensor_copy(pair_sel[:], pair_sel_f[:]).then_inc(pairs_rounded, 1)

            def gate_unit(c, u):
                if u < PAIRS:
                    s = slot(c, u)
                    c.wait(dve, silu_done, UNITS, u + 1)
                    c.gate(dve, dve_passed, hidden_done, UNITS, u - 1)
                    dve.tensor_tensor(gated[:, s], silu[:, s], up_psum[s][:, 1], ALU.mult).then_inc(gated_done, 1)

            def finish_hidden(c, u):
                s = slot(c, u)
                c.gate(dve, dve_passed, hidden_lo_done, UNITS, ring_user(u))
                if u < PAIRS:
                    c.gate(dve, dve_passed, gated_done, PAIRS, u + 1)
                    c.wait(dve, gate_ready, PAIRS, u + 1)
                    dve.tensor_tensor(hidden[:, ring(u)], gated[:, s], gate_psum[s][:],
                                      ALU.mult).then_inc(hidden_done, 1)
                else:
                    c.wait(dve, silu_done, UNITS, u + 1)
                    dve.tensor_tensor(hidden[:, ring(u)], silu[:, s], up_psum[s][:, 1],
                                      ALU.mult).then_inc(hidden_done, 1)

            def body(c):
                for u in range(UNITS):
                    following = unit_after(c, u, 1)
                    if u == PAIRS:
                        finish_hidden(c, u)
                    if following:
                        gate_unit(*following)
                    if u < PAIRS:
                        finish_hidden(c, u)
                    run_stages(c, u, chain, ln2)

            gate_unit(Chunk(0), 0)
            run_chunks(dve, body, CHUNKS_B)
            for stage in ("ln2_add", "ln2_stats", "ln2_norm"):
                ln2(Chunk(CHUNKS_B - 1), stage)

        @block.tensor
        def _(pe):
            pe.sem_inc(down_done, 1)
            pe.sem_inc(y_turned, 1)
            pe.wait_ge(shared.loaded, shared.all_loaded)

            def chain(c, stage):
                if stage == "heads_t":
                    c.wait(pe, ctx_loaded, 32, 32)
                    c.plus(-1).wait(pe, chain_dve, len(DVE_STEPS), at(DVE_STEPS, "gate_lo"))
                    for t in range(CT):
                        last = pe.transpose(chain_psum[:, t * P:(t + 1) * P], heads[:, t], ident[:])
                    last.then_inc(chain_pe, 1)
                elif stage == "proj":
                    w_act(pe, c, "heads_t")
                    for t in range(CT):
                        last = pe.matmul(chain_psum[:, t * P:(t + 1) * P], heads_t[:, t * P:(t + 1) * P], wo_t[:],
                                         start=True, stop=True)
                    last.then_inc(chain_pe, 1)
                elif stage == "x1_turn":
                    w_dve(pe, c, f"norm{CT - 1}")
                    c.plus(-2).wait(pe, ln2_dve, len(LN2_DVE), at(LN2_DVE, "add"))
                    for t in range(CT):
                        last = pe.transpose(chain_psum[:, t * P:(t + 1) * P], x1[:, c.parity, t], ident[:])
                    last.then_inc(chain_pe, 1)
                elif stage == "route":
                    w_act(pe, c, "x1_t")
                    w_dve(pe, c, "x_lo")
                    for t in range(CT):
                        last = pe.matmul(chain_psum[:, t * E:(t + 1) * E], x1_t[:, t * P:(t + 1) * P], wg[:],
                                         start=True, stop=True)
                    last.then_inc(chain_pe, 1)
                elif stage == "rank":
                    w_dve(pe, c, "chosen")
                    c.plus(-1).wait(pe, chain_dve, len(DVE_STEPS), at(DVE_STEPS, "carry"))
                    flat = chosen[:].rearrange("p t e -> p (t e)")
                    pe.matmul(chain_psum[:, 0:CT * E], tri[:], flat, start=True, stop=False)
                    for back in range(1, CT):
                        pe.matmul(chain_psum[:, back * E:CT * E], ones[:], flat[:, 0:(CT - back) * E],
                                  start=False, stop=False)
                    for t in range(CT):
                        last = pe.matmul(chain_psum[:, t * E:(t + 1) * E], ones[:], before[:],
                                         start=False, stop=t == CT - 1)
                    last.then_inc(chain_pe, 1)
                elif stage == "gates":
                    w_dve(pe, c, "weight")
                    for t in range(CT):
                        last = pe.transpose(chain_psum[0:E, t * P:(t + 1) * P], weight[:, t], ident[:])
                    last.then_inc(chain_pe, 1)

            def ln2(c, stage):
                if stage == "ln2_turn":
                    c.wait(pe, y_copied, 1, 1)
                    if c.it is None and c.k == CHUNKS_B - 1:
                        c.plus(-1).wait(pe, ln2_dve, len(LN2_DVE), at(LN2_DVE, "add"))
                    elif c.it is None and c.k == CHUNKS_B - 2:
                        c.plus(1).wait(pe, chain_dve, len(DVE_STEPS), at(DVE_STEPS, "gate_lo"))
                    else:
                        c.plus(2).wait(pe, chain_dve, len(DVE_STEPS), at(DVE_STEPS, "residual"))
                    for t in range(CT):
                        last = pe.transpose(chain_psum[:, t * P:(t + 1) * P], y_t[:, t * P:(t + 1) * P], ident[:])
                    last.then_inc(y_turned, 1)

            def up(c, u):
                s, par = slot(c, u), c.parity
                if u == 0:
                    w_dve(pe, c, "x_lo")
                if (u - 2) % UNITS < PAIRS:
                    c.wait(pe, gated_done, PAIRS, max(u - 1, 0))
                else:
                    c.wait(pe, hidden_done, UNITS, u - 1)
                for k in range(2):
                    dst = up_psum[s][:, k]
                    hi, lo = w13_hi[:, k, 2 * u:2 * u + 2, :], w13_lo[:, k, 2 * u:2 * u + 2, :]
                    pe.matmul(dst, hi, x_hi[:, par], start=True, stop=False)
                    pe.matmul(dst, hi, x_lo[:, par], start=False, stop=False)
                    last = pe.matmul(dst, lo, x_hi[:, par], start=False, stop=True)
                last.then_inc(up_ready, 1)

            def gate(c, u):
                if u < PAIRS:
                    if u == 0:
                        w_dve(pe, c, "gate_lo")
                    c.wait(pe, hidden_done, UNITS, u - 1)
                    pe.matmul(gate_psum[slot(c, u)][:], pair_sel[:, u * P:(u + 1) * P], gates[:, c.parity], start=True,
                              stop=True).then_inc(gate_ready, 1)

            def down(c, u):
                s = ring(u)
                if u == 0:
                    c.wait(pe, y_copied, 1, 0)
                    if c.it is None and c.k == 0:
                        pe.wait_ge(w_lo_done, 3)
                c.wait(pe, hidden_lo_done, UNITS, u + 1)
                pe.matmul(y_psum[:], w2_hi[:, u], hidden_hi[:, s], start=u == 0, stop=False)
                pe.matmul(y_psum[:], w2_lo[:, u], hidden_hi[:, s], start=False, stop=False)
                pe.matmul(y_psum[:], w2_hi[:, u], hidden_lo[:, s], start=False,
                          stop=u == UNITS - 1).then_inc(down_done, 1)

            first = Chunk(0)
            for stage, _ in STAGES:
                if stage == "rank":
                    pe.wait_ge(tri_cast, 1)
                    pe.wait_ge(pool_setup, 4)
                chain(first, stage)
                if stage == "route":
                    pe.wait_ge(w_lo_done, 2)
                    up(first, 0)
                elif stage == "rank":
                    up(first, 1)
            pe.wait_ge(pairs_rounded, 1)
            for u in range(2):
                gate(first, u)

            def body(c):
                for u in range(UNITS):
                    ahead, behind = unit_after(c, u, 2), unit_after(c, u, -2)
                    if ahead:
                        up(*ahead)
                    if behind:
                        down(*behind)
                    if ahead:
                        gate(*ahead)
                    run_stages(c, u, chain, ln2)

            run_chunks(pe, body, CHUNKS_B)
            for u in (UNITS - 2, UNITS - 1):
                down(Chunk(CHUNKS_B - 1), u)
            ln2(Chunk(CHUNKS_B - 1), "ln2_turn")


def kernel(**inputs):
    import concourse.bacc as bacc
    from concourse.bass_utils import run_bass_kernel_spmd

    a = {k: np.ascontiguousarray(v) for k, v in inputs.items()}
    x = a["L0_attn_x"]
    tokens = x.reshape(-1, x.shape[-1])
    ident, tri, spread, pairs, onesrow = make_tables(a["L0_ffn_Wg"].shape[1])
    arrays = {
        "x": tokens, "xT": np.ascontiguousarray(tokens.T), "gidx": a["L0_attn_global_indices"],
        "wqkvT": np.stack([np.ascontiguousarray(a[f"L0_attn_W{c}"].T) for c in "qkv"]),
        "bq": a["L0_attn_bq"], "bk": a["L0_attn_bk"], "bv": a["L0_attn_bv"], "bo": a["L0_attn_bo"],
        "WoT": np.ascontiguousarray(a["L0_attn_Wo"].T),
        "Wg": a["L0_ffn_Wg"], "W1": a["L0_ffn_W1"], "W2": a["L0_ffn_W2"], "W3": a["L0_ffn_W3"],
        "Ws1": a["L0_ffn_Ws1"], "Ws2": a["L0_ffn_Ws2"], "Ws3": a["L0_ffn_Ws3"],
        "t_ident": ident, "t_tri": tri, "t_spread": spread, "t_pairs": pairs, "t_onesrow": onesrow,
    }
    nc = bacc.Bacc("TRN2", target_bir_lowering=False, num_devices=1)
    d = {n: nc.dram_tensor(n, v.shape, mybir.dt.from_np(v.dtype), kind="ExternalInput").ap()
         for n, v in arrays.items()}
    out = nc.dram_tensor("out", tokens.shape, F32, kind="ExternalOutput").ap()
    scratch = nc.dram_tensor("scratch", tokens.shape, F32, kind="Internal").ap()
    with ExitStack() as outer:
        shared = Shared(nc, outer, d)
        with ExitStack() as ctx:
            build_attention(nc, ctx, d, scratch, shared)
        with ExitStack() as ctx:
            build_experts(nc, ctx, d, scratch, out, shared)
    r = run_bass_kernel_spmd(nc, [arrays], core_ids=[0])
    return r.results[0]["out"].reshape(x.shape)
```
